# Optimizing a Trainium2 kernel written in Bass

```python
import numpy as np
import jax
import jax.numpy as jnp

def _softmax(x, axis=-1):
    return jax.nn.softmax(x, axis=axis)

def _gelu(x):
    return jax.nn.gelu(x, approximate=True)

def _silu(x):
    return jax.nn.silu(x)

def _sigmoid(x):
    return jax.nn.sigmoid(x)

def _layernorm(x, axis=-1, eps=1e-05):
    m = jnp.mean(x, axis=axis, keepdims=True)
    v = jnp.var(x, axis=axis, keepdims=True)
    return (x - m) / jnp.sqrt(v + eps)

def _scatter_add(tgt, idx, src, axis=0):
    return tgt.at[idx].add(src)

def _segment_sum(src, seg, n):
    return jax.ops.segment_sum(src, seg, n)
kernel_name = 'mk_prb_d2_jaxref_r8_5742ad'

def setup_inputs(seed: int=0):
    np.random.seed(seed)
    _w = jnp.asarray

    def _L0_attn_setup():
        import jax, jax.numpy as jnp
        import numpy as np
        DIM = 512
        NUM_HEAD = 32
        NUM_KV_HEAD = 8
        ROPE_THETA = 10000.0
        B, T = (2, 256)

        def apply_rope(x, start_pos=0, theta=ROPE_THETA):
            d = x.shape[-1]
            half = d // 2
            inv_freq = 1.0 / theta ** (jnp.arange(0, half, dtype=jnp.float32) / half)
            pos = jnp.arange(x.shape[1], dtype=jnp.float32) + start_pos
            ang = pos[:, None] * inv_freq[None, :]
            cos = jnp.cos(ang)[None, :, None, :]
            sin = jnp.sin(ang)[None, :, None, :]
            x1, x2 = (x[..., :half], x[..., half:])
            return jnp.concatenate([x1 * cos - x2 * sin, x1 * sin + x2 * cos], axis=-1)
        key = jax.random.key(seed)
        ks = jax.random.split(key, 5)
        scale = 0.02
        X = jax.random.normal(ks[0], (B, T, DIM), dtype=jnp.float32)
        Wq = jax.random.normal(ks[1], (DIM, DIM), dtype=jnp.float32) * scale
        Wk = jax.random.normal(ks[2], (DIM, DIM // NUM_HEAD * NUM_KV_HEAD), dtype=jnp.float32) * scale
        Wv = jax.random.normal(ks[3], (DIM, DIM // NUM_HEAD * NUM_KV_HEAD), dtype=jnp.float32) * scale
        Wo = jax.random.normal(ks[4], (DIM, DIM), dtype=jnp.float32) * scale
        return {'X': X, 'Wq': Wq, 'Wk': Wk, 'Wv': Wv, 'Wo': Wo}
    _L0_attn_in = _L0_attn_setup()

    def _L0_ffn_setup():
        import jax, jax.numpy as jnp
        import numpy as np
        key = jax.random.key(seed)
        k = jax.random.split(key, 6)
        x = jax.random.normal(k[0], (4, 256, 512), jnp.float32)
        W = jax.random.normal(k[1], (512, 512), jnp.float32) * 0.02
        bias = jax.random.normal(k[2], (512,), jnp.float32) * 0.02
        A = jax.random.normal(k[3], (16, 16, 512), jnp.float32) * 0.02
        Bf = jax.random.normal(k[4], (16, 512, 16), jnp.float32) * 0.02
        coeffs = jax.random.uniform(k[5], (16,), jnp.float32)
        scales = jnp.full((16,), 0.5, jnp.float32)
        return {'x': x, 'W': W, 'bias': bias, 'A': A, 'Bf': Bf, 'coeffs': coeffs, 'scales': scales}
    _L0_ffn_in = _L0_ffn_setup()

    def _L1_attn_setup():
        import jax, jax.numpy as jnp
        import numpy as np
        HDC_DIM = 512
        N_HEADS = 4
        HEAD_DIM = HDC_DIM // N_HEADS

        def _ste_sign(w):
            alpha = jnp.mean(jnp.abs(w), axis=-1, keepdims=True)
            hard = alpha * jnp.sign(w)
            hard = jnp.where(hard == 0, alpha, hard)
            return jax.lax.stop_gradient(hard - w) + w
        key = jax.random.key(seed)
        kx, kq, kk, kv = jax.random.split(key, 4)
        B, T = (4, 256)
        x = jax.random.normal(kx, (B, T, HDC_DIM), dtype=jnp.float32)
        bv_q = jax.random.normal(kq, (N_HEADS, HEAD_DIM), dtype=jnp.float32) * 0.02
        bv_k = jax.random.normal(kk, (N_HEADS, HEAD_DIM), dtype=jnp.float32) * 0.02
        bv_v = jax.random.normal(kv, (N_HEADS, HEAD_DIM), dtype=jnp.float32) * 0.02
        return {'x': x, 'bv_q': bv_q, 'bv_k': bv_k, 'bv_v': bv_v}
    _L1_attn_in = _L1_attn_setup()

    def _L1_ffn_setup():
        import jax, jax.numpy as jnp
        import numpy as np
        DIM = 512
        INTER = 128
        E = 16
        GROUPS = 4
        LIM = 2
        K = 2
        SHARED_INTER = 2 * INTER
        SCALE = 1.0
        key = jax.random.key(seed)
        ks = jax.random.split(key, 16)

        def n(k, shape, s=0.02):
            return jax.random.normal(k, shape, jnp.float32) * s
        return {'x': jax.random.normal(ks[0], (1, 256, DIM), jnp.float32), 'router_w': n(ks[1], (DIM, E)), 'router_b': n(ks[2], (E,)), 'router_bias': n(ks[3], (E,), 1.0), 'ew1': n(ks[4], (E, DIM, INTER)), 'eb1': n(ks[5], (E, INTER)), 'ew2': n(ks[6], (E, DIM, INTER)), 'eb2': n(ks[7], (E, INTER)), 'ew3': n(ks[8], (E, INTER, DIM)), 'eb3': n(ks[9], (E, DIM)), 'sw1': n(ks[10], (DIM, SHARED_INTER)), 'sb1': n(ks[11], (SHARED_INTER,)), 'sw2': n(ks[12], (DIM, SHARED_INTER)), 'sb2': n(ks[13], (SHARED_INTER,)), 'sw3': n(ks[14], (SHARED_INTER, DIM)), 'sb3': n(ks[15], (DIM,))}
    _L1_ffn_in = _L1_ffn_setup()
    _d = {'L0_attn_X': _L0_attn_in['X'], 'L0_attn_Wq': _L0_attn_in['Wq'], 'L0_attn_Wk': _L0_attn_in['Wk'], 'L0_attn_Wv': _L0_attn_in['Wv'], 'L0_attn_Wo': _L0_attn_in['Wo'], 'L0_ffn_W': _L0_ffn_in['W'], 'L0_ffn_bias': _L0_ffn_in['bias'], 'L0_ffn_A': _L0_ffn_in['A'], 'L0_ffn_Bf': _L0_ffn_in['Bf'], 'L0_ffn_coeffs': _L0_ffn_in['coeffs'], 'L0_ffn_scales': _L0_ffn_in['scales'], 'L1_attn_bv_q': _L1_attn_in['bv_q'], 'L1_attn_bv_k': _L1_attn_in['bv_k'], 'L1_attn_bv_v': _L1_attn_in['bv_v'], 'L1_ffn_router_w': _L1_ffn_in['router_w'], 'L1_ffn_router_b': _L1_ffn_in['router_b'], 'L1_ffn_router_bias': _L1_ffn_in['router_bias'], 'L1_ffn_ew1': _L1_ffn_in['ew1'], 'L1_ffn_eb1': _L1_ffn_in['eb1'], 'L1_ffn_ew2': _L1_ffn_in['ew2'], 'L1_ffn_eb2': _L1_ffn_in['eb2'], 'L1_ffn_ew3': _L1_ffn_in['ew3'], 'L1_ffn_eb3': _L1_ffn_in['eb3'], 'L1_ffn_sw1': _L1_ffn_in['sw1'], 'L1_ffn_sb1': _L1_ffn_in['sb1'], 'L1_ffn_sw2': _L1_ffn_in['sw2'], 'L1_ffn_sb2': _L1_ffn_in['sb2'], 'L1_ffn_sw3': _L1_ffn_in['sw3'], 'L1_ffn_sb3': _L1_ffn_in['sb3']}
    _x0 = _d['L0_attn_X']
    _d['L0_attn_X'] = jax.random.normal(jax.random.fold_in(jax.random.key(seed), 1), (2, 1024, 512), dtype=_x0.dtype)
    del _x0
    return _d

def reference(L0_attn_X, L0_attn_Wq, L0_attn_Wk, L0_attn_Wv, L0_attn_Wo, L0_ffn_W, L0_ffn_bias, L0_ffn_A, L0_ffn_Bf, L0_ffn_coeffs, L0_ffn_scales, L1_attn_bv_q, L1_attn_bv_k, L1_attn_bv_v, L1_ffn_router_w, L1_ffn_router_b, L1_ffn_router_bias, L1_ffn_ew1, L1_ffn_eb1, L1_ffn_ew2, L1_ffn_eb2, L1_ffn_ew3, L1_ffn_eb3, L1_ffn_sw1, L1_ffn_sb1, L1_ffn_sw2, L1_ffn_sb2, L1_ffn_sw3, L1_ffn_sb3):

    def _L0_attn_ref(X, Wq, Wk, Wv, Wo):
        import jax, jax.numpy as jnp
        import numpy as np
        DIM = 512
        NUM_HEAD = 32
        NUM_KV_HEAD = 8
        ROPE_THETA = 10000.0
        B, T = (2, 256)

        def apply_rope(x, start_pos=0, theta=ROPE_THETA):
            d = x.shape[-1]
            half = d // 2
            inv_freq = 1.0 / theta ** (jnp.arange(0, half, dtype=jnp.float32) / half)
            pos = jnp.arange(x.shape[1], dtype=jnp.float32) + start_pos
            ang = pos[:, None] * inv_freq[None, :]
            cos = jnp.cos(ang)[None, :, None, :]
            sin = jnp.sin(ang)[None, :, None, :]
            x1, x2 = (x[..., :half], x[..., half:])
            return jnp.concatenate([x1 * cos - x2 * sin, x1 * sin + x2 * cos], axis=-1)
        Bs, Ts, C = X.shape
        H, Hkv = (NUM_HEAD, NUM_KV_HEAD)
        dh = C // H
        G = H // Hkv
        Q = apply_rope((X @ Wq).reshape(Bs, Ts, H, dh))
        K = apply_rope((X @ Wk).reshape(Bs, Ts, Hkv, dh))
        V = (X @ Wv).reshape(Bs, Ts, Hkv, dh)
        Qh = Q.transpose(0, 2, 1, 3).reshape(Bs, Hkv, G, Ts, dh)
        Kh = K.transpose(0, 2, 1, 3)
        Vh = V.transpose(0, 2, 1, 3)
        scores = jnp.einsum('bkgtd,bksd->bkgts', Qh, Kh) / jnp.sqrt(jnp.float32(dh))
        causal = jnp.tril(jnp.ones((Ts, Ts), dtype=bool))
        scores = jnp.where(causal[None, None, None], scores, -jnp.inf)
        attn = jax.nn.softmax(scores, axis=-1)
        out = jnp.einsum('bkgts,bksd->bkgtd', attn, Vh)
        out = out.reshape(Bs, H, Ts, dh).transpose(0, 2, 1, 3).reshape(Bs, Ts, C)
        return out @ Wo

    def _L0_ffn_ref(x, W, bias, A, Bf, coeffs, scales):
        import jax, jax.numpy as jnp
        import numpy as np
        out = jnp.einsum('bsd,od->bso', x, W) + bias
        xa = jnp.einsum('bsd,erd->ebsr', x, A)
        w = coeffs * scales
        upd = jnp.einsum('ebsr,eor,e->bso', xa, Bf, w)
        return out + upd

    def _L1_attn_ref(x, bv_q, bv_k, bv_v):
        import jax, jax.numpy as jnp
        import numpy as np
        HDC_DIM = 512
        N_HEADS = 4
        HEAD_DIM = HDC_DIM // N_HEADS

        def _ste_sign(w):
            alpha = jnp.mean(jnp.abs(w), axis=-1, keepdims=True)
            hard = alpha * jnp.sign(w)
            hard = jnp.where(hard == 0, alpha, hard)
            return jax.lax.stop_gradient(hard - w) + w
        B, T, D = x.shape
        H, HD = (N_HEADS, HEAD_DIM)
        scale = HD ** (-0.5)
        q_bind = _ste_sign(bv_q)
        k_bind = _ste_sign(bv_k)
        v_bind = _ste_sign(bv_v)
        xh = x.reshape(B, T, H, HD)
        Q = xh * q_bind
        K = xh * k_bind
        V = xh * v_bind
        scores = jnp.einsum('bthd,bshd->bhts', Q, K) * scale
        causal = jnp.tril(jnp.ones((T, T), dtype=bool))
        attn = jnp.where(causal, jax.nn.sigmoid(scores * 4.0), 0.0)
        out = jnp.einsum('bhts,bshd->bthd', attn, V)
        return out.reshape(B, T, D)

    def _L1_ffn_ref(x, router_w, router_b, router_bias, ew1, eb1, ew2, eb2, ew3, eb3, sw1, sb1, sw2, sb2, sw3, sb3):
        import jax, jax.numpy as jnp
        import numpy as np
        DIM = 512
        INTER = 128
        E = 16
        GROUPS = 4
        LIM = 2
        K = 2
        SHARED_INTER = 2 * INTER
        SCALE = 1.0
        shape = x.shape
        xt = x.reshape(-1, DIM)
        T = xt.shape[0]
        logits = xt @ router_w + router_b
        scores = jax.nn.softmax(logits.astype(jnp.float32), axis=-1) + router_bias
        g = scores.reshape(T, GROUPS, E // GROUPS)
        _, gidx = jax.lax.top_k(g.max(axis=-1), LIM)
        keep = jnp.zeros((T, GROUPS), bool).at[jnp.arange(T)[:, None], gidx].set(True)
        masked = jnp.where(keep[:, :, None], g, -jnp.inf).reshape(T, E)
        _, idx = jax.lax.top_k(masked, K)
        vals = (jnp.take_along_axis(scores, idx, axis=1) * SCALE).astype(x.dtype)
        gate = jnp.zeros((T, E), x.dtype).at[jnp.arange(T)[:, None], idx].add(vals)

        def step(y, p):
            w1, b1, w2, b2, w3, b3, ge = p
            h = jax.nn.silu(xt @ w1 + b1) * (xt @ w2 + b2)
            return (y + ge[:, None] * (h @ w3 + b3), None)
        y, _ = jax.lax.scan(step, jnp.zeros_like(xt), (ew1, eb1, ew2, eb2, ew3, eb3, gate.T))
        z = jax.nn.silu(xt @ sw1 + sb1) * (xt @ sw2 + sb2) @ sw3 + sb3
        return (y + z).reshape(shape)
    x = L0_attn_X
    xn = _layernorm(x, axis=-1)
    x = x + _L0_attn_ref(xn, L0_attn_Wq, L0_attn_Wk, L0_attn_Wv, L0_attn_Wo) + _L0_ffn_ref(xn, L0_ffn_W, L0_ffn_bias, L0_ffn_A, L0_ffn_Bf, L0_ffn_coeffs, L0_ffn_scales)
    xn = _layernorm(x, axis=-1)
    x = x + _L1_attn_ref(xn, L1_attn_bv_q, L1_attn_bv_k, L1_attn_bv_v) + _L1_ffn_ref(xn, L1_ffn_router_w, L1_ffn_router_b, L1_ffn_router_bias, L1_ffn_ew1, L1_ffn_eb1, L1_ffn_ew2, L1_ffn_eb2, L1_ffn_ew3, L1_ffn_eb3, L1_ffn_sw1, L1_ffn_sb1, L1_ffn_sw2, L1_ffn_sb2, L1_ffn_sw3, L1_ffn_sb3)
    return x

_drawn_inputs = setup_inputs


def setup_inputs(seed=0):
    import zlib

    import numpy as np

    out = dict(_drawn_inputs(seed))
    spreads = {'L0_ffn_scales': (0.5, 0.6)}
    factors = {'L0_attn_Wq': 8.0,
     'L0_attn_Wk': 8.0,
     'L0_ffn_coeffs': 3.532,
     'L1_attn_bv_q': 34.215,
     'L1_attn_bv_k': 34.352,
     'L1_ffn_router_w': 8.0,
     'L1_ffn_router_b': 64.0,
     'L1_ffn_eb1': 8.0,
     'L1_ffn_eb2': 8.0,
     'L1_ffn_sb1': 40.364,
     'L1_ffn_sb2': 39.069,
     'L1_ffn_sb3': 3.244}
    for name, (base, spread) in spreads.items():
        noise = np.random.default_rng([zlib.crc32(name.encode()), seed]).standard_normal(out[name].shape)
        drawn = base * np.exp(spread * noise) if base else spread * noise
        out[name] = jnp.asarray(drawn.astype(out[name].dtype))
    for name, factor in factors.items():
        out[name] = (out[name] * factor).astype(out[name].dtype)
    return out
```

```python
from contextlib import ExitStack

import numpy as np
import concourse.bass as bass
from concourse import mybir

F32 = mybir.dt.float32
F32R = mybir.dt.float32r
ALU = mybir.AluOpType
ACT = mybir.ActivationFunctionType
AX = mybir.AxisListType

P = 128
B, T, D = 2, 1024, 512
NB = B * T // P
TB = T // P
KT = D // P
H, HKV, DH = 32, 8, 16
G = H // HKV
HALF = DH // 2
QK = D + HKV * DH
QT = QK // P
LR = 256
BH, BD = 4, 128
E, INTER = 16, 128
EG = 4
NE = E + 2
EPS = 1e-5
MASKED = -float(2 ** 100)
CH = 512
NCH = B * T // CH
STACK = 4 * DH
SHIFT_ROW = 96
ROWS = SHIFT_ROW + 2


class Buffers:
    pass


def f32(ap):
    return ap.bitcast(F32)


def semaphores(nc, ctx, phase, names):
    return {name: ctx.enter_context(nc.semaphore(f"{phase}_{name}")) for name in names.split()}


def blocks(eng, total, step, first=3, last=3, period=2):
    n = 0
    while n < first:
        step(n, n // period, n % period)
        n += 1
    turns = (total - last - first) // period
    if turns > 0:
        with eng.Fori(0, turns) as i:
            for m in range(n, n + period):
                step(i * period + m, i + m // period, m % period)
        n += turns * period
    while n < total:
        step(n, n // period, n % period)
        n += 1


def phase_weights(nc, d, r, w):
    with ExitStack() as ctx:
        sb = lambda n, s, t=F32: ctx.enter_context(nc.sbuf_tensor(n, s, t))
        wqkv = sb("wqkv_raw", [P, KT, QK + HKV * DH])
        wo = sb("wo_raw", [P, KT, D])
        wl = sb("wl_raw", [P, KT, D])
        am = sb("a_raw", [P, 2, D])
        bf = sb("bf_raw", [P, KT, LR])
        bw = sb("bw", [P, KT, LR])
        bwT = sb("bwT", [P, 2, D])
        co = sb("coeffs_all", [P, E])
        sc = sb("scales_all", [P, E])
        we = sb("we", [P, E])
        turned = [ctx.enter_context(nc.psum_tensor(f"bw_turned{i}", [P, D], F32)) for i in range(2)]
        folded = [ctx.enter_context(nc.psum_tensor(f"w_folded{i}", [P, D], F32)) for i in range(KT)]
        s = semaphores(nc, ctx, "w", "x_in qkv_in wo_in low_in wl_in const_in kscaled qkv_done hi_done "
                 "we_done bw_done turned_done bwT_done folded_done folded_hi all_done idr ones")
        block = ctx.enter_context(nc.Block())

        @block.sync
        def _(sp):
            for k in range(KT):
                sp.dma_start(bf[:, k].rearrange("p (e r) -> p e r", e=E),
                             d["Bf"][:, k * P:(k + 1) * P].rearrange("e p r -> p e r")).then_inc(s["low_in"], 16)
            sp.dma_start(co[:], d["coeffs"].rearrange("(a e) -> a e", a=1).broadcast_to([P, E])).then_inc(s["low_in"], 16)
            sp.dma_start(sc[:], d["scales"].rearrange("(a e) -> a e", a=1).broadcast_to([P, E])).then_inc(s["low_in"], 16)
            sp.dma_start(am[:], d["A"].rearrange("e r d -> (e r) d").rearrange("(h p) d -> p h d", p=P)).then_inc(s["low_in"], 16)
            sp.dma_start(wl[:], d["W"].rearrange("(k p) d -> p k d", p=P)).then_inc(s["wl_in"], 16)
            for n in range(0, NB, 4):
                sp.dma_start(r.Y[:, n:n + 4], d["X"].rearrange("b t d -> (b t) d").rearrange(
                    "(n p) d -> p n d", p=P)[:, n:n + 4]).then_inc(s["x_in"], 16)
            sp.wait_ge(s["x_in"], 16 * NB // 4)

        @block.scalar
        def _(act):
            act.dma_start(r.ident[:], d["ident"]).then_inc(s["const_in"], 16)
            act.dma_start(r.mask[:], d["mask"]).then_inc(s["const_in"], 16)
            act.dma_start(r.cos[:], d["cos"]).then_inc(s["const_in"], 16)
            act.dma_start(r.sin[:], d["sin"]).then_inc(s["const_in"], 16)
            act.dma_start(r.bias[:], d["bias"].rearrange("(a e) -> a e", a=1).broadcast_to([P, D])).then_inc(s["const_in"], 16)
            act.dma_start(wqkv[:, :, 0:D], d["Wq"].rearrange("(k p) n -> p k n", p=P)).then_inc(s["qkv_in"], 16)
            act.dma_start(wqkv[:, :, D:QK], d["Wk"].rearrange("(k p) n -> p k n", p=P)).then_inc(s["qkv_in"], 16)
            act.dma_start(wqkv[:, :, QK:], d["Wv"].rearrange("(k p) n -> p k n", p=P)).then_inc(s["qkv_in"], 16)
            act.dma_start(wo[:], d["Wo"].rearrange("(k p) n -> p k n", p=P)).then_inc(s["wo_in"], 16)
            act.wait_ge(s["kscaled"], 1)
            nc.scalar.copy(w.qkv_h[:], wqkv[:]).then_inc(s["hi_done"], 1)
            act.wait_ge(s["wo_in"], 16)
            nc.scalar.copy(w.o_h[:], wo[:]).then_inc(s["hi_done"], 1)
            for k in range(KT):
                act.wait_ge(s["folded_done"], k + 1)
                nc.scalar.copy(w.l_h[:, k], folded[k][:]).then_inc(s["folded_hi"], 1)

        @block.gpsimd
        def _(pool):
            nc.gpsimd.memset(r.V[:], 1.0).then_inc(s["ones"], 1)
            pool.wait_ge(s["qkv_in"], 48)
            nc.gpsimd.tensor_scalar(wqkv[:, :, D:QK], wqkv[:, :, D:QK], DH ** -0.5, None, ALU.mult).then_inc(s["kscaled"], 1)
            pool.wait_ge(s["hi_done"], 1)
            nc.gpsimd.tensor_tensor(w.qkv_l[:], wqkv[:], f32(w.qkv_h[:]), ALU.subtract).then_inc(s["all_done"], 1)
            pool.wait_ge(s["hi_done"], 2)
            nc.gpsimd.tensor_tensor(w.o_l[:], wo[:], f32(w.o_h[:]), ALU.subtract).then_inc(s["all_done"], 1)

        @block.vector
        def _(dve):
            nc.vector.memset(r.eps[:], EPS).then_inc(s["ones"], 1)
            dve.wait_ge(s["low_in"], 16 * (KT + 3))
            nc.vector.tensor_tensor(we[:], co[:], sc[:], ALU.mult).then_inc(s["we_done"], 1)
            dve.wait_ge(s["we_done"], 1)
            for k in range(KT):
                nc.vector.tensor_tensor(bw[:, k].rearrange("p (e r) -> p e r", e=E),
                                        bf[:, k].rearrange("p (e r) -> p e r", e=E),
                                        we[:].rearrange("p (e a) -> p e a", a=1).broadcast_to([P, E, LR // E]),
                                        ALU.mult).then_inc(s["bw_done"], 1)
            dve.wait_ge(s["const_in"], 80)
            nc.vector.tensor_copy(r.ident_r[:], r.ident[:]).then_inc(s["idr"], 1)
            nc.vector.tensor_copy(r.mask_r[:], r.mask[:].rearrange("p (a s) -> p a s", a=1).broadcast_to([P, G, P])).then_inc(s["idr"], 1)
            for h in range(2):
                dve.wait_ge(s["turned_done"], h + 1)
                nc.vector.tensor_copy(bwT[:, h], turned[h][:]).then_inc(s["bwT_done"], 1)
            for k in range(KT):
                dve.wait_ge(s["folded_hi"], k + 1)
                nc.vector.tensor_tensor(w.l_l[:, k], folded[k][:], f32(w.l_h[:, k]), ALU.subtract).then_inc(s["all_done"], 1)

        @block.tensor
        def _(pe):
            pe.wait_ge(s["bw_done"], KT)
            pe.wait_ge(s["const_in"], 80)
            for h in range(2):
                for k in range(KT):
                    last = nc.tensor.transpose(turned[h][:, k * P:(k + 1) * P], bw[:, k, h * P:(h + 1) * P], r.ident[:])
                last.then_inc(s["turned_done"], 1)
            pe.wait_ge(s["bwT_done"], 2)
            pe.wait_ge(s["wl_in"], 16)
            for k in range(KT):
                for h in range(2):
                    nc.tensor.matmul(folded[k][:], am[:, h, k * P:(k + 1) * P], bwT[:, h], start=(h == 0), stop=False,
                                     skip_group_check=True)
                for o in range(KT):
                    last = nc.tensor.matmul(folded[k][:, o * P:(o + 1) * P], wl[:, o, k * P:(k + 1) * P], r.ident[:],
                                            start=False, stop=(o == KT - 1), skip_group_check=True)
                last.then_inc(s["folded_done"], 1)


def split_matmuls(nc, out, lhs, rhs, k):
    (lh, ll), (rh, rl) = lhs, rhs
    nc.tensor.matmul(out, lh, rh, start=(k == 0), stop=False)
    nc.tensor.matmul(out, lh, rl, start=False, stop=False)
    return nc.tensor.matmul(out, ll, rh, start=False, stop=(k == KT - 1))


def phase_project(nc, d, r, w):
    with ExitStack() as ctx:
        sb = lambda n, s, t=F32: ctx.enter_context(nc.sbuf_tensor(n, s, t))
        stats = sb("stats", [P, 2, 6])
        moments = sb("moments", [P, 2, 2])
        std = sb("std", [P, 2])
        rstd = sb("rstd", [P, 2])
        xn = sb("xn", [P, 2, D])
        xT_h = [sb(f"xT_h{i}", [P, KT, P], F32R) for i in range(2)]
        xT_l = [sb(f"xT_l{i}", [P, KT, P], F32R) for i in range(2)]
        by_cos = sb("by_cos", [P, QK])
        by_sin = sb("by_sin", [P, QK])
        turned = sb("turned", [P, 2, QK])
        qkT_h = sb("qkT_h", [P, 2, QT, P], F32R)
        qkT_l = sb("qkT_l", [P, 2, QT, P], F32R)
        ps = lambda n: ctx.enter_context(nc.psum_tensor(n, [P, D], F32))
        x_turn = [ps("x_turn0"), ps("x_turn1")]
        q_ps, kv_ps, lin_ps, q_turn, k_turn = ps("q_ps"), ps("kv_ps"), ps("lin_ps"), ps("q_turn"), ps("k_turn")
        s = semaphores(nc, ctx, "p", "stats_done moments_done std_done rstd_done xn_ready bias_added x_turned xhi_ready "
                 "xlo_ready q_done kv_done lin_done qmul_done kmul_done v_read lin_added rot_done qk_turned "
                 "qhi_ready qlo_ready stored0 stored1")
        stored = [s["stored0"], s["stored1"]]
        block = ctx.enter_context(nc.Block())

        @block.vector
        def _(dve):
            def statistics(n, par):
                nc.vector.bn_stats(stats[:, par], r.Y[:, n]).then_inc(s["stats_done"], 1)

            def norm(n, par):
                nc.vector.bn_aggr(moments[:, par], stats[:, par]).then_inc(s["moments_done"], 1)
                dve.wait_ge(s["std_done"], n + 1)
                nc.vector.reciprocal(rstd[:, par:par + 1], std[:, par:par + 1]).then_inc(s["rstd_done"], 1)
                dve.wait_ge(s["rstd_done"], n + 1)
                nc.vector.tensor_scalar(xn[:, par], r.Y[:, n], moments[:, par, 0:1], rstd[:, par:par + 1],
                                        ALU.subtract, ALU.mult).then_inc(s["xn_ready"], 1)

            def low_half(n, par):
                dve.wait_ge(s["xhi_ready"], n + 1)
                nc.vector.tensor_tensor(xT_l[par][:], x_turn[par][:].rearrange("p (k t) -> p k t", k=KT),
                                        f32(xT_h[par][:]), ALU.subtract).then_inc(s["xlo_ready"], 1)

            def rope_products(n):
                for ps_, a, b, ready, done in ((q_ps, 0, D, s["q_done"], s["qmul_done"]), (kv_ps, D, QK, s["kv_done"], s["kmul_done"])):
                    dve.wait_ge(ready, n + 1)
                    if a == 0 and not (isinstance(n, int) and n == 0):
                        dve.wait_ge(s["rot_done"], n * 2)
                    heads = (b - a) // DH
                    src = ps_[:, 0:b - a].rearrange("p (h x c) -> p h x c", x=2, c=HALF)
                    for table, out in ((r.cos, by_cos), (r.sin, by_sin)):
                        fac = table[:, n].rearrange("p (a x c) -> p a x c", a=1, x=2).broadcast_to([P, heads, 2, HALF])
                        last = nc.vector.tensor_tensor(
                            out[:, a:b].rearrange("p (h x c) -> p h x c", x=2, c=HALF), src, fac, ALU.mult)
                    last.then_inc(done, 1)

            def add_linear(n):
                dve.wait_ge(s["lin_done"], n + 1)
                dve.wait_ge(s["bias_added"], n + 1)
                nc.vector.tensor_tensor(r.Y[:, n], lin_ps[:], r.Y[:, n], ALU.add).then_inc(s["lin_added"], 1)

            def low_qk(n, par):
                dve.wait_ge(s["qhi_ready"], n + 1)
                nc.vector.tensor_tensor(qkT_l[:, par, 0:KT], q_turn[:].rearrange("p (k t) -> p k t", k=KT),
                                        f32(qkT_h[:, par, 0:KT]), ALU.subtract)
                nc.vector.tensor_tensor(qkT_l[:, par, KT], k_turn[:, 0:P],
                                        f32(qkT_h[:, par, KT]), ALU.subtract).then_inc(s["qlo_ready"], 1)

            for n in range(2):
                statistics(n, n)
                dve.wait_ge(s["stats_done"], n + 1)
                norm(n, n)
            low_half(0, 0)

            def step(n, k, par):
                static = isinstance(n, int)
                if not static or n + 2 < NB:
                    statistics(n + 2, par)
                    dve.wait_ge(s["stats_done"], n + 3)
                if not static or n + 1 < NB:
                    low_half(n + 1, 1 - par)
                if not static or n + 2 < NB:
                    norm(n + 2, par)
                rope_products(n)
                add_linear(n)
                if not static or n >= 1:
                    low_qk(n - 1, 1 - par)
            blocks(dve, NB, step)
            low_qk(NB - 1, 1)

        @block.scalar
        def _(act):
            def root(n, par):
                act.wait_ge(s["moments_done"], n + 1)
                nc.scalar.activation(std[:, par:par + 1], moments[:, par, 1:2], ACT.Sqrt, bias=r.eps[:]).then_inc(s["std_done"], 1)

            def high_half(n, par):
                act.wait_ge(s["x_turned"], n + 1)
                if not (isinstance(n, int) and n < 2):
                    act.wait_ge(s["lin_done"], n - 1)
                nc.scalar.copy(xT_h[par][:], x_turn[par][:].rearrange("p (k t) -> p k t", k=KT)).then_inc(s["xhi_ready"], 1)

            def keep_v(n):
                act.wait_ge(s["kmul_done"], n + 1)
                nc.scalar.copy(r.V[:, n, :, 0:DH], kv_ps[:, P:2 * P].rearrange("p (h c) -> p h c", c=DH)).then_inc(s["v_read"], 1)

            def high_qk(n, k, par):
                act.wait_ge(s["qk_turned"], n + 1)
                if not (isinstance(n, int) and n < 2):
                    act.wait_ge(stored[par], k * 32)
                nc.scalar.copy(qkT_h[:, par, 0:KT], q_turn[:].rearrange("p (k t) -> p k t", k=KT))
                nc.scalar.copy(qkT_h[:, par, KT], k_turn[:, 0:P]).then_inc(s["qhi_ready"], 1)

            root(0, 0)
            root(1, 1)
            high_half(0, 0)

            def step(n, k, par):
                static = isinstance(n, int)
                if not static or n + 1 < NB:
                    high_half(n + 1, 1 - par)
                if not static or n + 2 < NB:
                    root(n + 2, par)
                keep_v(n)
                if not static or n >= 1:
                    high_qk(n - 1, k if par else k - 1, 1 - par)
            blocks(act, NB, step)
            high_qk(NB - 1, (NB - 1) // 2, 1)

        @block.gpsimd
        def _(pool):
            def add_bias(n):
                pool.wait_ge(s["xn_ready"], n + 1)
                nc.gpsimd.tensor_tensor(r.Y[:, n], r.Y[:, n], r.bias[:], ALU.add).then_inc(s["bias_added"], 1)

            def rotate(n, par):
                pool.wait_ge(s["kmul_done"], n + 1)
                if not (isinstance(n, int) and n < 2):
                    pool.wait_ge(s["qk_turned"], n - 1)
                c = by_cos[:].rearrange("p (h x c) -> p h x c", x=2, c=HALF)
                sn = by_sin[:].rearrange("p (h x c) -> p h x c", x=2, c=HALF)
                o = turned[:, par].rearrange("p (h x c) -> p h x c", x=2, c=HALF)
                nc.gpsimd.tensor_tensor(o[:, :, 0], c[:, :, 0], sn[:, :, 1], ALU.subtract).then_inc(s["rot_done"], 1)
                nc.gpsimd.tensor_tensor(o[:, :, 1], c[:, :, 1], sn[:, :, 0], ALU.add).then_inc(s["rot_done"], 1)

            add_bias(0)

            def step(n, k, par):
                if not isinstance(n, int) or n + 1 < NB:
                    add_bias(n + 1)
                rotate(n, par)
            blocks(pool, NB, step)

        @block.tensor
        def _(pe):
            def turn_x(n, par):
                pe.wait_ge(s["xn_ready"], n + 1)
                if not (isinstance(n, int) and n < 2):
                    pe.wait_ge(s["xlo_ready"], n - 1)
                for k in range(KT):
                    last = nc.tensor.transpose(x_turn[par][:, k * P:(k + 1) * P], xn[:, par, k * P:(k + 1) * P], r.ident[:])
                last.then_inc(s["x_turned"], 1)

            def project(n, par):
                first = isinstance(n, int) and n == 0
                pe.wait_ge(s["xlo_ready"], n + 1)
                for out, cols, wh, wlo, free, done in (
                        (q_ps[:], (0, D), w.qkv_h, w.qkv_l, s["qmul_done"], s["q_done"]),
                        (kv_ps[:, 0:2 * P], (D, QK + P), w.qkv_h, w.qkv_l, s["v_read"], s["kv_done"]),
                        (lin_ps[:], (0, D), w.l_h, w.l_l, s["lin_added"], s["lin_done"])):
                    if not first:
                        pe.wait_ge(free, n)
                    for k in range(KT):
                        last = split_matmuls(nc, out, (xT_h[par][:, k], xT_l[par][:, k]),
                                             (wh[:, k, cols[0]:cols[1]], wlo[:, k, cols[0]:cols[1]]), k)
                    last.then_inc(done, 1)

            def turn_qk(n, par):
                pe.wait_ge(s["rot_done"], 2 * n + 2)
                if not (isinstance(n, int) and n == 0):
                    pe.wait_ge(s["qlo_ready"], n)
                for k in range(KT):
                    nc.tensor.transpose(q_turn[:, k * P:(k + 1) * P], turned[:, par, k * P:(k + 1) * P], r.ident[:])
                nc.tensor.transpose(k_turn[:, 0:P], turned[:, par, D:QK], r.ident[:]).then_inc(s["qk_turned"], 1)

            turn_x(0, 0)

            def step(n, k, par):
                static = isinstance(n, int)
                if not static or n + 1 < NB:
                    turn_x(n + 1, 1 - par)
                project(n, par)
                if not static or n >= 1:
                    turn_qk(n - 1, 1 - par)
            blocks(pe, NB, step)
            turn_qk(NB - 1, 1)

        @block.sync
        def _(sp):
            def step(n, k, par):
                sp.wait_ge(s["qlo_ready"], n + 1)
                for half, src in enumerate((qkT_h, qkT_l)):
                    sp.dma_start(r.qk_dram[half].rearrange("(q p) t -> p q t", p=P)[:, :, bass.ds(n * P, P)],
                                 f32(src[:, par])).then_inc(stored[par], 16)
            blocks(sp, NB, step)
            for par in range(2):
                sp.wait_ge(stored[par], 32 * NB // 2)


def units():
    return [(tc, sb) for tc in range(T // CH) for sb in range((tc + 1) * CH // P)]


def max_units():
    out = []
    for tb in range(TB):
        for sc in range(tb * P // CH + 1):
            w = min((tb + 1) * P - sc * CH, CH)
            heads = 4 if w <= CH // 4 else 2 if w <= CH // 2 else 1
            out += [(tb, sc, h, heads, w) for h in range(0, G, heads)]
    return sorted(out, key=lambda m: m[0] >= CH // P)


def phase_attention(nc, d, r):
    U, M = units(), max_units()
    NU, NM = len(U), len(M)
    NG = B * HKV
    NBUF = 3
    TAIL = 2
    HEAD = NM * (NU - TAIL) // NU
    TURN_SHIFT = TAIL
    DIAG = [u for u, (tc, sb) in enumerate(U) if sb * P >= tc * CH]
    ND = len(DIAG)
    M_LATE = [m[0] for m in M].index(CH // P)
    LAST0 = CH // P - 1
    TURN_O0 = LAST0 + 3
    TURN_O1 = 1
    with ExitStack() as ctx:
        sb_ = lambda n, s, t=F32: ctx.enter_context(nc.sbuf_tensor(n, s, t))
        qs = [sb_(f"q_stack{i}", [ROWS, G, T], F32R) for i in range(NBUF)]
        ks = [sb_(f"k_stack{i}", [ROWS, T], F32R) for i in range(NBUF)]
        v = [sb_(f"v_cur{i}", [P, TB, 2 * DH]) for i in range(NBUF)]
        probs = [sb_(f"probs{i}", [P, G, CH]) for i in range(3)]
        negmax = sb_("negmax", [P, 2, G, TB])
        shift = sb_("shift", [P, G * TB])
        shiftT_h = sb_("shiftT_h", [G * TB, P], F32R)
        shiftT_l = sb_("shiftT_l", [G * TB, P], F32R)
        o_sb = sb_("o_sb", [P, 2, CH])
        rden = sb_("rden", [P, CH // P, G])
        s_ps = [ctx.enter_context(nc.psum_tensor(f"s_ps{i}", [P, 2, CH], F32)) for i in range(2)]
        m_ps = [ctx.enter_context(nc.psum_tensor(f"m_ps{i}", [P, CH], F32)) for i in range(2)]
        o_ps = ctx.enter_context(nc.psum_tensor("o_ps", [P, CH], F32))
        t_ps = ctx.enter_context(nc.psum_tensor("t_ps", [P, CH], F32))
        s = semaphores(nc, ctx, "a", "pad_done q0_in0 q0_in1 q0_in2 q1_in0 q1_in1 q1_in2 k_in0 k_in1 k_in2 v_ready m_scored m_read combined "
                 "turned turned_read shift_hi shift_ready shift_in0 shift_in1 shift_in2 scored exped masked pv_done o_read "
                 "rden_done mask_go")
        q0_in, q1_in, k_in = [s["q0_in0"], s["q0_in1"], s["q0_in2"]], [s["q1_in0"], s["q1_in1"], s["q1_in2"]], [s["k_in0"], s["k_in1"], s["k_in2"]]
        shift_in = [s["shift_in0"], s["shift_in1"], s["shift_in2"]]
        block = ctx.enter_context(nc.Block())
        NPAD = 3 * NBUF

        def width(u):
            tc, sb = U[u]
            off = max(0, sb * P - tc * CH)
            return tc, sb, off

        @block.sync
        def _(sp):
            def place(g):
                return (g // HKV, g % HKV)

            def load_q(g, k, par, tc):
                b, kv = place(g)
                for j, half in enumerate((0, 0, 1, 1)):
                    sp.dma_start(f32(qs[par][DH * j:DH * j + DH, :, tc * CH:(tc + 1) * CH]),
                                 r.qk_dram[half, bass.ds(kv * (G * DH), G * DH), bass.ds(b * T + tc * CH, CH)].rearrange(
                                     "(h c) t -> c h t", c=DH)).then_inc((q0_in, q1_in)[tc][par], 16)

            def load_k(g, k, par):
                b, kv = place(g)
                for j, half in enumerate((0, 1, 0, 1)):
                    sp.dma_start(f32(ks[par][DH * j:DH * j + DH, :]),
                                 r.qk_dram[half, bass.ds(D + kv * DH, DH), bass.ds(b * T, T)]).then_inc(k_in[par], 16)

            def send_shift(g, par):
                sp.wait_ge(s["shift_ready"], g + 1)
                for j, src in enumerate((shiftT_h, shiftT_l)):
                    sp.dma_start(f32(qs[par][SHIFT_ROW + j:SHIFT_ROW + j + 1]).rearrange("a h (n t) -> a (h n) t", t=P),
                                 f32(src[:])).then_inc(shift_in[par], 16)

            for g in range(NBUF):
                load_k(g, 0, g)
                load_q(g, 0, g, 0)
                load_q(g, 0, g, 1)
            send_shift(0, 0)

            def step(g, k, par):
                static = isinstance(g, int)
                if not static or g + 1 < NG:
                    send_shift(g + 1, (par + 1) % NBUF)
                if not static or g + NBUF < NG:
                    sp.wait_ge(s["scored"], 2 * NU * g + 2 * (LAST0 + 1))
                    load_q(g + NBUF, k, par, 0)
                    sp.wait_ge(s["scored"], 2 * NU * (g + 1))
                    load_k(g + NBUF, k, par)
                    load_q(g + NBUF, k, par, 1)
            blocks(sp, NG, step, 2, 5, NBUF)

        @block.gpsimd
        def _(pool):
            for i in range(NBUF):
                nc.gpsimd.memset(f32(qs[i][64:96]), 0.0).then_inc(s["pad_done"], 1)
                nc.gpsimd.memset(f32(ks[i][64:96]), 0.0).then_inc(s["pad_done"], 1)
                nc.gpsimd.memset(f32(ks[i][SHIFT_ROW:ROWS]), 1.0).then_inc(s["pad_done"], 1)

            def take_v(g, par):
                nc.gpsimd.tensor_copy(v[par][:], r.V[:, bass.ds(g // HKV * TB, TB), g % HKV]).then_inc(s["v_ready"], 1)

            pool.wait_ge(s["pad_done"], NPAD)
            take_v(0, 0)

            def step(g, k, par):
                if not isinstance(g, int) or g + 1 < NG:
                    if not (isinstance(g, int) and g < 2):
                        pool.wait_ge(s["pv_done"], (g - 1) * NU)
                    take_v(g + 1, (par + 1) % NBUF)
                for i, u in enumerate(DIAG):
                    tc, sb, off = width(u)
                    pool.wait_ge(s["exped"], 2 * NU * g + 2 * u + 2)
                    pool.sem_inc(s["mask_go"], 1)
                    blk = probs[u % 3][:, :, off:off + P]
                    nc.gpsimd.affine_select(out=blk, in_=blk, compare_op=ALU.is_ge, fill=0.0, base=0,
                                            pattern=[[0, G], [1, P]], channel_multiplier=-1).then_inc(s["masked"], 1)
            blocks(pool, NG, step, 2, 2, NBUF)

        @block.scalar
        def _(act):
            def step(g, k, par):
                for u in range(NU):
                    tc, sb, off = width(u)
                    if not (isinstance(g, int) and g == 0 and u < 3):
                        act.wait_ge(s["pv_done"], NU * g + u - 2)
                    for hp in range(2):
                        act.wait_ge(s["scored"], 2 * NU * g + 2 * u + hp + 1)
                        nc.scalar.activation(probs[u % 3][:, 2 * hp:2 * hp + 2, off:], s_ps[hp][:, :, off:],
                                             ACT.Exp).then_inc(s["exped"], 1)
            blocks(act, NG, step, 2, 2, NBUF)

        def maxima_beside(g, u):
            if u < TAIL:
                later, lo, n, i = 1, HEAD, NM - HEAD, u
            else:
                later, lo, n, i = 2, 0, HEAD, u - TAIL
            if isinstance(g, int) and g + later >= NG:
                return []
            of = TAIL if u < TAIL else NU - TAIL
            return [(g + later, later, m) for m in range(lo + n * i // of, lo + n * (i + 1) // of)]

        @block.vector
        def _(dve):
            def max_unit(g, m):
                tb, sc, h, heads, w = M[m]
                dve.wait_ge(s["m_scored"], NM * g + m + 1)
                nc.vector.tensor_reduce(negmax[:, sc, h:h + heads, tb],
                                        m_ps[m % 2][:, 0:heads * w].rearrange("p (h s) -> p h s", h=heads), AX.X,
                                        ALU.max, negate=True).then_inc(s["m_read"], 1)

            def combine(g):
                dve.wait_ge(s["m_read"], NM * (g + 1))
                out = shift[:].rearrange("p (h n) -> p h n", n=TB)
                nc.vector.tensor_tensor(out[:, :, CH // P:], negmax[:, 0, :, CH // P:], negmax[:, 1, :, CH // P:], ALU.min)
                nc.vector.tensor_copy(out[:, :, 0:CH // P], negmax[:, 0, :, 0:CH // P]).then_inc(s["combined"], 1)

            def take_shift(g, use, sent, before):
                dve.wait_ge(s["turned"], use + 1)
                if not (isinstance(g, int) and g == 0):
                    dve.wait_ge(shift_in[before], 32 * sent)
                nc.vector.tensor_copy(shiftT_h[:], t_ps[0:G * TB, 0:P]).then_inc(s["shift_hi"], 1)
                dve.wait_ge(s["shift_hi"], g + 1)
                nc.vector.tensor_tensor(shiftT_l[:], t_ps[0:G * TB, 0:P], f32(shiftT_h[:]), ALU.subtract).then_inc(s["shift_ready"], 1)
                dve.wait_ge(s["shift_ready"], g + 1)
                dve.sem_inc(s["turned_read"], 1)

            def copy_o(g, tc):
                dve.wait_ge(s["pv_done"], NU * g + (LAST0 + 1 if tc == 0 else NU))
                nc.vector.tensor_copy(o_sb[:, tc], o_ps[:]).then_inc(s["o_read"], 1)

            def normalise(g, tc, use, count):
                dve.wait_ge(s["turned"], use + 1)
                o = t_ps[:].rearrange("p (n h c) -> p n h c", h=G, c=2 * DH)
                nc.vector.reciprocal(rden[:], o[:, :, :, DH]).then_inc(s["rden_done"], 1)
                dve.wait_ge(s["rden_done"], count + 1)
                nc.vector.tensor_tensor(
                    r.AN[:, bass.ds(g // HKV * TB + tc * (CH // P), CH // P), bass.ds(g % HKV * (G * DH), G * DH)].rearrange(
                        "p n (h c) -> p n h c", c=DH),
                    o[:, :, :, 0:DH], rden[:].rearrange("p n (h a) -> p n h a", a=1).broadcast_to([P, CH // P, G, DH]),
                    ALU.mult).then_inc(s["turned_read"], 1)

            for m in range(NM):
                max_unit(0, m)
            combine(0)
            dve.wait_ge(s["combined"], 1)
            for m in range(HEAD // 2):
                max_unit(1, m)
            take_shift(0, 0, 0, 0)
            for m in range(HEAD // 2, HEAD):
                max_unit(1, m)

            def step(g, k, par):
                static = isinstance(g, int)
                more = not static or g + 1 < NG
                for u in range(NU):
                    if u == LAST0 + 2:
                        copy_o(g, 0)
                    if more and u == TURN_SHIFT:
                        combine(g + 1)
                        dve.wait_ge(s["combined"], g + 2)
                    for gm, later, m in maxima_beside(g, u):
                        max_unit(gm, m)
                    if u == TURN_O1 and not (static and g == 0):
                        normalise(g - 1, 1, 3 * g, 2 * g - 1)
                    if more and u == TURN_SHIFT:
                        take_shift(g + 1, 3 * g + 1, k + 1, par)
                    if u == TURN_O0:
                        normalise(g, 0, 3 * g + 2 if more else 3 * g + 1, 2 * g)
                copy_o(g, 1)
            blocks(dve, NG, step, 2, 2, NBUF)
            normalise(NG - 1, 1, 3 * NG - 1, 2 * NG - 1)

        @block.tensor
        def _(pe):
            def max_scores(g, k, par, m):
                tb, sc, h, heads, w = M[m]
                if m == 0:
                    pe.wait_ge(k_in[par], 64 * (k + 1))
                    pe.wait_ge(q0_in[par], 64 * (k + 1))
                if m == M_LATE:
                    pe.wait_ge(q1_in[par], 64 * (k + 1))
                if not (isinstance(g, int) and g == 0 and m < 2):
                    pe.wait_ge(s["m_read"], NM * g + m - 1)
                diag = tb * P - sc * CH
                bank = m_ps[m % 2]
                for j in range(heads):
                    last = nc.tensor.matmul(bank[:, j * w:(j + 1) * w], qs[par][0:SHIFT_ROW, h + j, tb * P:(tb + 1) * P],
                                            ks[par][0:SHIFT_ROW, sc * CH:sc * CH + w], start=(j == 0),
                                            stop=(diag >= CH and j == heads - 1), skip_group_check=True)
                if diag < CH:
                    last = nc.tensor.matmul(bank[:, 0:heads * w].rearrange("p (h s) -> p h s", h=heads)[:, :, diag:diag + P],
                                            r.ident_r[:], r.mask_r[:, 0:heads], start=False, stop=True,
                                            skip_group_check=True)
                last.then_inc(s["m_scored"], 1)

            def scores(g, u, hp, par):
                tc, sb, off = width(u)
                if not (isinstance(g, int) and g == 0 and u == 0):
                    pe.wait_ge(s["exped"], 2 * NU * g + 2 * u + hp - 1)
                for j in range(2):
                    h = 2 * hp + j
                    last = nc.tensor.matmul(s_ps[hp][:, j, off:], ks[par][:, sb * P:(sb + 1) * P],
                                            qs[par][:, h, tc * CH + off:(tc + 1) * CH], start=True, stop=True)
                last.then_inc(s["scored"], 1)

            def pv(g, u, par):
                tc, sb, off = width(u)
                pe.wait_ge(s["exped"], 2 * NU * g + 2 * u + 2)
                if u in DIAG:
                    pe.wait_ge(s["masked"], ND * g + DIAG.index(u) + 1)
                if u == 0:
                    pe.wait_ge(s["v_ready"], g + 1)
                if sb == 0 and not (isinstance(g, int) and g == 0 and tc == 0):
                    pe.wait_ge(s["o_read"], 2 * g + tc)
                for h in range(G):
                    last = nc.tensor.matmul(o_ps[2 * DH * h:2 * DH * (h + 1), off:], v[par][:, sb, :],
                                            probs[u % 3][:, h, off:], start=(sb == 0),
                                            stop=(sb == (tc + 1) * CH // P - 1), skip_group_check=True)
                last.then_inc(s["pv_done"], 1)

            def turn_o(g, tc, use):
                pe.wait_ge(s["o_read"], 2 * g + tc + 1)
                pe.wait_ge(s["turned_read"], use)
                for j in range(CH // P):
                    last = nc.tensor.transpose(t_ps[:, j * P:(j + 1) * P], o_sb[:, tc, j * P:(j + 1) * P], r.ident[:])
                last.then_inc(s["turned"], 1)

            def turn_shift(g, use):
                pe.wait_ge(s["combined"], g + 1)
                if not (isinstance(g, int) and g == 0):
                    pe.wait_ge(s["turned_read"], use)
                nc.tensor.transpose(t_ps[0:G * TB, 0:P], shift[:], r.ident[:]).then_inc(s["turned"], 1)

            pe.wait_ge(s["pad_done"], NPAD)
            for m in range(NM):
                max_scores(0, 0, 0, m)
            for m in range(HEAD // 2):
                max_scores(1, 0, 1, m)
            turn_shift(0, 0)
            for m in range(HEAD // 2, HEAD):
                max_scores(1, 0, 1, m)

            def step(g, k, par):
                static = isinstance(g, int)
                more = not static or g + 1 < NG
                pe.wait_ge(shift_in[par], 32 * (k + 1))
                for u in range(NU):
                    beside = [(gm, k + (par + later) // NBUF, (par + later) % NBUF, m)
                              for gm, later, m in maxima_beside(g, u)]
                    half = (len(beside) + 1) // 2
                    for hp in range(2):
                        for unit in beside[:half] if hp == 0 else beside[half:]:
                            max_scores(*unit)
                        scores(g, u, hp, par)
                    if u == TURN_O1 and not (static and g == 0):
                        turn_o(g - 1, 1, 3 * g)
                    if more and u == TURN_SHIFT:
                        turn_shift(g + 1, 3 * g + 1)
                    if u == TURN_O0:
                        turn_o(g, 0, 3 * g + 2 if more else 3 * g + 1)
                    if u >= 1:
                        pv(g, u - 1, par)
                pv(g, NU - 1, par)
            blocks(pe, NG, step, 2, 2, NBUF)
            turn_o(NG - 1, 1, 3 * NG - 1)


def phase_mix(nc, d, r, w):
    with ExitStack() as ctx:
        sb = lambda n, s, t=F32: ctx.enter_context(nc.sbuf_tensor(n, s, t))
        an = sb("an", [P, 2, D])
        aT_h = [sb(f"aT_h{i}", [P, KT, P], F32R) for i in range(2)]
        aT_l = [sb(f"aT_l{i}", [P, KT, P], F32R) for i in range(2)]
        stats = sb("stats1", [P, 2, 6])
        moments = sb("moments1", [P, 2, 2])
        std = sb("std1", [P, 2])
        rstd = sb("rstd1", [P, 2])
        xn = sb("xn1", [P, 2, D])
        xT = [sb(f"xT_full{i}", [P, KT, P]) for i in range(2)]
        router_w = sb("router_w", [P, KT, E])
        router_b = sb("router_b", [P, E])
        ps = lambda n: ctx.enter_context(nc.psum_tensor(n, [P, D], F32))
        a_turn = [ps("a_turn0"), ps("a_turn1")]
        o_ps = [ps("mix_ps0"), ps("mix_ps1")]
        x_turn = [ps("x1_turn0"), ps("x1_turn1")]
        l_ps = ps("logits_ps")
        s = semaphores(nc, ctx, "m", "router_in an_ready a_turned ahi_ready alo_ready mixed added stats_done moments_done "
                 "std_done rstd_done xn_ready xn_kept x_turned xhi_ready xlo_ready logits_done logits_read copy_go stats_go")
        block = ctx.enter_context(nc.Block())
        tiles = lambda ap: ap.rearrange("p (k t) -> p k t", k=KT)

        @block.sync
        def _(sp):
            sp.dma_start(router_w[:], d["router_w"].rearrange("(k p) e -> p k e", p=P)).then_inc(s["router_in"], 16)
            sp.dma_start(router_b[:], d["router_b"].rearrange("(a e) -> a e", a=1).broadcast_to([P, E])).then_inc(s["router_in"], 16)
            sp.wait_ge(s["router_in"], 32)

        @block.gpsimd
        def _(pool):
            def stage(n, par):
                if not (isinstance(n, int) and n < 2):
                    pool.wait_ge(s["a_turned"], n - 1)
                    pool.sem_inc(s["copy_go"], 1)
                nc.gpsimd.tensor_copy(an[:, par], r.AN[:, n]).then_inc(s["an_ready"], 1)

            def keep(n, par):
                pool.wait_ge(s["xn_ready"], n + 1)
                pool.sem_inc(s["copy_go"], 1)
                nc.gpsimd.tensor_copy(r.AN[:, n], xn[:, par]).then_inc(s["xn_kept"], 1)

            stage(0, 0)
            stage(1, 1)

            def step(n, k, par):
                if not isinstance(n, int) or n + 2 < NB:
                    stage(n + 2, par)
                keep(n, par)
            blocks(pool, NB, step)

        @block.scalar
        def _(act):
            def high_a(n, par):
                act.wait_ge(s["a_turned"], n + 1)
                if not (isinstance(n, int) and n < 2):
                    act.wait_ge(s["mixed"], n - 1)
                nc.scalar.copy(aT_h[par][:], tiles(a_turn[par][:])).then_inc(s["ahi_ready"], 1)

            def root(n, par):
                act.wait_ge(s["moments_done"], n + 1)
                nc.scalar.activation(std[:, par:par + 1], moments[:, par, 1:2], ACT.Sqrt, bias=r.eps[:]).then_inc(s["std_done"], 1)

            def high_x(n, par):
                act.wait_ge(s["x_turned"], n + 1)
                if not (isinstance(n, int) and n < 2):
                    act.wait_ge(s["logits_done"], n - 1)
                nc.scalar.copy(xT[par][:], tiles(x_turn[par][:])).then_inc(s["xhi_ready"], 1)
                nc.scalar.copy(r.XH[:, :, bass.ds(n * P, P)], tiles(x_turn[par][:])).then_inc(s["xhi_ready"], 1)

            high_a(0, 0)

            def step(n, k, par):
                static = isinstance(n, int)
                if not static or n + 1 < NB:
                    high_a(n + 1, 1 - par)
                if not static or n >= 1:
                    high_x(n - 1, 1 - par)
                root(n, par)
            blocks(act, NB, step)
            high_x(NB - 1, 1)

        @block.vector
        def _(dve):
            def low_a(n, par):
                dve.wait_ge(s["ahi_ready"], n + 1)
                nc.vector.tensor_tensor(aT_l[par][:], tiles(a_turn[par][:]), f32(aT_h[par][:]), ALU.subtract).then_inc(s["alo_ready"], 1)

            def add(n, par):
                dve.wait_ge(s["mixed"], n + 1)
                nc.vector.tensor_tensor(r.Y[:, n], o_ps[par][:], r.Y[:, n], ALU.add).then_inc(s["added"], 1)
                dve.wait_ge(s["added"], n + 1)
                dve.sem_inc(s["stats_go"], 1)
                nc.vector.bn_stats(stats[:, par], r.Y[:, n]).then_inc(s["stats_done"], 1)

            def low_x(n, par):
                dve.wait_ge(s["xhi_ready"], 2 * n + 2)
                nc.vector.tensor_tensor(r.XL[:, :, bass.ds(n * P, P)], tiles(x_turn[par][:]), f32(r.XH[:, :, bass.ds(n * P, P)]), ALU.subtract).then_inc(s["xlo_ready"], 1)

            def norm(n, par):
                nc.vector.bn_aggr(moments[:, par], stats[:, par]).then_inc(s["moments_done"], 1)
                dve.wait_ge(s["std_done"], n + 1)
                nc.vector.reciprocal(rstd[:, par:par + 1], std[:, par:par + 1]).then_inc(s["rstd_done"], 1)
                dve.wait_ge(s["rstd_done"], n + 1)
                if not (isinstance(n, int) and n < 2):
                    dve.wait_ge(s["xn_kept"], n - 1)
                nc.vector.tensor_scalar(xn[:, par], r.Y[:, n], moments[:, par, 0:1], rstd[:, par:par + 1],
                                        ALU.subtract, ALU.mult).then_inc(s["xn_ready"], 1)

            def take_logits(n):
                dve.wait_ge(s["logits_done"], n + 1)
                nc.vector.tensor_tensor(r.LG[:, n], l_ps[:, 0:E], router_b[:], ALU.add).then_inc(s["logits_read"], 1)

            dve.wait_ge(s["router_in"], 32)
            low_a(0, 0)

            def step(n, k, par):
                static = isinstance(n, int)
                if not static or n + 1 < NB:
                    low_a(n + 1, 1 - par)
                add(n, par)
                dve.wait_ge(s["stats_done"], n + 1)
                if not static or n >= 1:
                    low_x(n - 1, 1 - par)
                norm(n, par)
                if not static or n >= 2:
                    take_logits(n - 2)
            blocks(dve, NB, step)
            low_x(NB - 1, 1)
            take_logits(NB - 2)
            take_logits(NB - 1)

        @block.tensor
        def _(pe):
            def turn_a(n, par):
                pe.wait_ge(s["an_ready"], n + 1)
                if not (isinstance(n, int) and n < 2):
                    pe.wait_ge(s["alo_ready"], n - 1)
                for k in range(KT):
                    last = nc.tensor.transpose(a_turn[par][:, k * P:(k + 1) * P], an[:, par, k * P:(k + 1) * P], r.ident[:])
                last.then_inc(s["a_turned"], 1)

            def mix(n, par):
                pe.wait_ge(s["alo_ready"], n + 1)
                if not (isinstance(n, int) and n < 2):
                    pe.wait_ge(s["added"], n - 1)
                for k in range(KT):
                    last = split_matmuls(nc, o_ps[par][:], (aT_h[par][:, k], aT_l[par][:, k]), (w.o_h[:, k], w.o_l[:, k]), k)
                last.then_inc(s["mixed"], 1)

            def turn_x(n, par):
                pe.wait_ge(s["xn_ready"], n + 1)
                if not (isinstance(n, int) and n < 2):
                    pe.wait_ge(s["xlo_ready"], n - 1)
                for k in range(KT):
                    last = nc.tensor.transpose(x_turn[par][:, k * P:(k + 1) * P], xn[:, par, k * P:(k + 1) * P], r.ident[:])
                last.then_inc(s["x_turned"], 1)

            def logits(n, par):
                pe.wait_ge(s["xhi_ready"], 2 * n + 1)
                if not (isinstance(n, int) and n < 1):
                    pe.wait_ge(s["logits_read"], n)
                for k in range(KT):
                    last = nc.tensor.matmul(l_ps[:, 0:E], xT[par][:, k], router_w[:, k], start=(k == 0), stop=(k == KT - 1))
                last.then_inc(s["logits_done"], 1)

            pe.wait_ge(s["router_in"], 32)
            turn_a(0, 0)

            def step(n, k, par):
                static = isinstance(n, int)
                if not static or n + 1 < NB:
                    turn_a(n + 1, 1 - par)
                mix(n, par)
                if not static or n >= 2:
                    logits(n - 2, par)
                if not static or n >= 1:
                    turn_x(n - 1, 1 - par)
            blocks(pe, NB, step)
            logits(NB - 2, 0)
            turn_x(NB - 1, 1)
            logits(NB - 1, 1)


def phase_bind(nc, d, r):
    U = units()
    NU = len(U)
    DIAG = [u for u, (tc, sb) in enumerate(U) if sb * P >= tc * CH]
    ND = len(DIAG)
    NG = B * BH
    SCALE = 4.0 * float(np.float32(BD ** -0.5))
    with ExitStack() as ctx:
        sb_ = lambda n, s, t=F32: ctx.enter_context(nc.sbuf_tensor(n, s, t))
        bv = sb_("bv", [P, 3, BH, BD])
        alpha = sb_("alpha", [P, 3, BH])
        sign = sb_("sign", [P, 3, BH, BD])
        bind = sb_("bind", [P, 3, BH, BD])
        cols = sb_("bind_cols", [P, 2, BH])
        xs = [sb_(f"xs{i}", [P, T]) for i in range(2)]
        qT = [sb_(f"qT{i}", [P, T]) for i in range(2)]
        kT = [sb_(f"kT{i}", [P, T]) for i in range(2)]
        vb = [sb_(f"vb{i}", [P, TB, BD]) for i in range(2)]
        gate = [sb_(f"gate{i}", [P, CH]) for i in range(3)]
        s_ps = [ctx.enter_context(nc.psum_tensor(f"bs_ps{i}", [P, CH], F32)) for i in range(3)]
        o_ps = [ctx.enter_context(nc.psum_tensor(f"bo_ps{i}", [P, CH], F32)) for i in range(2)]
        c_ps = [ctx.enter_context(nc.psum_tensor(f"bc_ps{i}", [P, CH], F32)) for i in range(2)]
        s = semaphores(nc, ctx, "b", "bv_in summed alpha_done sign_done hard_done less_done bound turned cols_done xs_ready "
                 "q_ready k_ready v_ready scored gated masked pv_done added mask_go")
        block = ctx.enter_context(nc.Block())

        def width(u):
            tc, sb = U[u]
            return tc, sb, max(0, sb * P - tc * CH)

        @block.sync
        def _(sp):
            for i, src in enumerate((d["bvq"], d["bvk"], d["bvv"])):
                sp.dma_start(bv[:, i], src.rearrange("(a h) c -> a h c", a=1).broadcast_to([P, BH, BD])).then_inc(s["bv_in"], 16)
            sp.wait_ge(s["bv_in"], 48)

        @block.gpsimd
        def _(pool):
            def prepare(g, par, first=False):
                b, h = g // BH, g % BH
                if not first:
                    pool.wait_ge(s["k_ready"], g - 1)
                    pool.wait_ge(s["pv_done"], NU * (g - 1))
                nc.gpsimd.tensor_tensor(xs[par][:], f32(r.XH[:, h, bass.ds(b * T, T)]), f32(r.XL[:, h, bass.ds(b * T, T)]),
                                        ALU.add).then_inc(s["xs_ready"], 1)
                nc.gpsimd.tensor_tensor(vb[par][:], r.AN[:, bass.ds(b * TB, TB), bass.ds(h * BD, BD)],
                                        bind[:, 2, bass.ds(h, 1), :].broadcast_to([P, TB, BD]), ALU.mult).then_inc(s["v_ready"], 1)

            pool.wait_ge(s["bound"], 1)
            prepare(0, 0, True)
            prepare(1, 1, True)

            def step(g, k, par):
                for u in DIAG:
                    tc, sb, off = width(u)
                    pool.wait_ge(s["gated"], NU * g + u + 1)
                    pool.sem_inc(s["mask_go"], 1)
                    blk = gate[u % 3][:, off:off + P]
                    nc.gpsimd.affine_select(out=blk, in_=blk, compare_op=ALU.is_ge, fill=0.0, base=0,
                                            pattern=[[1, P]], channel_multiplier=-1).then_inc(s["masked"], 1)
                if not isinstance(g, int) or g + 2 < NG:
                    prepare(g + 2, par)
            blocks(pool, NG, step, 1, 3)

        @block.scalar
        def _(act):
            def step(g, k, par):
                for u in range(NU):
                    tc, sb, off = width(u)
                    act.wait_ge(s["scored"], NU * g + u + 1)
                    if not (isinstance(g, int) and g == 0 and u < 3):
                        act.wait_ge(s["pv_done"], NU * g + u - 2)
                    nc.scalar.activation(gate[u % 3][:, off:], s_ps[u % 3][:, off:], ACT.Sigmoid, scale=SCALE).then_inc(s["gated"], 1)
            blocks(act, NG, step, 1, 1)

        @block.vector
        def _(dve):
            dve.wait_ge(s["bv_in"], 48)
            nc.vector.tensor_reduce(alpha[:], bv[:], AX.X, ALU.add, apply_absolute_value=True).then_inc(s["summed"], 1)
            nc.vector.tensor_scalar(sign[:], bv[:], 0.0, 2.0, ALU.is_ge, ALU.mult).then_inc(s["sign_done"], 1)
            dve.wait_ge(s["summed"], 1)
            nc.vector.tensor_scalar(alpha[:], alpha[:], 1.0 / BD, None, ALU.mult).then_inc(s["alpha_done"], 1)
            dve.wait_ge(s["sign_done"], 1)
            nc.vector.tensor_scalar(sign[:], sign[:], -1.0, None, ALU.add).then_inc(s["sign_done"], 1)
            dve.wait_ge(s["sign_done"], 2)
            dve.wait_ge(s["alpha_done"], 1)
            nc.vector.tensor_tensor(bind[:], sign[:], alpha[:].rearrange("p i (h a) -> p i h a", a=1).broadcast_to(
                [P, 3, BH, BD]), ALU.mult).then_inc(s["hard_done"], 1)
            dve.wait_ge(s["hard_done"], 1)
            nc.vector.tensor_tensor(sign[:], bind[:], bv[:], ALU.subtract).then_inc(s["less_done"], 1)
            dve.wait_ge(s["less_done"], 1)
            nc.vector.tensor_tensor(bind[:], sign[:], bv[:], ALU.add).then_inc(s["bound"], 1)
            dve.wait_ge(s["turned"], 1)
            for i in range(2):
                last = nc.vector.tensor_copy(cols[:, i], c_ps[i][:].rearrange("p (h c) -> p h c", h=BH)[:, :, 0])
            last.then_inc(s["cols_done"], 1)
            dve.wait_ge(s["cols_done"], 1)

            def make_qk(g, par, first=False):
                h = g % BH
                dve.wait_ge(s["xs_ready"], g + 1)
                if not first:
                    dve.wait_ge(s["scored"], NU * (g - 1))
                nc.vector.tensor_scalar(qT[par][:], xs[par][:], cols[:, 0, bass.ds(h, 1)], None, ALU.mult).then_inc(s["q_ready"], 1)
                nc.vector.tensor_scalar(kT[par][:], xs[par][:], cols[:, 1, bass.ds(h, 1)], None, ALU.mult).then_inc(s["k_ready"], 1)

            make_qk(0, 0, True)
            make_qk(1, 1, True)

            def step(g, k, par):
                b, h = g // BH, g % BH
                for tc in range(2):
                    dve.wait_ge(s["pv_done"], NU * g + (CH // P if tc == 0 else NU))
                    y = r.Y[:, bass.ds(b * TB + tc * (CH // P), CH // P), bass.ds(h * BD, BD)]
                    nc.vector.tensor_tensor(y, o_ps[tc][:].rearrange("p (n c) -> p n c", c=BD), y, ALU.add).then_inc(s["added"], 1)
                if not isinstance(g, int) or g + 2 < NG:
                    make_qk(g + 2, par)
            blocks(dve, NG, step, 1, 3)

        @block.tensor
        def _(pe):
            pe.wait_ge(s["bound"], 1)
            for i in range(2):
                for h in range(BH):
                    last = nc.tensor.transpose(c_ps[i][:, h * BD:(h + 1) * BD], bind[:, i, h], r.ident[:])
            last.then_inc(s["turned"], 1)

            def scores(g, u, par):
                tc, sb, off = width(u)
                if u == 0:
                    pe.wait_ge(s["k_ready"], g + 1)
                if not (isinstance(g, int) and g == 0 and u < 3):
                    pe.wait_ge(s["gated"], NU * g + u - 2)
                nc.tensor.matmul(s_ps[u % 3][:, off:], kT[par][:, sb * P:(sb + 1) * P],
                                 qT[par][:, tc * CH + off:(tc + 1) * CH], start=True, stop=True).then_inc(s["scored"], 1)

            def pv(g, u, par):
                tc, sb, off = width(u)
                pe.wait_ge(s["gated"], NU * g + u + 1)
                if u in DIAG:
                    pe.wait_ge(s["masked"], ND * g + DIAG.index(u) + 1)
                if u == 0:
                    pe.wait_ge(s["v_ready"], g + 1)
                if sb == 0 and not (isinstance(g, int) and g == 0):
                    pe.wait_ge(s["added"], 2 * g - 1 + tc)
                for j in range(off // P, CH // P):
                    last = nc.tensor.matmul(o_ps[tc][:, j * P:(j + 1) * P], gate[u % 3][:, j * P:(j + 1) * P], vb[par][:, sb],
                                            start=(sb == 0 and j == 0), stop=(sb == tc * CH // P + j), skip_group_check=True)
                last.then_inc(s["pv_done"], 1)

            def step(g, k, par):
                for u in range(NU):
                    scores(g, u, par)
                    if u >= 1:
                        pv(g, u - 1, par)
                pv(g, NU - 1, par)
            blocks(pe, NG, step, 1, 1)


def phase_route(nc, d, r):
    BIG = float(2 ** 100)
    with ExitStack() as ctx:
        sb = lambda n, s, t=F32: ctx.enter_context(nc.sbuf_tensor(n, s, t))
        NGR = E // EG
        rb = sb("router_bias", [P, E])
        b3 = sb("b3", [E + 1, D])
        top = sb("top", [P, NB])
        less = sb("less", [P, NB, E])
        ex = sb("ex", [P, NB, E])
        den = sb("den", [P, NB])
        rden = sb("rden1", [P, NB])
        prob = sb("prob", [P, NB, E])
        sc = sb("route_scores", [P, NB, E])
        desc = sb("desc", [P, E])
        desc_i = sb("desc_i", [P, E], mybir.dt.int32)
        gm = sb("gm", [P, NB, EG])
        gate_T = sb("gate_T", [E + 1, NB * P])
        tmp = {k: (sb(f"best_{k}", [P, NB]), sb(f"eq_{k}", [P, NB, E]), sb(f"rank_{k}", [P, NB, E]),
                   sb(f"least_{k}", [P, NB]), sb(f"hot_{k}", [P, NB, E])) for k in ("g0", "g1", "e0", "e1")}
        keep = sb("keep", [P, NB, EG])
        pen = sb("pen", [P, NB, EG])
        masked = sb("masked", [P, NB, E])
        again = sb("again", [P, NB, E])
        chosen = sb("chosen", [P, NB, E])
        t_ps = [ctx.enter_context(nc.psum_tensor(f"gt_ps{i}", [P, CH], F32)) for i in range(NCH)]
        y_ps = [ctx.enter_context(nc.psum_tensor(f"b3_ps{i}", [P, D], F32)) for i in range(4)]
        s = semaphores(nc, ctx, "r", "in_done less_done exp_done gates turned copied biased added iota_done chain")
        block = ctx.enter_context(nc.Block())
        wide = lambda ap, k: ap.rearrange("p (n a) -> p n a", a=1).broadcast_to([P, NB, k])

        @block.sync
        def _(sp):
            sp.dma_start(rb[:], d["router_bias"].rearrange("(a e) -> a e", a=1).broadcast_to([P, E])).then_inc(s["in_done"], 16)
            sp.dma_start(b3[0:E], d["eb3"]).then_inc(s["in_done"], 16)
            sp.dma_start(b3[E:E + 1], d["sb3"].rearrange("(a e) -> a e", a=1)).then_inc(s["in_done"], 16)
            sp.wait_ge(s["in_done"], 48)

        @block.gpsimd
        def _(pool):
            nc.gpsimd.iota(desc_i[:], pattern=[[-1, E]], base=E, channel_multiplier=0).then_inc(s["iota_done"], 1)

        @block.scalar
        def _(act):
            act.wait_ge(s["less_done"], 1)
            nc.scalar.activation(ex[:], less[:], ACT.Exp).then_inc(s["exp_done"], 1)

        @block.vector
        def _(dve):
            count = [0]

            def done(ins):
                count[0] += 1
                ins.then_inc(s["chain"], 1)
                dve.wait_ge(s["chain"], count[0])

            V = nc.vector

            def first_best(key, vals, k):
                best, eq, rank, least, hot = tmp[key]
                done(V.tensor_reduce(best[:], vals, AX.X, ALU.max))
                done(V.tensor_tensor(eq[:, :, 0:k], vals, wide(best[:], k), ALU.is_equal))
                done(V.tensor_tensor(rank[:, :, 0:k], eq[:, :, 0:k],
                                     desc[:, 0:k].rearrange("p (a e) -> p a e", a=1).broadcast_to([P, NB, k]), ALU.mult))
                done(V.tensor_reduce(least[:], rank[:, :, 0:k], AX.X, ALU.max))
                done(V.tensor_tensor(hot[:, :, 0:k], rank[:, :, 0:k], wide(least[:], k), ALU.is_equal))
                return hot[:, :, 0:k]

            done(V.tensor_reduce(top[:], r.LG[:], AX.X, ALU.max))
            V.tensor_tensor(less[:], r.LG[:], wide(top[:], E), ALU.subtract).then_inc(s["less_done"], 1)
            dve.wait_ge(s["exp_done"], 1)
            done(V.tensor_reduce(den[:], ex[:], AX.X, ALU.add))
            done(V.reciprocal(rden[:], den[:]))
            done(V.tensor_tensor(prob[:], ex[:], wide(rden[:], E), ALU.mult))
            dve.wait_ge(s["in_done"], 48)
            dve.wait_ge(s["iota_done"], 1)
            done(V.tensor_copy(desc[:], desc_i[:]))
            done(V.tensor_tensor(sc[:], prob[:], rb[:].rearrange("p (a e) -> p a e", a=1).broadcast_to([P, NB, E]), ALU.add))
            done(V.tensor_reduce(gm[:], sc[:].rearrange("p n (g e) -> p n g e", e=NGR), AX.X, ALU.max))
            hot0 = first_best("g0", gm[:], EG)
            done(V.scalar_tensor_tensor(again[:, :, 0:EG], hot0, -BIG, gm[:], ALU.mult, ALU.add))
            hot1 = first_best("g1", again[:, :, 0:EG], EG)
            done(V.tensor_tensor(keep[:], hot0, hot1, ALU.add))
            done(V.tensor_scalar(pen[:], keep[:], -1.0, BIG, ALU.add, ALU.mult))
            done(V.tensor_tensor(masked[:].rearrange("p n (g e) -> p n g e", e=NGR),
                                 sc[:].rearrange("p n (g e) -> p n g e", e=NGR),
                                 pen[:].rearrange("p n (g a) -> p n g a", a=1).broadcast_to([P, NB, EG, NGR]), ALU.add))
            hot0 = first_best("e0", masked[:], E)
            done(V.scalar_tensor_tensor(again[:], hot0, -2.0 * BIG, masked[:], ALU.mult, ALU.add))
            hot1 = first_best("e1", again[:], E)
            done(V.tensor_tensor(chosen[:], hot0, hot1, ALU.add))
            V.memset(r.gates[:, :, E:NE], 1.0).then_inc(s["gates"], 1)
            V.tensor_tensor(r.gates[:, :, 0:E], chosen[:], sc[:], ALU.mult).then_inc(s["gates"], 1)
            for c in range(NCH):
                dve.wait_ge(s["turned"], c + 1)
                V.tensor_copy(gate_T[:, c * CH:(c + 1) * CH], t_ps[c][0:E + 1, :]).then_inc(s["copied"], 1)
            for n in range(NB):
                dve.wait_ge(s["biased"], n + 1)
                V.tensor_tensor(r.Y[:, n], y_ps[n % 4][:], r.Y[:, n], ALU.add).then_inc(s["added"], 1)

        @block.tensor
        def _(pe):
            pe.wait_ge(s["gates"], 2)
            pe.wait_ge(s["in_done"], 48)
            for c in range(NCH):
                for j in range(CH // P):
                    last = nc.tensor.transpose(t_ps[c][0:E + 1, j * P:(j + 1) * P], r.gates[:, c * (CH // P) + j, 0:E + 1],
                                               r.ident[:])
                last.then_inc(s["turned"], 1)
            for n in range(NB):
                pe.wait_ge(s["copied"], n // (CH // P) + 1)
                if n >= 4:
                    pe.wait_ge(s["added"], n - 3)
                nc.tensor.matmul(y_ps[n % 4][:], gate_T[:, n * P:(n + 1) * P], b3[:], start=True, stop=True).then_inc(s["biased"], 1)


def phase_experts(nc, d, r):
    with ExitStack() as ctx:
        sb = lambda n, s, t=F32: ctx.enter_context(nc.sbuf_tensor(n, s, t))
        raw = [sb(f"w_raw{i}", [P, 3, D]) for i in range(2)]
        w_h = [sb(f"w_h{i}", [P, 3, D], F32R) for i in range(2)]
        w_l = [sb(f"w_l{i}", [P, 3, D], F32R) for i in range(2)]
        b1 = sb("b1", [P, NE])
        b2 = sb("b2", [P, NE])
        sil = [sb(f"sil{i}", [P, CH]) for i in range(2)]
        hid = [sb(f"hid{i}", [P, CH]) for i in range(2)]
        hid_h = [sb(f"hid_h{i}", [P, CH], F32R) for i in range(2)]
        hid_l = [sb(f"hid_l{i}", [P, CH], F32R) for i in range(2)]
        h1_ps = [ctx.enter_context(nc.psum_tensor(f"h1_ps{i}", [P, CH], F32)) for i in range(2)]
        h2_ps = [ctx.enter_context(nc.psum_tensor(f"h2_ps{i}", [P, CH], F32)) for i in range(2)]
        y_ps = [ctx.enter_context(nc.psum_tensor(f"y_ps{i}", [P, D], F32)) for i in range(4)]
        s = semaphores(nc, ctx, "e", "b_in w_in0 w_in1 whi_ready wlo_ready up1_done up2_done sil_done hid_done hhi_done "
                 "hlo_done down_done y_added stored go act_go")
        w_in = [s["w_in0"], s["w_in1"]]
        block = ctx.enter_context(nc.Block())
        NJ = CH // P

        @block.sync
        def _(sp):
            def load(e, par):
                if isinstance(e, int) and e >= E:
                    half = slice((e - E) * INTER, (e - E + 1) * INTER)
                    w1, w2, w3 = d["sw1"][:, half], d["sw2"][:, half], d["sw3"][half, :]
                else:
                    w1, w2, w3 = d["ew1"][e], d["ew2"][e], d["ew3"][e]
                for i, src in enumerate((w1, w2)):
                    sp.dma_start(raw[par][:, i].rearrange("p (k i) -> p k i", k=KT),
                                 src.rearrange("(k p) i -> p k i", p=P)).then_inc(w_in[par], 16)
                sp.dma_start(raw[par][:, 2], w3).then_inc(w_in[par], 16)

            load(0, 0)
            with nc.allow_non_contiguous_dma("biases with the hidden units on partitions"):
                for dst, eb, sb_ in ((b1, d["eb1"], d["sb1"]), (b2, d["eb2"], d["sb2"])):
                    sp.dma_start(dst[:, 0:E], eb.rearrange("e i -> i e")).then_inc(s["b_in"], 16)
                    sp.dma_start(dst[:, E:NE], sb_.rearrange("(h i) -> i h", h=2)).then_inc(s["b_in"], 16)
            load(1, 1)

            def step(e, k, par):
                if not isinstance(e, int) or e + 2 < NE:
                    sp.wait_ge(s["wlo_ready"], e + 1)
                    load(e + 2, par)
            blocks(sp, NE, step, 2, 4)
            yv = d["out"].rearrange("b t d -> (b t) d").rearrange("(n p) d -> p n d", p=P)
            for c in range(NCH):
                sp.wait_ge(s["y_added"], NB * (NE - 1) + NJ * (c + 1))
                sp.dma_start(yv[:, c * NJ:(c + 1) * NJ], r.Y[:, c * NJ:(c + 1) * NJ]).then_inc(s["stored"], 16)
            sp.wait_ge(s["stored"], 16 * NCH)

        @block.gpsimd
        def _(pool):
            def split(e, k, par, first=False):
                pool.wait_ge(w_in[par], 48 * (k + 1))
                if not first:
                    pool.wait_ge(s["down_done"], NCH * (e - 1))
                pool.sem_inc(s["go"], 1)
                nc.gpsimd.tensor_copy(w_h[par][:], raw[par][:]).then_inc(s["whi_ready"], 1)
                pool.wait_ge(s["whi_ready"], e + 1)
                nc.gpsimd.tensor_tensor(w_l[par][:], raw[par][:], f32(w_h[par][:]), ALU.subtract).then_inc(s["wlo_ready"], 1)

            split(0, 0, 0, True)

            def step(e, k, par):
                for c in range(NCH):
                    q = e * NCH + c
                    pool.wait_ge(s["hhi_done"], q + 1)
                    nc.gpsimd.tensor_tensor(hid_l[c % 2][:], hid[c % 2][:], f32(hid_h[c % 2][:]), ALU.subtract).then_inc(s["hlo_done"], 1)
                    if c == 1 and (not isinstance(e, int) or e + 1 < NE):
                        split(e + 1, k + 1 if par else k, 1 - par, isinstance(e, int) and e == 0)
            blocks(pool, NE, step, 2, 4)

        @block.scalar
        def _(act):
            act.wait_ge(s["b_in"], 64)

            def step(e, k, par):
                for c in range(NCH):
                    q, i = e * NCH + c, c % 2
                    act.wait_ge(s["up1_done"], q + 1)
                    if not (isinstance(e, int) and e == 0 and c < 2):
                        act.wait_ge(s["hid_done"], q - 1)
                    act.sem_inc(s["act_go"], 1)
                    nc.scalar.activation(sil[i][:], h1_ps[i][:], ACT.Silu, bias=b1[:, bass.ds(e, 1)]).then_inc(s["sil_done"], 1)
                    act.wait_ge(s["hid_done"], q + 1)
                    if not (isinstance(e, int) and e == 0 and c < 2):
                        act.wait_ge(s["down_done"], q - 1)
                    nc.scalar.copy(hid_h[i][:], hid[i][:]).then_inc(s["hhi_done"], 1)
            blocks(act, NE, step, 2, 4)

        @block.vector
        def _(dve):
            dve.wait_ge(s["b_in"], 64)

            def gather(e, c, q):
                for j in range(NJ):
                    n = c * NJ + j
                    dve.wait_ge(s["down_done"], q + 1)
                    nc.vector.scalar_tensor_tensor(r.Y[:, n], y_ps[j][:], r.gates[:, n, bass.ds(e, 1)], r.Y[:, n],
                                                   ALU.mult, ALU.add).then_inc(s["y_added"], 1)

            def step(e, k, par):
                for c in range(NCH):
                    q, i = e * NCH + c, c % 2
                    dve.wait_ge(s["up2_done"], q + 1)
                    dve.wait_ge(s["sil_done"], q + 1)
                    if not (isinstance(e, int) and e == 0 and c < 2):
                        dve.wait_ge(s["hlo_done"], q - 1)
                    nc.vector.scalar_tensor_tensor(hid[i][:], h2_ps[i][:], b2[:, bass.ds(e, 1)], sil[i][:],
                                                   ALU.add, ALU.mult).then_inc(s["hid_done"], 1)
                    if c >= 1:
                        gather(e, c - 1, q - 1)
                    elif not (isinstance(e, int) and e == 0):
                        gather(e - 1, NCH - 1, q - 1)
            blocks(dve, NE, step, 2, 4)
            gather(NE - 1, NCH - 1, NE * NCH - 1)

        @block.tensor
        def _(pe):
            def up(e, c, par):
                q, i = e * NCH + c, c % 2
                if c == 0:
                    pe.wait_ge(s["wlo_ready"], e + 1)
                if not (isinstance(e, int) and e == 0 and c < 2):
                    pe.wait_ge(s["hid_done"], q - 1)
                for m, (out, done) in enumerate(((h1_ps[i], s["up1_done"]), (h2_ps[i], s["up2_done"]))):
                    for k in range(KT):
                        last = split_matmuls(
                            nc, out[:], (w_h[par][:, m, k * P:(k + 1) * P], w_l[par][:, m, k * P:(k + 1) * P]),
                            (r.XH[:, k, c * CH:(c + 1) * CH], r.XL[:, k, c * CH:(c + 1) * CH]), k)
                    last.then_inc(done, 1)

            def down(q, c, par):
                pe.wait_ge(s["hlo_done"], q + 1)
                i = c % 2
                if not (isinstance(q, int) and q == 0):
                    pe.wait_ge(s["y_added"], NJ * q)
                for j in range(NJ):
                    t = slice(j * P, (j + 1) * P)
                    nc.tensor.matmul(y_ps[j][:], hid_h[i][:, t], w_h[par][:, 2], start=True, stop=False)
                    nc.tensor.matmul(y_ps[j][:], hid_h[i][:, t], w_l[par][:, 2], start=False, stop=False)
                    last = nc.tensor.matmul(y_ps[j][:], hid_l[i][:, t], w_h[par][:, 2], start=False, stop=True)
                last.then_inc(s["down_done"], 1)

            def step(e, k, par):
                for c in range(NCH):
                    up(e, c, par)
                    if c >= 1:
                        down(e * NCH + c - 1, c - 1, par)
                    elif not (isinstance(e, int) and e == 0):
                        down(e * NCH - 1, NCH - 1, 1 - par)
            blocks(pe, NE, step, 2, 4)
            down(NE * NCH - 1, NCH - 1, (NE - 1) % 2)


def program(nc, d):
    r, w = Buffers(), Buffers()
    with ExitStack() as ctx:
        sb = sb_late = lambda n, s, t=F32: ctx.enter_context(nc.sbuf_tensor(n, s, t))
        r.Y = sb("Y", [P, NB, D])
        r.AN = sb("AN", [P, NB, D])
        r.ident = sb("ident", [P, P])
        r.ident_r = sb("ident_r", [P, P], F32R)
        r.mask_r = sb("mask_r", [P, G, P], F32R)
        r.eps = sb("eps", [P, 1])
        w.o_h = sb("wo_h", [P, KT, D], F32R)
        w.o_l = sb("wo_l", [P, KT, D], F32R)
        r.qk_dram = nc.dram_tensor("qk_turned", [2, QK, B * T], F32, kind="Internal").ap()
        with ExitStack() as early:
            sb = lambda n, s, t=F32: early.enter_context(nc.sbuf_tensor(n, s, t))
            r.V = sb("V", [P, NB, HKV, 2 * DH])
            with ExitStack() as first:
                sb = lambda n, s, t=F32: first.enter_context(nc.sbuf_tensor(n, s, t))
                r.mask = sb("mask", [P, P])
                r.cos = sb("cos", [P, NB, DH])
                r.sin = sb("sin", [P, NB, DH])
                r.bias = sb("bias", [P, D])
                w.qkv_h = sb("wqkv_h", [P, KT, QK + P], F32R)
                w.qkv_l = sb("wqkv_l", [P, KT, QK + P], F32R)
                w.l_h = sb("wl_h", [P, KT, D], F32R)
                w.l_l = sb("wl_l", [P, KT, D], F32R)
                phase_weights(nc, d, r, w)
                phase_project(nc, d, r, w)
            phase_attention(nc, d, r)
        r.XH = sb_late("x1T_hi", [P, KT, B * T], F32R)
        r.XL = sb_late("x1T_lo", [P, KT, B * T], F32R)
        r.LG = sb_late("logits", [P, NB, E])
        r.gates = sb_late("gates", [P, NB, NE])
        phase_mix(nc, d, r, w)
        phase_bind(nc, d, r)
        phase_route(nc, d, r)
        phase_experts(nc, d, r)


_SHORT = {
    "L0_attn_X": "X", "L0_attn_Wq": "Wq", "L0_attn_Wk": "Wk", "L0_attn_Wv": "Wv", "L0_attn_Wo": "Wo",
    "L0_ffn_W": "W", "L0_ffn_bias": "bias", "L0_ffn_A": "A", "L0_ffn_Bf": "Bf", "L0_ffn_coeffs": "coeffs",
    "L0_ffn_scales": "scales", "L1_attn_bv_q": "bvq", "L1_attn_bv_k": "bvk", "L1_attn_bv_v": "bvv",
    "L1_ffn_router_w": "router_w", "L1_ffn_router_b": "router_b", "L1_ffn_router_bias": "router_bias",
    "L1_ffn_ew1": "ew1", "L1_ffn_eb1": "eb1", "L1_ffn_ew2": "ew2", "L1_ffn_eb2": "eb2", "L1_ffn_ew3": "ew3",
    "L1_ffn_eb3": "eb3", "L1_ffn_sw1": "sw1", "L1_ffn_sb1": "sb1", "L1_ffn_sw2": "sw2", "L1_ffn_sb2": "sb2",
    "L1_ffn_sw3": "sw3", "L1_ffn_sb3": "sb3",
}
_OUT = ((B, T, D), "float32")


def shape_constants():
    half = np.float32(HALF)
    inv = (np.float32(1.0) / np.float32(10000.0) ** (np.arange(HALF, dtype=np.float32) / half)).astype(np.float32)
    ang = np.arange(T, dtype=np.float32)[:, None] * inv[None, :]
    wide = lambda a: np.ascontiguousarray(
        np.tile(np.concatenate([a, a], 1).reshape(TB, P, DH).transpose(1, 0, 2), (1, B, 1)).astype(np.float32))
    i = np.arange(P)
    return {
        "ident": np.eye(P, dtype=np.float32),
        "mask": np.where(i[None, :] > i[:, None], np.float32(MASKED), np.float32(0)).astype(np.float32),
        "cos": wide(np.cos(ang)), "sin": wide(np.sin(ang)),
    }


def kernel(**inputs):
    import concourse.bacc as _bacc
    from concourse.bass_utils import run_bass_kernel_spmd as _run

    nc = _bacc.Bacc("TRN2", target_bir_lowering=False, num_devices=1)
    given = {short: np.ascontiguousarray(inputs[name]) for name, short in _SHORT.items()}
    given.update(shape_constants())
    arrays = {f"in_{short}_dram": a for short, a in given.items()}
    d = {
        short: nc.dram_tensor(f"in_{short}_dram", a.shape, mybir.dt.from_np(a.dtype), kind="ExternalInput").ap()
        for short, a in given.items()}
    d["out"] = nc.dram_tensor("out_0_dram", _OUT[0], F32, kind="ExternalOutput").ap()
    program(nc, d)
    r = _run(nc, [arrays], core_ids=[0])
    return r.results[0]["out_0_dram"]
```

```python
from contextlib import ExitStack

import numpy as np
import concourse.bass as bass
from concourse import mybir

F32 = mybir.dt.float32
F32R = mybir.dt.float32r
ALU = mybir.AluOpType
ACT = mybir.ActivationFunctionType
AX = mybir.AxisListType

P = 128
B, T, D = 2, 1024, 512
NB = B * T // P
TB = T // P
KT = D // P
H, HKV, DH = 32, 8, 16
G = H // HKV
HALF = DH // 2
QK = D + HKV * DH
QT = QK // P
LR = 256
BH, BD = 4, 128
E, INTER = 16, 128
EG = 4
SH = 2
TL = 256
TILES = (2 * B * T + E * (TL - 1)) // TL
MOST = B * T // TL
COLS = TILES * TL // P
EPS = 1e-5
MASKED = -float(2 ** 100)
CH = 512
NCH = B * T // CH
STACK = 4 * DH
SHIFT_ROW = 96
ROWS = SHIFT_ROW + 2


class Buffers:
    pass


def f32(ap):
    return ap.bitcast(F32)


def semaphores(nc, ctx, phase, names):
    return {name: ctx.enter_context(nc.semaphore(f"{phase}_{name}")) for name in names.split()}


def retire(nc, s):
    with nc.Block() as block:
        @block.sync
        def _(sp):
            for name in s:
                sp.sem_clear(s[name])


def blocks(eng, total, step, first=3, last=3, period=2):
    n = 0
    while n < first:
        step(n, n // period, n % period)
        n += 1
    turns = (total - last - first) // period
    if turns > 0:
        with eng.Fori(0, turns) as i:
            for m in range(n, n + period):
                step(i * period + m, i + m // period, m % period)
        n += turns * period
    while n < total:
        step(n, n // period, n % period)
        n += 1


def phase_weights(nc, d, r, w):
    with ExitStack() as ctx:
        sb = lambda n, s, t=F32: ctx.enter_context(nc.sbuf_tensor(n, s, t))
        wqkv = sb("wqkv_raw", [P, KT, QK + HKV * DH])
        wo = sb("wo_raw", [P, KT, D])
        wl = sb("wl_raw", [P, KT, D])
        am = sb("a_raw", [P, 2, D])
        bf = sb("bf_raw", [P, KT, LR])
        bw = sb("bw", [P, KT, LR])
        bwT = sb("bwT", [P, 2, D])
        co = sb("coeffs_all", [P, E])
        sc = sb("scales_all", [P, E])
        we = sb("we", [P, E])
        turned = [ctx.enter_context(nc.psum_tensor(f"bw_turned{i}", [P, D], F32)) for i in range(2)]
        folded = [ctx.enter_context(nc.psum_tensor(f"w_folded{i}", [P, D], F32)) for i in range(KT)]
        s = semaphores(nc, ctx, "w", "x_in qkv_in wo_in low_in wl_in const_in kscaled qkv_done hi_done "
                 "we_done bw_done turned_done bwT_done folded_done folded_hi all_done idr ones")
        block = ctx.enter_context(nc.Block())

        @block.sync
        def _(sp):
            for k in range(KT):
                sp.dma_start(bf[:, k].rearrange("p (e r) -> p e r", e=E),
                             d["Bf"][:, k * P:(k + 1) * P].rearrange("e p r -> p e r")).then_inc(s["low_in"], 16)
            sp.dma_start(co[:], d["coeffs"].rearrange("(a e) -> a e", a=1).broadcast_to([P, E])).then_inc(s["low_in"], 16)
            sp.dma_start(sc[:], d["scales"].rearrange("(a e) -> a e", a=1).broadcast_to([P, E])).then_inc(s["low_in"], 16)
            sp.dma_start(am[:], d["A"].rearrange("e r d -> (e r) d").rearrange("(h p) d -> p h d", p=P)).then_inc(s["low_in"], 16)
            sp.dma_start(wl[:], d["W"].rearrange("(k p) d -> p k d", p=P)).then_inc(s["wl_in"], 16)
            for n in range(0, NB, 4):
                sp.dma_start(r.Y[:, n:n + 4], d["X"].rearrange("b t d -> (b t) d").rearrange(
                    "(n p) d -> p n d", p=P)[:, n:n + 4]).then_inc(s["x_in"], 16)
            sp.wait_ge(s["x_in"], 16 * NB // 4)

        @block.scalar
        def _(act):
            act.dma_start(r.ident[:], d["ident"]).then_inc(s["const_in"], 16)
            act.dma_start(r.mask[:], d["mask"]).then_inc(s["const_in"], 16)
            act.dma_start(r.cos[:], d["cos"]).then_inc(s["const_in"], 16)
            act.dma_start(r.sin[:], d["sin"]).then_inc(s["const_in"], 16)
            act.dma_start(r.bias[:], d["bias"].rearrange("(a e) -> a e", a=1).broadcast_to([P, D])).then_inc(s["const_in"], 16)
            act.dma_start(wqkv[:, :, 0:D], d["Wq"].rearrange("(k p) n -> p k n", p=P)).then_inc(s["qkv_in"], 16)
            act.dma_start(wqkv[:, :, D:QK], d["Wk"].rearrange("(k p) n -> p k n", p=P)).then_inc(s["qkv_in"], 16)
            act.dma_start(wqkv[:, :, QK:], d["Wv"].rearrange("(k p) n -> p k n", p=P)).then_inc(s["qkv_in"], 16)
            act.dma_start(wo[:], d["Wo"].rearrange("(k p) n -> p k n", p=P)).then_inc(s["wo_in"], 16)
            act.wait_ge(s["kscaled"], 1)
            nc.scalar.copy(w.qkv_h[:], wqkv[:]).then_inc(s["hi_done"], 1)
            act.wait_ge(s["wo_in"], 16)
            nc.scalar.copy(w.o_h[:], wo[:]).then_inc(s["hi_done"], 1)
            for k in range(KT):
                act.wait_ge(s["folded_done"], k + 1)
                nc.scalar.copy(w.l_h[:, k], folded[k][:]).then_inc(s["folded_hi"], 1)

        @block.gpsimd
        def _(pool):
            nc.gpsimd.memset(r.V[:], 1.0).then_inc(s["ones"], 1)
            pool.wait_ge(s["qkv_in"], 48)
            nc.gpsimd.tensor_scalar(wqkv[:, :, D:QK], wqkv[:, :, D:QK], DH ** -0.5, None, ALU.mult).then_inc(s["kscaled"], 1)
            pool.wait_ge(s["hi_done"], 1)
            nc.gpsimd.tensor_tensor(w.qkv_l[:], wqkv[:], f32(w.qkv_h[:]), ALU.subtract).then_inc(s["all_done"], 1)
            pool.wait_ge(s["hi_done"], 2)
            nc.gpsimd.tensor_tensor(w.o_l[:], wo[:], f32(w.o_h[:]), ALU.subtract).then_inc(s["all_done"], 1)

        @block.vector
        def _(dve):
            nc.vector.memset(r.eps[:], EPS).then_inc(s["ones"], 1)
            dve.wait_ge(s["low_in"], 16 * (KT + 3))
            nc.vector.tensor_tensor(we[:], co[:], sc[:], ALU.mult).then_inc(s["we_done"], 1)
            dve.wait_ge(s["we_done"], 1)
            for k in range(KT):
                nc.vector.tensor_tensor(bw[:, k].rearrange("p (e r) -> p e r", e=E),
                                        bf[:, k].rearrange("p (e r) -> p e r", e=E),
                                        we[:].rearrange("p (e a) -> p e a", a=1).broadcast_to([P, E, LR // E]),
                                        ALU.mult).then_inc(s["bw_done"], 1)
            dve.wait_ge(s["const_in"], 80)
            nc.vector.tensor_copy(r.ident_r[:], r.ident[:]).then_inc(s["idr"], 1)
            nc.vector.tensor_copy(r.mask_r[:], r.mask[:].rearrange("p (a s) -> p a s", a=1).broadcast_to([P, G, P])).then_inc(s["idr"], 1)
            for h in range(2):
                dve.wait_ge(s["turned_done"], h + 1)
                nc.vector.tensor_copy(bwT[:, h], turned[h][:]).then_inc(s["bwT_done"], 1)
            for k in range(KT):
                dve.wait_ge(s["folded_hi"], k + 1)
                nc.vector.tensor_tensor(w.l_l[:, k], folded[k][:], f32(w.l_h[:, k]), ALU.subtract).then_inc(s["all_done"], 1)

        @block.tensor
        def _(pe):
            pe.wait_ge(s["bw_done"], KT)
            pe.wait_ge(s["const_in"], 80)
            for h in range(2):
                for k in range(KT):
                    last = nc.tensor.transpose(turned[h][:, k * P:(k + 1) * P], bw[:, k, h * P:(h + 1) * P], r.ident[:])
                last.then_inc(s["turned_done"], 1)
            pe.wait_ge(s["bwT_done"], 2)
            pe.wait_ge(s["wl_in"], 16)
            for k in range(KT):
                for h in range(2):
                    nc.tensor.matmul(folded[k][:], am[:, h, k * P:(k + 1) * P], bwT[:, h], start=(h == 0), stop=False,
                                     skip_group_check=True)
                for o in range(KT):
                    last = nc.tensor.matmul(folded[k][:, o * P:(o + 1) * P], wl[:, o, k * P:(k + 1) * P], r.ident[:],
                                            start=False, stop=(o == KT - 1), skip_group_check=True)
                last.then_inc(s["folded_done"], 1)
    return s


def split_matmuls(nc, out, lhs, rhs, k):
    (lh, ll), (rh, rl) = lhs, rhs
    nc.tensor.matmul(out, lh, rh, start=(k == 0), stop=False)
    nc.tensor.matmul(out, lh, rl, start=False, stop=False)
    return nc.tensor.matmul(out, ll, rh, start=False, stop=(k == KT - 1))


def phase_project(nc, d, r, w):
    with ExitStack() as ctx:
        sb = lambda n, s, t=F32: ctx.enter_context(nc.sbuf_tensor(n, s, t))
        stats = sb("stats", [P, 2, 6])
        moments = sb("moments", [P, 2, 2])
        std = sb("std", [P, 2])
        rstd = sb("rstd", [P, 2])
        xn = sb("xn", [P, 2, D])
        xT_h = [sb(f"xT_h{i}", [P, KT, P], F32R) for i in range(2)]
        xT_l = [sb(f"xT_l{i}", [P, KT, P], F32R) for i in range(2)]
        by_cos = sb("by_cos", [P, QK])
        by_sin = sb("by_sin", [P, QK])
        turned = sb("turned", [P, 2, QK])
        qkT_h = sb("qkT_h", [P, 2, QT, P], F32R)
        qkT_l = sb("qkT_l", [P, 2, QT, P], F32R)
        ps = lambda n: ctx.enter_context(nc.psum_tensor(n, [P, D], F32))
        x_turn = [ps("x_turn0"), ps("x_turn1")]
        q_ps, kv_ps, lin_ps, q_turn, k_turn = ps("q_ps"), ps("kv_ps"), ps("lin_ps"), ps("q_turn"), ps("k_turn")
        s = semaphores(nc, ctx, "p", "stats_done moments_done std_done rstd_done xn_ready bias_added x_turned xhi_ready "
                 "xlo_ready q_done kv_done lin_done qmul_done kmul_done v_read lin_added rot_done qk_turned "
                 "qhi_ready qlo_ready stored0 stored1")
        stored = [s["stored0"], s["stored1"]]
        block = ctx.enter_context(nc.Block())

        @block.vector
        def _(dve):
            def statistics(n, par):
                nc.vector.bn_stats(stats[:, par], r.Y[:, n]).then_inc(s["stats_done"], 1)

            def norm(n, par):
                nc.vector.bn_aggr(moments[:, par], stats[:, par]).then_inc(s["moments_done"], 1)
                dve.wait_ge(s["std_done"], n + 1)
                nc.vector.reciprocal(rstd[:, par:par + 1], std[:, par:par + 1]).then_inc(s["rstd_done"], 1)
                dve.wait_ge(s["rstd_done"], n + 1)
                nc.vector.tensor_scalar(xn[:, par], r.Y[:, n], moments[:, par, 0:1], rstd[:, par:par + 1],
                                        ALU.subtract, ALU.mult).then_inc(s["xn_ready"], 1)

            def low_half(n, par):
                dve.wait_ge(s["xhi_ready"], n + 1)
                nc.vector.tensor_tensor(xT_l[par][:], x_turn[par][:].rearrange("p (k t) -> p k t", k=KT),
                                        f32(xT_h[par][:]), ALU.subtract).then_inc(s["xlo_ready"], 1)

            def rope_products(n):
                for ps_, a, b, ready, done in ((q_ps, 0, D, s["q_done"], s["qmul_done"]), (kv_ps, D, QK, s["kv_done"], s["kmul_done"])):
                    dve.wait_ge(ready, n + 1)
                    if a == 0 and not (isinstance(n, int) and n == 0):
                        dve.wait_ge(s["rot_done"], n * 2)
                    heads = (b - a) // DH
                    src = ps_[:, 0:b - a].rearrange("p (h x c) -> p h x c", x=2, c=HALF)
                    for table, out in ((r.cos, by_cos), (r.sin, by_sin)):
                        fac = table[:, n].rearrange("p (a x c) -> p a x c", a=1, x=2).broadcast_to([P, heads, 2, HALF])
                        last = nc.vector.tensor_tensor(
                            out[:, a:b].rearrange("p (h x c) -> p h x c", x=2, c=HALF), src, fac, ALU.mult)
                    last.then_inc(done, 1)

            def add_linear(n):
                dve.wait_ge(s["lin_done"], n + 1)
                dve.wait_ge(s["bias_added"], n + 1)
                nc.vector.tensor_tensor(r.Y[:, n], lin_ps[:], r.Y[:, n], ALU.add).then_inc(s["lin_added"], 1)

            def low_qk(n, par):
                dve.wait_ge(s["qhi_ready"], n + 1)
                nc.vector.tensor_tensor(qkT_l[:, par, 0:KT], q_turn[:].rearrange("p (k t) -> p k t", k=KT),
                                        f32(qkT_h[:, par, 0:KT]), ALU.subtract)
                nc.vector.tensor_tensor(qkT_l[:, par, KT], k_turn[:, 0:P],
                                        f32(qkT_h[:, par, KT]), ALU.subtract).then_inc(s["qlo_ready"], 1)

            for n in range(2):
                statistics(n, n)
                dve.wait_ge(s["stats_done"], n + 1)
                norm(n, n)
            low_half(0, 0)

            def step(n, k, par):
                static = isinstance(n, int)
                if not static or n + 2 < NB:
                    statistics(n + 2, par)
                    dve.wait_ge(s["stats_done"], n + 3)
                if not static or n + 1 < NB:
                    low_half(n + 1, 1 - par)
                if not static or n + 2 < NB:
                    norm(n + 2, par)
                rope_products(n)
                add_linear(n)
                if not static or n >= 1:
                    low_qk(n - 1, 1 - par)
            blocks(dve, NB, step)
            low_qk(NB - 1, 1)

        @block.scalar
        def _(act):
            def root(n, par):
                act.wait_ge(s["moments_done"], n + 1)
                nc.scalar.activation(std[:, par:par + 1], moments[:, par, 1:2], ACT.Sqrt, bias=r.eps[:]).then_inc(s["std_done"], 1)

            def high_half(n, par):
                act.wait_ge(s["x_turned"], n + 1)
                if not (isinstance(n, int) and n < 2):
                    act.wait_ge(s["lin_done"], n - 1)
                nc.scalar.copy(xT_h[par][:], x_turn[par][:].rearrange("p (k t) -> p k t", k=KT)).then_inc(s["xhi_ready"], 1)

            def keep_v(n):
                act.wait_ge(s["kmul_done"], n + 1)
                nc.scalar.copy(r.V[:, n, :, 0:DH], kv_ps[:, P:2 * P].rearrange("p (h c) -> p h c", c=DH)).then_inc(s["v_read"], 1)

            def high_qk(n, k, par):
                act.wait_ge(s["qk_turned"], n + 1)
                if not (isinstance(n, int) and n < 2):
                    act.wait_ge(stored[par], k * 32)
                nc.scalar.copy(qkT_h[:, par, 0:KT], q_turn[:].rearrange("p (k t) -> p k t", k=KT))
                nc.scalar.copy(qkT_h[:, par, KT], k_turn[:, 0:P]).then_inc(s["qhi_ready"], 1)

            root(0, 0)
            root(1, 1)
            high_half(0, 0)

            def step(n, k, par):
                static = isinstance(n, int)
                if not static or n + 1 < NB:
                    high_half(n + 1, 1 - par)
                if not static or n + 2 < NB:
                    root(n + 2, par)
                keep_v(n)
                if not static or n >= 1:
                    high_qk(n - 1, k if par else k - 1, 1 - par)
            blocks(act, NB, step)
            high_qk(NB - 1, (NB - 1) // 2, 1)

        @block.gpsimd
        def _(pool):
            def add_bias(n):
                pool.wait_ge(s["xn_ready"], n + 1)
                nc.gpsimd.tensor_tensor(r.Y[:, n], r.Y[:, n], r.bias[:], ALU.add).then_inc(s["bias_added"], 1)

            def rotate(n, par):
                pool.wait_ge(s["kmul_done"], n + 1)
                if not (isinstance(n, int) and n < 2):
                    pool.wait_ge(s["qk_turned"], n - 1)
                c = by_cos[:].rearrange("p (h x c) -> p h x c", x=2, c=HALF)
                sn = by_sin[:].rearrange("p (h x c) -> p h x c", x=2, c=HALF)
                o = turned[:, par].rearrange("p (h x c) -> p h x c", x=2, c=HALF)
                nc.gpsimd.tensor_tensor(o[:, :, 0], c[:, :, 0], sn[:, :, 1], ALU.subtract).then_inc(s["rot_done"], 1)
                nc.gpsimd.tensor_tensor(o[:, :, 1], c[:, :, 1], sn[:, :, 0], ALU.add).then_inc(s["rot_done"], 1)

            add_bias(0)

            def step(n, k, par):
                if not isinstance(n, int) or n + 1 < NB:
                    add_bias(n + 1)
                rotate(n, par)
            blocks(pool, NB, step)

        @block.tensor
        def _(pe):
            def turn_x(n, par):
                pe.wait_ge(s["xn_ready"], n + 1)
                if not (isinstance(n, int) and n < 2):
                    pe.wait_ge(s["xlo_ready"], n - 1)
                for k in range(KT):
                    last = nc.tensor.transpose(x_turn[par][:, k * P:(k + 1) * P], xn[:, par, k * P:(k + 1) * P], r.ident[:])
                last.then_inc(s["x_turned"], 1)

            def project(n, par):
                first = isinstance(n, int) and n == 0
                pe.wait_ge(s["xlo_ready"], n + 1)
                for out, cols, wh, wlo, free, done in (
                        (q_ps[:], (0, D), w.qkv_h, w.qkv_l, s["qmul_done"], s["q_done"]),
                        (kv_ps[:, 0:2 * P], (D, QK + P), w.qkv_h, w.qkv_l, s["v_read"], s["kv_done"]),
                        (lin_ps[:], (0, D), w.l_h, w.l_l, s["lin_added"], s["lin_done"])):
                    if not first:
                        pe.wait_ge(free, n)
                    for k in range(KT):
                        last = split_matmuls(nc, out, (xT_h[par][:, k], xT_l[par][:, k]),
                                             (wh[:, k, cols[0]:cols[1]], wlo[:, k, cols[0]:cols[1]]), k)
                    last.then_inc(done, 1)

            def turn_qk(n, par):
                pe.wait_ge(s["rot_done"], 2 * n + 2)
                if not (isinstance(n, int) and n == 0):
                    pe.wait_ge(s["qlo_ready"], n)
                for k in range(KT):
                    nc.tensor.transpose(q_turn[:, k * P:(k + 1) * P], turned[:, par, k * P:(k + 1) * P], r.ident[:])
                nc.tensor.transpose(k_turn[:, 0:P], turned[:, par, D:QK], r.ident[:]).then_inc(s["qk_turned"], 1)

            turn_x(0, 0)

            def step(n, k, par):
                static = isinstance(n, int)
                if not static or n + 1 < NB:
                    turn_x(n + 1, 1 - par)
                project(n, par)
                if not static or n >= 1:
                    turn_qk(n - 1, 1 - par)
            blocks(pe, NB, step)
            turn_qk(NB - 1, 1)

        @block.sync
        def _(sp):
            def step(n, k, par):
                sp.wait_ge(s["qlo_ready"], n + 1)
                for half, src in enumerate((qkT_h, qkT_l)):
                    sp.dma_start(r.qk_dram[half].rearrange("(q p) t -> p q t", p=P)[:, :, bass.ds(n * P, P)],
                                 f32(src[:, par])).then_inc(stored[par], 16)
            blocks(sp, NB, step)
            for par in range(2):
                sp.wait_ge(stored[par], 32 * NB // 2)
    return s


def units():
    return [(tc, sb) for tc in range(T // CH) for sb in range((tc + 1) * CH // P)]


def max_units():
    out = []
    for tb in range(TB):
        for sc in range(tb * P // CH + 1):
            w = min((tb + 1) * P - sc * CH, CH)
            heads = 4 if w <= CH // 4 else 2 if w <= CH // 2 else 1
            out += [(tb, sc, h, heads, w) for h in range(0, G, heads)]
    return sorted(out, key=lambda m: m[0] >= CH // P)


def phase_attention(nc, d, r):
    U, M = units(), max_units()
    NU, NM = len(U), len(M)
    NG = B * HKV
    NBUF = 3
    TAIL = 2
    columns = [2 * CH - max(0, sb * P - tc * CH) for tc, sb in U]
    share = lambda u: round(NM * sum(columns[:u]) / sum(columns))
    HEAD = NM - share(TAIL)
    LAG = 2
    DIAG = [u for u, (tc, sb) in enumerate(U) if sb * P >= tc * CH]
    ND = len(DIAG)
    M_LATE = [m[0] for m in M].index(CH // P)
    LAST0 = CH // P - 1
    COPY_O0 = LAST0 + LAG + 1
    TURN_O0 = COPY_O0 + 1
    COPY_O1 = LAG
    TURN_O1 = COPY_O1 + 1
    TURN_SHIFT = TURN_O1 + 1
    with ExitStack() as ctx:
        sb_ = lambda n, s, t=F32: ctx.enter_context(nc.sbuf_tensor(n, s, t))
        qs = [sb_(f"q_stack{i}", [ROWS, G, T], F32R) for i in range(NBUF)]
        ks = [sb_(f"k_stack{i}", [ROWS, T], F32R) for i in range(NBUF)]
        v = [sb_(f"v_cur{i}", [P, TB, 2 * DH]) for i in range(NBUF)]
        probs = [sb_(f"probs{i}", [P, G, CH]) for i in range(3)]
        negmax = sb_("negmax", [P, 2, G, TB])
        shift = sb_("shift", [P, G * TB])
        shiftT_h = sb_("shiftT_h", [G * TB, P], F32R)
        shiftT_l = sb_("shiftT_l", [G * TB, P], F32R)
        o_sb = sb_("o_sb", [P, 2, CH])
        rden = sb_("rden", [P, CH // P, G])
        s_ps = [ctx.enter_context(nc.psum_tensor(f"s_ps{i}", [P, 2, CH], F32)) for i in range(2)]
        m_ps = [ctx.enter_context(nc.psum_tensor(f"m_ps{i}", [P, CH], F32)) for i in range(2)]
        o_ps = ctx.enter_context(nc.psum_tensor("o_ps", [P, CH], F32))
        t_ps = ctx.enter_context(nc.psum_tensor("t_ps", [P, CH], F32))
        s = semaphores(nc, ctx, "a", "pad_done q0_in0 q0_in1 q0_in2 q1_in0 q1_in1 q1_in2 k_in0 k_in1 k_in2 v_ready m_scored m_read combined "
                 "turned turned_read shift_hi shift_ready shift_in0 shift_in1 shift_in2 scored exped masked pv_done o_read "
                 "rden_done mask_go")
        q0_in, q1_in, k_in = [s["q0_in0"], s["q0_in1"], s["q0_in2"]], [s["q1_in0"], s["q1_in1"], s["q1_in2"]], [s["k_in0"], s["k_in1"], s["k_in2"]]
        shift_in = [s["shift_in0"], s["shift_in1"], s["shift_in2"]]
        block = ctx.enter_context(nc.Block())
        NPAD = 3 * NBUF

        def width(u):
            tc, sb = U[u]
            off = max(0, sb * P - tc * CH)
            return tc, sb, off

        @block.sync
        def _(sp):
            def place(g):
                return (g // HKV, g % HKV)

            def load_q(g, k, par, tc):
                b, kv = place(g)
                for j, half in enumerate((0, 0, 1, 1)):
                    sp.dma_start(f32(qs[par][DH * j:DH * j + DH, :, tc * CH:(tc + 1) * CH]),
                                 r.qk_dram[half, bass.ds(kv * (G * DH), G * DH), bass.ds(b * T + tc * CH, CH)].rearrange(
                                     "(h c) t -> c h t", c=DH)).then_inc((q0_in, q1_in)[tc][par], 16)

            def load_k(g, k, par):
                b, kv = place(g)
                for j, half in enumerate((0, 1, 0, 1)):
                    sp.dma_start(f32(ks[par][DH * j:DH * j + DH, :]),
                                 r.qk_dram[half, bass.ds(D + kv * DH, DH), bass.ds(b * T, T)]).then_inc(k_in[par], 16)

            def send_shift(g, par):
                sp.wait_ge(s["shift_ready"], g + 1)
                for j, src in enumerate((shiftT_h, shiftT_l)):
                    sp.dma_start(f32(qs[par][SHIFT_ROW + j:SHIFT_ROW + j + 1]).rearrange("a h (n t) -> a (h n) t", t=P),
                                 f32(src[:])).then_inc(shift_in[par], 16)

            for g in range(NBUF):
                load_k(g, 0, g)
                load_q(g, 0, g, 0)
                load_q(g, 0, g, 1)
            send_shift(0, 0)

            def step(g, k, par):
                static = isinstance(g, int)
                if not static or g + 1 < NG:
                    send_shift(g + 1, (par + 1) % NBUF)
                if not static or g + NBUF < NG:
                    sp.wait_ge(s["scored"], 2 * NU * g + 2 * (LAST0 + 1))
                    load_q(g + NBUF, k, par, 0)
                    sp.wait_ge(s["scored"], 2 * NU * (g + 1))
                    load_k(g + NBUF, k, par)
                    load_q(g + NBUF, k, par, 1)
            blocks(sp, NG, step, 2, 5, NBUF)

        @block.gpsimd
        def _(pool):
            for i in range(NBUF):
                nc.gpsimd.memset(f32(qs[i][64:96]), 0.0).then_inc(s["pad_done"], 1)
                nc.gpsimd.memset(f32(ks[i][64:96]), 0.0).then_inc(s["pad_done"], 1)
                nc.gpsimd.memset(f32(ks[i][SHIFT_ROW:ROWS]), 1.0).then_inc(s["pad_done"], 1)

            def take_v(g, par):
                nc.gpsimd.tensor_copy(v[par][:], r.V[:, bass.ds(g // HKV * TB, TB), g % HKV]).then_inc(s["v_ready"], 1)

            pool.wait_ge(s["pad_done"], NPAD)
            take_v(0, 0)

            def step(g, k, par):
                if not isinstance(g, int) or g + 1 < NG:
                    if not (isinstance(g, int) and g < 2):
                        pool.wait_ge(s["pv_done"], (g - 1) * NU)
                    take_v(g + 1, (par + 1) % NBUF)
                for i, u in enumerate(DIAG):
                    tc, sb, off = width(u)
                    pool.wait_ge(s["exped"], 2 * NU * g + 2 * u + 2)
                    pool.sem_inc(s["mask_go"], 1)
                    blk = probs[u % 3][:, :, off:off + P]
                    nc.gpsimd.affine_select(out=blk, in_=blk, compare_op=ALU.is_ge, fill=0.0, base=0,
                                            pattern=[[0, G], [1, P]], channel_multiplier=-1).then_inc(s["masked"], 1)
            blocks(pool, NG, step, 2, 2, NBUF)

        @block.scalar
        def _(act):
            def copy_o(g, tc):
                act.wait_ge(s["pv_done"], NU * g + (LAST0 + 1 if tc == 0 else NU))
                if not (isinstance(g, int) and g == 0):
                    act.wait_ge(s["turned"], 3 * g + tc)
                nc.scalar.copy(o_sb[:, tc], o_ps[:]).then_inc(s["o_read"], 1)

            def step(g, k, par):
                for u in range(NU):
                    tc, sb, off = width(u)
                    if u == COPY_O1 and not (isinstance(g, int) and g == 0):
                        copy_o(g - 1, 1)
                    if u == COPY_O0:
                        copy_o(g, 0)
                    if not (isinstance(g, int) and g == 0 and u < 3):
                        act.wait_ge(s["pv_done"], NU * g + u - 2)
                    for hp in range(2):
                        act.wait_ge(s["scored"], 2 * NU * g + 2 * u + hp + 1)
                        nc.scalar.activation(probs[u % 3][:, 2 * hp:2 * hp + 2, off:], s_ps[hp][:, :, off:],
                                             ACT.Exp).then_inc(s["exped"], 1)
            blocks(act, NG, step, 2, 2, NBUF)
            copy_o(NG - 1, 1)

        def maxima_beside(g, u):
            if u < TAIL:
                later, first, last = 1, share(u) + HEAD, share(u + 1) + HEAD
            else:
                later, first, last = 2, share(u) - share(TAIL), share(u + 1) - share(TAIL)
            if isinstance(g, int) and g + later >= NG:
                return []
            return [(g + later, later, m) for m in range(first, last)]

        @block.vector
        def _(dve):
            def max_unit(g, m):
                tb, sc, h, heads, w = M[m]
                dve.wait_ge(s["m_scored"], NM * g + m + 1)
                nc.vector.tensor_reduce(negmax[:, sc, h:h + heads, tb],
                                        m_ps[m % 2][:, 0:heads * w].rearrange("p (h s) -> p h s", h=heads), AX.X,
                                        ALU.max, negate=True).then_inc(s["m_read"], 1)

            def combine(g):
                dve.wait_ge(s["m_read"], NM * (g + 1))
                out = shift[:].rearrange("p (h n) -> p h n", n=TB)
                nc.vector.tensor_tensor(out[:, :, CH // P:], negmax[:, 0, :, CH // P:], negmax[:, 1, :, CH // P:], ALU.min)
                nc.vector.tensor_copy(out[:, :, 0:CH // P], negmax[:, 0, :, 0:CH // P]).then_inc(s["combined"], 1)

            def take_shift(g, use, sent, before):
                dve.wait_ge(s["turned"], use + 1)
                if not (isinstance(g, int) and g == 0):
                    dve.wait_ge(shift_in[before], 32 * sent)
                nc.vector.tensor_copy(shiftT_h[:], t_ps[0:G * TB, 0:P]).then_inc(s["shift_hi"], 1)
                dve.wait_ge(s["shift_hi"], g + 1)
                nc.vector.tensor_tensor(shiftT_l[:], t_ps[0:G * TB, 0:P], f32(shiftT_h[:]), ALU.subtract).then_inc(s["shift_ready"], 1)
                dve.wait_ge(s["shift_ready"], g + 1)
                dve.sem_inc(s["turned_read"], 1)

            def normalise(g, tc, use, count):
                dve.wait_ge(s["turned"], use + 1)
                o = t_ps[:].rearrange("p (n h c) -> p n h c", h=G, c=2 * DH)
                nc.vector.reciprocal(rden[:], o[:, :, :, DH]).then_inc(s["rden_done"], 1)
                dve.wait_ge(s["rden_done"], count + 1)
                nc.vector.tensor_tensor(
                    r.AN[:, bass.ds(g // HKV * TB + tc * (CH // P), CH // P), bass.ds(g % HKV * (G * DH), G * DH)].rearrange(
                        "p n (h c) -> p n h c", c=DH),
                    o[:, :, :, 0:DH], rden[:].rearrange("p n (h a) -> p n h a", a=1).broadcast_to([P, CH // P, G, DH]),
                    ALU.mult).then_inc(s["turned_read"], 1)

            for m in range(NM):
                max_unit(0, m)
            combine(0)
            dve.wait_ge(s["combined"], 1)
            for m in range(HEAD // 2):
                max_unit(1, m)
            take_shift(0, 0, 0, 0)
            for m in range(HEAD // 2, HEAD):
                max_unit(1, m)

            def step(g, k, par):
                static = isinstance(g, int)
                more = not static or g + 1 < NG
                for u in range(NU):
                    if more and u == TAIL:
                        combine(g + 1)
                        dve.wait_ge(s["combined"], g + 2)
                    for gm, later, m in maxima_beside(g, u):
                        max_unit(gm, m)
                    if u == TURN_O1 and not (static and g == 0):
                        normalise(g - 1, 1, 3 * g, 2 * g - 1)
                    if more and u == TURN_SHIFT:
                        take_shift(g + 1, 3 * g + 1, k + 1, par)
                    if u == TURN_O0:
                        normalise(g, 0, 3 * g + 2 if more else 3 * g + 1, 2 * g)
            blocks(dve, NG, step, 2, 2, NBUF)
            normalise(NG - 1, 1, 3 * NG - 1, 2 * NG - 1)

        @block.tensor
        def _(pe):
            def max_scores(g, k, par, m):
                tb, sc, h, heads, w = M[m]
                if m == 0:
                    pe.wait_ge(k_in[par], 64 * (k + 1))
                    pe.wait_ge(q0_in[par], 64 * (k + 1))
                if m == M_LATE:
                    pe.wait_ge(q1_in[par], 64 * (k + 1))
                if not (isinstance(g, int) and g == 0 and m < 2):
                    pe.wait_ge(s["m_read"], NM * g + m - 1)
                diag = tb * P - sc * CH
                bank = m_ps[m % 2]
                for j in range(heads):
                    last = nc.tensor.matmul(bank[:, j * w:(j + 1) * w], qs[par][0:SHIFT_ROW, h + j, tb * P:(tb + 1) * P],
                                            ks[par][0:SHIFT_ROW, sc * CH:sc * CH + w], start=(j == 0),
                                            stop=(diag >= CH and j == heads - 1), skip_group_check=True)
                if diag < CH:
                    last = nc.tensor.matmul(bank[:, 0:heads * w].rearrange("p (h s) -> p h s", h=heads)[:, :, diag:diag + P],
                                            r.ident_r[:], r.mask_r[:, 0:heads], start=False, stop=True,
                                            skip_group_check=True)
                last.then_inc(s["m_scored"], 1)

            def scores(g, u, hp, par):
                tc, sb, off = width(u)
                if not (isinstance(g, int) and g == 0 and u == 0):
                    pe.wait_ge(s["exped"], 2 * NU * g + 2 * u + hp - 1)
                for j in range(2):
                    h = 2 * hp + j
                    last = nc.tensor.matmul(s_ps[hp][:, j, off:], ks[par][:, sb * P:(sb + 1) * P],
                                            qs[par][:, h, tc * CH + off:(tc + 1) * CH], start=True, stop=True)
                last.then_inc(s["scored"], 1)

            def pv(g, u, par):
                tc, sb, off = width(u)
                pe.wait_ge(s["exped"], 2 * NU * g + 2 * u + 2)
                if u in DIAG:
                    pe.wait_ge(s["masked"], ND * g + DIAG.index(u) + 1)
                if u == 0:
                    pe.wait_ge(s["v_ready"], g + 1)
                if sb == 0 and not (isinstance(g, int) and g == 0 and tc == 0):
                    pe.wait_ge(s["o_read"], 2 * g + tc)
                for h in range(G):
                    last = nc.tensor.matmul(o_ps[2 * DH * h:2 * DH * (h + 1), off:], v[par][:, sb, :],
                                            probs[u % 3][:, h, off:], start=(sb == 0),
                                            stop=(sb == (tc + 1) * CH // P - 1), skip_group_check=True)
                last.then_inc(s["pv_done"], 1)

            def turn_o(g, tc, use):
                pe.wait_ge(s["o_read"], 2 * g + tc + 1)
                pe.wait_ge(s["turned_read"], use)
                for j in range(CH // P):
                    last = nc.tensor.transpose(t_ps[:, j * P:(j + 1) * P], o_sb[:, tc, j * P:(j + 1) * P], r.ident[:])
                last.then_inc(s["turned"], 1)

            def turn_shift(g, use):
                pe.wait_ge(s["combined"], g + 1)
                if not (isinstance(g, int) and g == 0):
                    pe.wait_ge(s["turned_read"], use)
                nc.tensor.transpose(t_ps[0:G * TB, 0:P], shift[:], r.ident[:]).then_inc(s["turned"], 1)

            pe.wait_ge(s["pad_done"], NPAD)
            for m in range(NM):
                max_scores(0, 0, 0, m)
            for m in range(HEAD // 2):
                max_scores(1, 0, 1, m)
            turn_shift(0, 0)
            for m in range(HEAD // 2, HEAD):
                max_scores(1, 0, 1, m)

            def step(g, k, par):
                static = isinstance(g, int)
                more = not static or g + 1 < NG
                pe.wait_ge(shift_in[par], 32 * (k + 1))
                for u in range(NU):
                    beside = [(gm, k + (par + later) // NBUF, (par + later) % NBUF, m)
                              for gm, later, m in maxima_beside(g, u)]
                    for unit in beside[0:1]:
                        max_scores(*unit)
                    scores(g, u, 0, par)
                    for unit in beside[1:2]:
                        max_scores(*unit)
                    if u == TURN_O1 and not (static and g == 0):
                        turn_o(g - 1, 1, 3 * g)
                    if more and u == TURN_SHIFT:
                        turn_shift(g + 1, 3 * g + 1)
                    if u == TURN_O0:
                        turn_o(g, 0, 3 * g + 2 if more else 3 * g + 1)
                    if u >= LAG:
                        pv(g, u - LAG, par)
                    elif not (static and g == 0):
                        pv(g - 1, NU + u - LAG, (par - 1) % NBUF)
                    for unit in beside[2:]:
                        max_scores(*unit)
                    scores(g, u, 1, par)
            blocks(pe, NG, step, 2, 2, NBUF)
            for u in range(NU - LAG, NU):
                pv(NG - 1, u, (NG - 1) % NBUF)
            turn_o(NG - 1, 1, 3 * NG - 1)


def phase_mix(nc, d, r, w):
    with ExitStack() as ctx:
        sb = lambda n, s, t=F32: ctx.enter_context(nc.sbuf_tensor(n, s, t))
        an = sb("an", [P, 2, D])
        aT_h = [sb(f"aT_h{i}", [P, KT, P], F32R) for i in range(2)]
        aT_l = [sb(f"aT_l{i}", [P, KT, P], F32R) for i in range(2)]
        stats = sb("stats1", [P, 2, 6])
        moments = sb("moments1", [P, 2, 2])
        std = sb("std1", [P, 2])
        rstd = sb("rstd1", [P, 2])
        xn = sb("xn1", [P, 2, D])
        xT = [sb(f"xT_full{i}", [P, KT, P]) for i in range(2)]
        router_w = sb("router_w", [P, KT, E])
        router_b = sb("router_b", [P, E])
        ps = lambda n: ctx.enter_context(nc.psum_tensor(n, [P, D], F32))
        a_turn = [ps("a_turn0"), ps("a_turn1")]
        o_ps = [ps("mix_ps0"), ps("mix_ps1")]
        x_turn = [ps("x1_turn0"), ps("x1_turn1")]
        l_ps = ps("logits_ps")
        s = semaphores(nc, ctx, "m", "router_in an_ready a_turned ahi_ready alo_ready mixed added stats_done moments_done "
                 "std_done rstd_done xn_ready xn_kept x_turned xhi_ready xlo_ready logits_done logits_read copy_go stats_go")
        block = ctx.enter_context(nc.Block())
        tiles = lambda ap: ap.rearrange("p (k t) -> p k t", k=KT)

        @block.sync
        def _(sp):
            sp.dma_start(router_w[:], d["router_w"].rearrange("(k p) e -> p k e", p=P)).then_inc(s["router_in"], 16)
            sp.dma_start(router_b[:], d["router_b"].rearrange("(a e) -> a e", a=1).broadcast_to([P, E])).then_inc(s["router_in"], 16)
            sp.wait_ge(s["router_in"], 32)

        @block.gpsimd
        def _(pool):
            def stage(n, par):
                if not (isinstance(n, int) and n < 2):
                    pool.wait_ge(s["a_turned"], n - 1)
                    pool.sem_inc(s["copy_go"], 1)
                nc.gpsimd.tensor_copy(an[:, par], r.AN[:, n]).then_inc(s["an_ready"], 1)

            def keep(n, par):
                pool.wait_ge(s["xn_ready"], n + 1)
                pool.sem_inc(s["copy_go"], 1)
                nc.gpsimd.tensor_copy(r.AN[:, n], xn[:, par]).then_inc(s["xn_kept"], 1)

            stage(0, 0)
            stage(1, 1)

            def step(n, k, par):
                if not isinstance(n, int) or n + 2 < NB:
                    stage(n + 2, par)
                keep(n, par)
            blocks(pool, NB, step)

        @block.scalar
        def _(act):
            def high_a(n, par):
                act.wait_ge(s["a_turned"], n + 1)
                if not (isinstance(n, int) and n < 2):
                    act.wait_ge(s["mixed"], n - 1)
                nc.scalar.copy(aT_h[par][:], tiles(a_turn[par][:])).then_inc(s["ahi_ready"], 1)

            def root(n, par):
                act.wait_ge(s["moments_done"], n + 1)
                nc.scalar.activation(std[:, par:par + 1], moments[:, par, 1:2], ACT.Sqrt, bias=r.eps[:]).then_inc(s["std_done"], 1)

            def high_x(n, par):
                act.wait_ge(s["x_turned"], n + 1)
                if not (isinstance(n, int) and n < 2):
                    act.wait_ge(s["logits_done"], n - 1)
                nc.scalar.copy(xT[par][:], tiles(x_turn[par][:])).then_inc(s["xhi_ready"], 1)
                nc.scalar.copy(r.XH[:, :, bass.ds(n * P, P)], tiles(x_turn[par][:])).then_inc(s["xhi_ready"], 1)

            high_a(0, 0)

            def step(n, k, par):
                static = isinstance(n, int)
                if not static or n + 1 < NB:
                    high_a(n + 1, 1 - par)
                if not static or n >= 1:
                    high_x(n - 1, 1 - par)
                root(n, par)
            blocks(act, NB, step)
            high_x(NB - 1, 1)

        @block.vector
        def _(dve):
            def low_a(n, par):
                dve.wait_ge(s["ahi_ready"], n + 1)
                nc.vector.tensor_tensor(aT_l[par][:], tiles(a_turn[par][:]), f32(aT_h[par][:]), ALU.subtract).then_inc(s["alo_ready"], 1)

            def add(n, par):
                dve.wait_ge(s["mixed"], n + 1)
                nc.vector.tensor_tensor(r.Y[:, n], o_ps[par][:], r.Y[:, n], ALU.add).then_inc(s["added"], 1)
                dve.wait_ge(s["added"], n + 1)
                dve.sem_inc(s["stats_go"], 1)
                nc.vector.bn_stats(stats[:, par], r.Y[:, n]).then_inc(s["stats_done"], 1)

            def low_x(n, par):
                dve.wait_ge(s["xhi_ready"], 2 * n + 2)
                nc.vector.tensor_tensor(r.XL[:, :, bass.ds(n * P, P)], tiles(x_turn[par][:]), f32(r.XH[:, :, bass.ds(n * P, P)]), ALU.subtract).then_inc(s["xlo_ready"], 1)

            def norm(n, par):
                nc.vector.bn_aggr(moments[:, par], stats[:, par]).then_inc(s["moments_done"], 1)
                dve.wait_ge(s["std_done"], n + 1)
                nc.vector.reciprocal(rstd[:, par:par + 1], std[:, par:par + 1]).then_inc(s["rstd_done"], 1)
                dve.wait_ge(s["rstd_done"], n + 1)
                if not (isinstance(n, int) and n < 2):
                    dve.wait_ge(s["xn_kept"], n - 1)
                nc.vector.tensor_scalar(xn[:, par], r.Y[:, n], moments[:, par, 0:1], rstd[:, par:par + 1],
                                        ALU.subtract, ALU.mult).then_inc(s["xn_ready"], 1)

            def take_logits(n):
                dve.wait_ge(s["logits_done"], n + 1)
                nc.vector.tensor_tensor(r.LG[:, n], l_ps[:, 0:E], router_b[:], ALU.add).then_inc(s["logits_read"], 1)

            dve.wait_ge(s["router_in"], 32)
            low_a(0, 0)

            def step(n, k, par):
                static = isinstance(n, int)
                if not static or n + 1 < NB:
                    low_a(n + 1, 1 - par)
                add(n, par)
                dve.wait_ge(s["stats_done"], n + 1)
                if not static or n >= 1:
                    low_x(n - 1, 1 - par)
                norm(n, par)
                if not static or n >= 2:
                    take_logits(n - 2)
            blocks(dve, NB, step)
            low_x(NB - 1, 1)
            take_logits(NB - 2)
            take_logits(NB - 1)

        @block.tensor
        def _(pe):
            def turn_a(n, par):
                pe.wait_ge(s["an_ready"], n + 1)
                if not (isinstance(n, int) and n < 2):
                    pe.wait_ge(s["alo_ready"], n - 1)
                for k in range(KT):
                    last = nc.tensor.transpose(a_turn[par][:, k * P:(k + 1) * P], an[:, par, k * P:(k + 1) * P], r.ident[:])
                last.then_inc(s["a_turned"], 1)

            def mix(n, par):
                pe.wait_ge(s["alo_ready"], n + 1)
                if not (isinstance(n, int) and n < 2):
                    pe.wait_ge(s["added"], n - 1)
                for k in range(KT):
                    last = split_matmuls(nc, o_ps[par][:], (aT_h[par][:, k], aT_l[par][:, k]), (w.o_h[:, k], w.o_l[:, k]), k)
                last.then_inc(s["mixed"], 1)

            def turn_x(n, par):
                pe.wait_ge(s["xn_ready"], n + 1)
                if not (isinstance(n, int) and n < 2):
                    pe.wait_ge(s["xlo_ready"], n - 1)
                for k in range(KT):
                    last = nc.tensor.transpose(x_turn[par][:, k * P:(k + 1) * P], xn[:, par, k * P:(k + 1) * P], r.ident[:])
                last.then_inc(s["x_turned"], 1)

            def logits(n, par):
                pe.wait_ge(s["xhi_ready"], 2 * n + 1)
                if not (isinstance(n, int) and n < 1):
                    pe.wait_ge(s["logits_read"], n)
                for k in range(KT):
                    last = nc.tensor.matmul(l_ps[:, 0:E], xT[par][:, k], router_w[:, k], start=(k == 0), stop=(k == KT - 1))
                last.then_inc(s["logits_done"], 1)

            pe.wait_ge(s["router_in"], 32)
            turn_a(0, 0)

            def step(n, k, par):
                static = isinstance(n, int)
                if not static or n + 1 < NB:
                    turn_a(n + 1, 1 - par)
                mix(n, par)
                if not static or n >= 2:
                    logits(n - 2, par)
                if not static or n >= 1:
                    turn_x(n - 1, 1 - par)
            blocks(pe, NB, step)
            logits(NB - 2, 0)
            turn_x(NB - 1, 1)
            logits(NB - 1, 1)


def phase_bind(nc, d, r):
    U = units()
    NU = len(U)
    DIAG = [u for u, (tc, sb) in enumerate(U) if sb * P >= tc * CH]
    ND = len(DIAG)
    NG = B * BH
    SCALE = 4.0 * float(np.float32(BD ** -0.5))
    with ExitStack() as ctx:
        sb_ = lambda n, s, t=F32: ctx.enter_context(nc.sbuf_tensor(n, s, t))
        bv = sb_("bv", [P, 3, BH, BD])
        alpha = sb_("alpha", [P, 3, BH])
        sign = sb_("sign", [P, 3, BH, BD])
        bind = sb_("bind", [P, 3, BH, BD])
        cols = sb_("bind_cols", [P, 2, BH])
        xs = [sb_(f"xs{i}", [P, T]) for i in range(2)]
        qT = [sb_(f"qT{i}", [P, T]) for i in range(2)]
        kT = [sb_(f"kT{i}", [P, T]) for i in range(2)]
        vb = [sb_(f"vb{i}", [P, TB, BD]) for i in range(2)]
        gate = [sb_(f"gate{i}", [P, CH]) for i in range(3)]
        s_ps = [ctx.enter_context(nc.psum_tensor(f"bs_ps{i}", [P, CH], F32)) for i in range(3)]
        o_ps = [ctx.enter_context(nc.psum_tensor(f"bo_ps{i}", [P, CH], F32)) for i in range(2)]
        c_ps = [ctx.enter_context(nc.psum_tensor(f"bc_ps{i}", [P, CH], F32)) for i in range(2)]
        s = semaphores(nc, ctx, "b", "bv_in x_stored summed alpha_done sign_done hard_done less_done bound turned cols_done xs_ready "
                 "q_ready k_ready v_ready scored gated masked pv_done added mask_go")
        block = ctx.enter_context(nc.Block())

        def width(u):
            tc, sb = U[u]
            return tc, sb, max(0, sb * P - tc * CH)

        @block.sync
        def _(sp):
            for i, src in enumerate((d["bvq"], d["bvk"], d["bvv"])):
                sp.dma_start(bv[:, i], src.rearrange("(a h) c -> a h c", a=1).broadcast_to([P, BH, BD])).then_inc(s["bv_in"], 16)
            sp.dma_start(r.x_dram.rearrange("(n p) d -> p n d", p=P), r.AN[:]).then_inc(s["x_stored"], 16)
            sp.wait_ge(s["bv_in"], 48)
            sp.wait_ge(s["x_stored"], 16)

        @block.gpsimd
        def _(pool):
            def prepare(g, par, first=False):
                b, h = g // BH, g % BH
                if not first:
                    pool.wait_ge(s["k_ready"], g - 1)
                    pool.wait_ge(s["pv_done"], NU * (g - 1))
                nc.gpsimd.tensor_tensor(xs[par][:], f32(r.XH[:, h, bass.ds(b * T, T)]), f32(r.XL[:, h, bass.ds(b * T, T)]),
                                        ALU.add).then_inc(s["xs_ready"], 1)
                nc.gpsimd.tensor_tensor(vb[par][:], r.AN[:, bass.ds(b * TB, TB), bass.ds(h * BD, BD)],
                                        bind[:, 2, bass.ds(h, 1), :].broadcast_to([P, TB, BD]), ALU.mult).then_inc(s["v_ready"], 1)

            pool.wait_ge(s["bound"], 1)
            prepare(0, 0, True)
            prepare(1, 1, True)

            def step(g, k, par):
                for u in DIAG:
                    tc, sb, off = width(u)
                    pool.wait_ge(s["gated"], NU * g + u + 1)
                    pool.sem_inc(s["mask_go"], 1)
                    blk = gate[u % 3][:, off:off + P]
                    nc.gpsimd.affine_select(out=blk, in_=blk, compare_op=ALU.is_ge, fill=0.0, base=0,
                                            pattern=[[1, P]], channel_multiplier=-1).then_inc(s["masked"], 1)
                if not isinstance(g, int) or g + 2 < NG:
                    prepare(g + 2, par)
            blocks(pool, NG, step, 1, 3)

        @block.scalar
        def _(act):
            def step(g, k, par):
                for u in range(NU):
                    tc, sb, off = width(u)
                    act.wait_ge(s["scored"], NU * g + u + 1)
                    if not (isinstance(g, int) and g == 0 and u < 3):
                        act.wait_ge(s["pv_done"], NU * g + u - 2)
                    nc.scalar.activation(gate[u % 3][:, off:], s_ps[u % 3][:, off:], ACT.Sigmoid, scale=SCALE).then_inc(s["gated"], 1)
            blocks(act, NG, step, 1, 1)

        @block.vector
        def _(dve):
            dve.wait_ge(s["bv_in"], 48)
            nc.vector.tensor_reduce(alpha[:], bv[:], AX.X, ALU.add, apply_absolute_value=True).then_inc(s["summed"], 1)
            nc.vector.tensor_scalar(sign[:], bv[:], 0.0, 2.0, ALU.is_ge, ALU.mult).then_inc(s["sign_done"], 1)
            dve.wait_ge(s["summed"], 1)
            nc.vector.tensor_scalar(alpha[:], alpha[:], 1.0 / BD, None, ALU.mult).then_inc(s["alpha_done"], 1)
            dve.wait_ge(s["sign_done"], 1)
            nc.vector.tensor_scalar(sign[:], sign[:], -1.0, None, ALU.add).then_inc(s["sign_done"], 1)
            dve.wait_ge(s["sign_done"], 2)
            dve.wait_ge(s["alpha_done"], 1)
            nc.vector.tensor_tensor(bind[:], sign[:], alpha[:].rearrange("p i (h a) -> p i h a", a=1).broadcast_to(
                [P, 3, BH, BD]), ALU.mult).then_inc(s["hard_done"], 1)
            dve.wait_ge(s["hard_done"], 1)
            nc.vector.tensor_tensor(sign[:], bind[:], bv[:], ALU.subtract).then_inc(s["less_done"], 1)
            dve.wait_ge(s["less_done"], 1)
            nc.vector.tensor_tensor(bind[:], sign[:], bv[:], ALU.add).then_inc(s["bound"], 1)
            dve.wait_ge(s["turned"], 1)
            for i in range(2):
                last = nc.vector.tensor_copy(cols[:, i], c_ps[i][:].rearrange("p (h c) -> p h c", h=BH)[:, :, 0])
            last.then_inc(s["cols_done"], 1)
            dve.wait_ge(s["cols_done"], 1)

            def make_qk(g, par, first=False):
                h = g % BH
                dve.wait_ge(s["xs_ready"], g + 1)
                if not first:
                    dve.wait_ge(s["scored"], NU * (g - 1))
                nc.vector.tensor_scalar(qT[par][:], xs[par][:], cols[:, 0, bass.ds(h, 1)], None, ALU.mult).then_inc(s["q_ready"], 1)
                nc.vector.tensor_scalar(kT[par][:], xs[par][:], cols[:, 1, bass.ds(h, 1)], None, ALU.mult).then_inc(s["k_ready"], 1)

            make_qk(0, 0, True)
            make_qk(1, 1, True)

            def step(g, k, par):
                b, h = g // BH, g % BH
                for tc in range(2):
                    dve.wait_ge(s["pv_done"], NU * g + (CH // P if tc == 0 else NU))
                    y = r.Y[:, bass.ds(b * TB + tc * (CH // P), CH // P), bass.ds(h * BD, BD)]
                    nc.vector.tensor_tensor(y, o_ps[tc][:].rearrange("p (n c) -> p n c", c=BD), y, ALU.add).then_inc(s["added"], 1)
                if not isinstance(g, int) or g + 2 < NG:
                    make_qk(g + 2, par)
            blocks(dve, NG, step, 1, 3)

        @block.tensor
        def _(pe):
            pe.wait_ge(s["bound"], 1)
            for i in range(2):
                for h in range(BH):
                    last = nc.tensor.transpose(c_ps[i][:, h * BD:(h + 1) * BD], bind[:, i, h], r.ident[:])
            last.then_inc(s["turned"], 1)

            def scores(g, u, par):
                tc, sb, off = width(u)
                if u == 0:
                    pe.wait_ge(s["k_ready"], g + 1)
                if not (isinstance(g, int) and g == 0 and u < 3):
                    pe.wait_ge(s["gated"], NU * g + u - 2)
                nc.tensor.matmul(s_ps[u % 3][:, off:], kT[par][:, sb * P:(sb + 1) * P],
                                 qT[par][:, tc * CH + off:(tc + 1) * CH], start=True, stop=True).then_inc(s["scored"], 1)

            def pv(g, u, par):
                tc, sb, off = width(u)
                pe.wait_ge(s["gated"], NU * g + u + 1)
                if u in DIAG:
                    pe.wait_ge(s["masked"], ND * g + DIAG.index(u) + 1)
                if u == 0:
                    pe.wait_ge(s["v_ready"], g + 1)
                if sb == 0 and not (isinstance(g, int) and g == 0):
                    pe.wait_ge(s["added"], 2 * g - 1 + tc)
                for j in range(off // P, CH // P):
                    last = nc.tensor.matmul(o_ps[tc][:, j * P:(j + 1) * P], gate[u % 3][:, j * P:(j + 1) * P], vb[par][:, sb],
                                            start=(sb == 0 and j == 0), stop=(sb == tc * CH // P + j), skip_group_check=True)
                last.then_inc(s["pv_done"], 1)

            def step(g, k, par):
                for u in range(NU):
                    scores(g, u, par)
                    if u >= 1:
                        pv(g, u - 1, par)
                pv(g, NU - 1, par)
            blocks(pe, NG, step, 1, 1)


def phase_route(nc, d, r):
    BIG = float(2 ** 100)
    with ExitStack() as ctx:
        sb = lambda n, s, t=F32: ctx.enter_context(nc.sbuf_tensor(n, s, t))
        NGR = E // EG
        rb = sb("router_bias", [P, E])
        b3 = sb("b3", [E + 1, D])
        top = sb("top", [P, NB])
        less = sb("less", [P, NB, E])
        before = sb("before", [P, P])
        ones = sb("ones", [P, P])
        steps_i = sb("steps_i", [P, TILES + 1], mybir.dt.int32)
        steps = sb("steps", [P, TILES + 1])
        upto = sb("upto", [P, E, E])
        count = sb("count", [P, E])
        over = sb("over", [P, E, MOST])
        tiles = sb("tiles", [P, E])
        summed = sb("summed", [P, E, E])
        end = sb("end", [P, E])
        begin = sb("begin", [P, E])
        begun = sb("begun", [P, TILES, E])
        of_tile = sb("of_tile", [P, TILES])
        picked = sb("picked", [P, 2, NB, E])
        rank = sb("pair_rank", [P, 2, NB])
        first = sb("pair_first", [P, 2, NB])
        passed = sb("passed", [P, 2 * NB, NB])
        column = sb("column", [P, 2, NB])
        scaled = sb("scaled", [P, 2, NB])
        hots = sb("hots", [P, 2, NB, E])
        ex = sb("ex", [P, NB, E])
        den = sb("den", [P, NB])
        rden = sb("rden1", [P, NB])
        prob = sb("prob", [P, NB, E])
        sc = sb("route_scores", [P, NB, E])
        desc = sb("desc", [P, E])
        desc_i = sb("desc_i", [P, E], mybir.dt.int32)
        gm = sb("gm", [P, NB, EG])
        gate_T = sb("gate_T", [E + 1, NB * P])
        tmp = {k: (sb(f"best_{k}", [P, NB]), sb(f"eq_{k}", [P, NB, E]), sb(f"rank_{k}", [P, NB, E]),
                   sb(f"least_{k}", [P, NB]), sb(f"hot_{k}", [P, NB, E])) for k in ("g0", "g1", "e0", "e1")}
        keep = sb("keep", [P, NB, EG])
        pen = sb("pen", [P, NB, EG])
        masked = sb("masked", [P, NB, E])
        again = sb("again", [P, NB, E])
        chosen = sb("chosen", [P, NB, E])
        t_ps = [ctx.enter_context(nc.psum_tensor(f"gt_ps{i}", [P, CH], F32)) for i in range(NCH)]
        y_ps = [ctx.enter_context(nc.psum_tensor(f"b3_ps{i}", [P, D], F32)) for i in range(2)]
        rank_ps = ctx.enter_context(nc.psum_tensor("rank_ps", [P, CH], F32))
        count_ps = ctx.enter_context(nc.psum_tensor("count_ps", [P, CH], F32))
        gates = sb("gates", [P, NB, E + 1])
        s = semaphores(nc, ctx, "r", "in_done less_done exp_done gates turned copied biased added iota_done ones_done "
                 "chosen_done ranked chain")
        block = ctx.enter_context(nc.Block())
        wide = lambda ap, k: ap.rearrange("p (n a) -> p n a", a=1).broadcast_to([P, NB, k])

        @block.sync
        def _(sp):
            sp.dma_start(rb[:], d["router_bias"].rearrange("(a e) -> a e", a=1).broadcast_to([P, E])).then_inc(s["in_done"], 16)
            sp.dma_start(b3[0:E], d["eb3"]).then_inc(s["in_done"], 16)
            sp.dma_start(b3[E:E + 1], d["sb3"].rearrange("(a e) -> a e", a=1)).then_inc(s["in_done"], 16)
            sp.dma_start(before[:], d["before"]).then_inc(s["in_done"], 16)
            sp.dma_start(upto[:], d["upto"].rearrange("(a e) f -> a e f", a=1).broadcast_to([P, E, E])).then_inc(s["in_done"], 16)
            sp.wait_ge(s["in_done"], 80)

        @block.gpsimd
        def _(pool):
            nc.gpsimd.iota(desc_i[:], pattern=[[-1, E]], base=E, channel_multiplier=0).then_inc(s["iota_done"], 1)
            nc.gpsimd.iota(steps_i[:], pattern=[[1, TILES + 1]], base=0, channel_multiplier=0).then_inc(s["iota_done"], 1)
            nc.gpsimd.iota(r.token[:], pattern=[[P, NB]], base=0, channel_multiplier=1).then_inc(s["iota_done"], 1)
            nc.gpsimd.memset(ones[:], 1.0).then_inc(s["ones_done"], 1)

        @block.scalar
        def _(act):
            act.wait_ge(s["less_done"], 1)
            nc.scalar.activation(ex[:], less[:], ACT.Exp).then_inc(s["exp_done"], 1)

        @block.vector
        def _(dve):
            made = [0]

            def done(ins):
                made[0] += 1
                ins.then_inc(s["chain"], 1)
                dve.wait_ge(s["chain"], made[0])

            V = nc.vector

            def first_best(key, vals, k):
                best, eq, rank, least, hot = tmp[key]
                hot = hots[:, int(key[1])] if key[0] == "e" else hot[:]
                done(V.tensor_reduce(best[:], vals, AX.X, ALU.max))
                done(V.tensor_tensor(eq[:, :, 0:k], vals, wide(best[:], k), ALU.is_equal))
                done(V.tensor_tensor(rank[:, :, 0:k], eq[:, :, 0:k],
                                     desc[:, 0:k].rearrange("p (a e) -> p a e", a=1).broadcast_to([P, NB, k]), ALU.mult))
                done(V.tensor_reduce(least[:], rank[:, :, 0:k], AX.X, ALU.max))
                done(V.tensor_tensor(hot[:, :, 0:k], rank[:, :, 0:k], wide(least[:], k), ALU.is_equal))
                return hot[:, :, 0:k]

            done(V.tensor_reduce(top[:], r.LG[:], AX.X, ALU.max))
            V.tensor_tensor(less[:], r.LG[:], wide(top[:], E), ALU.subtract).then_inc(s["less_done"], 1)
            dve.wait_ge(s["exp_done"], 1)
            done(V.tensor_reduce(den[:], ex[:], AX.X, ALU.add))
            done(V.reciprocal(rden[:], den[:]))
            done(V.tensor_tensor(prob[:], ex[:], wide(rden[:], E), ALU.mult))
            dve.wait_ge(s["in_done"], 80)
            dve.wait_ge(s["iota_done"], 3)
            done(V.tensor_copy(desc[:], desc_i[:]))
            done(V.tensor_copy(steps[:], steps_i[:]))
            done(V.tensor_tensor(sc[:], prob[:], rb[:].rearrange("p (a e) -> p a e", a=1).broadcast_to([P, NB, E]), ALU.add))
            done(V.tensor_reduce(gm[:], sc[:].rearrange("p n (g e) -> p n g e", e=NGR), AX.X, ALU.max))
            hot0 = first_best("g0", gm[:], EG)
            done(V.scalar_tensor_tensor(again[:, :, 0:EG], hot0, -BIG, gm[:], ALU.mult, ALU.add))
            hot1 = first_best("g1", again[:, :, 0:EG], EG)
            done(V.tensor_tensor(keep[:], hot0, hot1, ALU.add))
            done(V.tensor_scalar(pen[:], keep[:], -1.0, BIG, ALU.add, ALU.mult))
            done(V.tensor_tensor(masked[:].rearrange("p n (g e) -> p n g e", e=NGR),
                                 sc[:].rearrange("p n (g e) -> p n g e", e=NGR),
                                 pen[:].rearrange("p n (g a) -> p n g a", a=1).broadcast_to([P, NB, EG, NGR]), ALU.add))
            hot0 = first_best("e0", masked[:], E)
            done(V.scalar_tensor_tensor(again[:], hot0, -2.0 * BIG, masked[:], ALU.mult, ALU.add))
            hot1 = first_best("e1", again[:], E)
            V.tensor_tensor(chosen[:], hot0, hot1, ALU.add).then_inc(s["chosen_done"], 1)
            dve.wait_ge(s["chosen_done"], 1)
            V.memset(gates[:, :, E:E + 1], 1.0).then_inc(s["gates"], 1)
            V.tensor_tensor(gates[:, :, 0:E], chosen[:], sc[:], ALU.mult).then_inc(s["gates"], 1)
            pairs = lambda ap: ap.rearrange("p s n e -> p s (n e)")
            both = lambda ap: ap.rearrange("p (a n) e -> p a (n e)", a=1).broadcast_to([P, 2, NB * E])
            done(V.tensor_tensor(pairs(picked[:]), pairs(hots[:]), both(sc[:]), ALU.mult))
            done(V.tensor_reduce(r.value[:], picked[:], AX.X, ALU.add))
            dve.wait_ge(s["ranked"], 1)
            done(V.tensor_copy(count[:], count_ps[:, 0:E]))
            done(V.tensor_scalar(column[:].rearrange("p s n -> p (s n)")[:, 0:MOST], steps[:, 0:MOST], float(TL), None, ALU.mult))
            done(V.tensor_tensor(over[:], count[:].rearrange("p (e a) -> p e a", a=1).broadcast_to([P, E, MOST]),
                                 column[:].rearrange("p s n -> p (s n)")[:, 0:MOST].rearrange("p (a j) -> p a j", a=1).broadcast_to([P, E, MOST]), ALU.is_gt))
            done(V.tensor_reduce(tiles[:], over[:], AX.X, ALU.add))
            done(V.tensor_tensor(summed[:], upto[:], tiles[:].rearrange("p (a e) -> p a e", a=1).broadcast_to([P, E, E]), ALU.mult))
            done(V.tensor_reduce(end[:], summed[:], AX.X, ALU.add))
            done(V.tensor_tensor(begin[:], end[:], tiles[:], ALU.subtract))
            done(V.tensor_tensor(begun[:], steps[:, 0:TILES].rearrange("p (t a) -> p t a", a=1).broadcast_to([P, TILES, E]),
                                 end[:].rearrange("p (a e) -> p a e", a=1).broadcast_to([P, TILES, E]), ALU.is_ge))
            done(V.tensor_reduce(of_tile[:], begun[:], AX.X, ALU.add))
            done(V.tensor_scalar(of_tile[:], of_tile[:], float(E - 1), None, ALU.min))
            done(V.tensor_copy(r.tile_expert[:], of_tile[0:1]))
            done(V.tensor_tensor(pairs(picked[:]), pairs(hots[:]), rank_ps[:, 0:NB * E].rearrange("p (a f) -> p a f", a=1).broadcast_to([P, 2, NB * E]), ALU.mult))
            done(V.tensor_reduce(rank[:], picked[:], AX.X, ALU.add))
            done(V.tensor_tensor(picked[:].rearrange("p s n e -> p (s n) e"), hots[:].rearrange("p s n e -> p (s n) e"),
                                 begin[:].rearrange("p (a e) -> p a e", a=1).broadcast_to([P, 2 * NB, E]), ALU.mult))
            done(V.tensor_reduce(first[:], picked[:], AX.X, ALU.add))
            flat = lambda ap: ap.rearrange("p s n -> p (s n)")
            done(V.tensor_scalar(scaled[:, 0], steps[:, 1:NB + 1], float(P), None, ALU.mult))
            done(V.tensor_tensor(passed[:], flat(rank[:]).rearrange("p (f a) -> p f a", a=1).broadcast_to([P, 2 * NB, NB]),
                                 scaled[:, 0].rearrange("p (a j) -> p a j", a=1).broadcast_to([P, 2 * NB, NB]), ALU.is_ge))
            done(V.tensor_reduce(flat(column[:]), passed[:], AX.X, ALU.add))
            done(V.tensor_scalar(scaled[:], rank[:], float(COLS), None, ALU.mult))
            done(V.scalar_tensor_tensor(rank[:], column[:], float(1 - P * COLS), scaled[:], ALU.mult, ALU.add))
            done(V.scalar_tensor_tensor(scaled[:], first[:], float(TL // P), rank[:], ALU.mult, ALU.add))
            done(V.tensor_copy(r.address[:], scaled[:]))
            for c in range(NCH):
                dve.wait_ge(s["turned"], c + 1)
                V.tensor_copy(gate_T[:, c * CH:(c + 1) * CH], t_ps[c][0:E + 1, :]).then_inc(s["copied"], 1)
            for n in range(NB):
                dve.wait_ge(s["biased"], n + 1)
                V.tensor_tensor(r.Y[:, n], y_ps[n % 2][:], r.Y[:, n], ALU.add).then_inc(s["added"], 1)

        @block.tensor
        def _(pe):
            pe.wait_ge(s["in_done"], 80)
            pe.wait_ge(s["ones_done"], 1)
            pe.wait_ge(s["chosen_done"], 1)
            pick = chosen[:].rearrange("p n e -> p (n e)")
            nc.tensor.matmul(rank_ps[:, 0:NB * E], before[:], pick, start=True, stop=False, skip_group_check=True)
            for back in range(1, NB):
                nc.tensor.matmul(rank_ps[:, back * E:NB * E], ones[:], pick[:, 0:(NB - back) * E], start=False,
                                 stop=(back == NB - 1), skip_group_check=True)
            for n in range(NB):
                last = nc.tensor.matmul(count_ps[:, 0:E], ones[:], chosen[:, n], start=(n == 0), stop=(n == NB - 1))
            last.then_inc(s["ranked"], 1)
            pe.wait_ge(s["gates"], 2)
            for c in range(NCH):
                for j in range(CH // P):
                    last = nc.tensor.transpose(t_ps[c][0:E + 1, j * P:(j + 1) * P], gates[:, c * (CH // P) + j],
                                               r.ident[:])
                last.then_inc(s["turned"], 1)
            for n in range(NB):
                pe.wait_ge(s["copied"], n // (CH // P) + 1)
                if n >= 2:
                    pe.wait_ge(s["added"], n - 1)
                nc.tensor.matmul(y_ps[n % 2][:], gate_T[:, n * P:(n + 1) * P], b3[:], start=True, stop=True).then_inc(s["biased"], 1)


def phase_shared(nc, d, r):
    with ExitStack() as ctx:
        sb = lambda n, s, t=F32: ctx.enter_context(nc.sbuf_tensor(n, s, t))
        raw = [sb(f"w_raw{i}", [P, 3, D]) for i in range(2)]
        w_h = [sb(f"w_h{i}", [P, 3, D], F32R) for i in range(2)]
        w_l = [sb(f"w_l{i}", [P, 3, D], F32R) for i in range(2)]
        b1 = sb("b1", [P, SH])
        b2 = sb("b2", [P, SH])
        sil = [sb(f"sil{i}", [P, CH]) for i in range(2)]
        hid = [sb(f"hid{i}", [P, CH]) for i in range(2)]
        hid_h = [sb(f"hid_h{i}", [P, CH], F32R) for i in range(2)]
        hid_l = [sb(f"hid_l{i}", [P, CH], F32R) for i in range(2)]
        zero = sb("zero", [P, COLS], mybir.dt.int32)
        h1_ps = [ctx.enter_context(nc.psum_tensor(f"h1_ps{i}", [P, CH], F32)) for i in range(2)]
        h2_ps = [ctx.enter_context(nc.psum_tensor(f"h2_ps{i}", [P, CH], F32)) for i in range(2)]
        y_ps = [ctx.enter_context(nc.psum_tensor(f"y_ps{i}", [P, D], F32)) for i in range(4)]
        s = semaphores(nc, ctx, "e", "b_in w_in0 w_in1 whi_ready wlo_ready up1_done up2_done sil_done hid_done hhi_done "
                 "hlo_done down_done y_added go act_go zero_done table_clear scattered")
        w_in = [s["w_in0"], s["w_in1"]]
        block = ctx.enter_context(nc.Block())
        NJ = CH // P

        @block.sync
        def _(sp):
            def load(e, par):
                half = slice(e * INTER, (e + 1) * INTER)
                w3 = d["sw3"][half, :]
                for i, src in enumerate((d["sw1"][:, half], d["sw2"][:, half])):
                    sp.dma_start(raw[par][:, i].rearrange("p (k i) -> p k i", k=KT),
                                 src.rearrange("(k p) i -> p k i", p=P)).then_inc(w_in[par], 16)
                sp.dma_start(raw[par][:, 2], w3).then_inc(w_in[par], 16)

            load(0, 0)
            with nc.allow_non_contiguous_dma("biases with the hidden units on partitions"):
                for dst, src in ((b1, d["sb1"]), (b2, d["sb2"])):
                    sp.dma_start(dst[:], src.rearrange("(h i) -> i h", h=2)).then_inc(s["b_in"], 16)
            load(1, 1)

        @block.gpsimd
        def _(pool):
            def split(e, k, par, first=False):
                pool.wait_ge(w_in[par], 48 * (k + 1))
                if not first:
                    pool.wait_ge(s["down_done"], NCH * (e - 1))
                pool.sem_inc(s["go"], 1)
                nc.gpsimd.tensor_copy(w_h[par][:], raw[par][:]).then_inc(s["whi_ready"], 1)
                pool.wait_ge(s["whi_ready"], e + 1)
                nc.gpsimd.tensor_tensor(w_l[par][:], raw[par][:], f32(w_h[par][:]), ALU.subtract).then_inc(s["wlo_ready"], 1)

            def scatter(n):
                if n == 0:
                    pool.wait_ge(s["table_clear"], 16)
                for choice in range(2):
                    nc.gpsimd.indirect_dma_start(
                        r.slot_token, bass.IndirectOffsetOnAxis(ap=r.address[:, choice, n:n + 1], axis=0),
                        r.token[:, n:n + 1], None).then_inc(s["scattered"], 16)

            split(0, 0, 0, True)

            def step(e, k, par):
                for c in range(NCH):
                    q = e * NCH + c
                    pool.wait_ge(s["hhi_done"], q + 1)
                    nc.gpsimd.tensor_tensor(hid_l[c % 2][:], hid[c % 2][:], f32(hid_h[c % 2][:]), ALU.subtract).then_inc(s["hlo_done"], 1)
                    for n in range(q * NB // (SH * NCH), (q + 1) * NB // (SH * NCH)):
                        scatter(n)
                    if c == 1 and (not isinstance(e, int) or e + 1 < SH):
                        split(e + 1, k + 1 if par else k, 1 - par, isinstance(e, int) and e == 0)
            blocks(pool, SH, step, SH, 0)
            pool.wait_ge(s["scattered"], 2 * NB * 16)

        @block.scalar
        def _(act):
            act.wait_ge(s["zero_done"], 1)
            act.dma_start(r.slot_token.rearrange("(p c) a -> p (c a)", p=P), zero[:]).then_inc(s["table_clear"], 16)
            act.wait_ge(s["b_in"], 32)

            def step(e, k, par):
                for c in range(NCH):
                    q, i = e * NCH + c, c % 2
                    act.wait_ge(s["up1_done"], q + 1)
                    if not (isinstance(e, int) and e == 0 and c < 2):
                        act.wait_ge(s["hid_done"], q - 1)
                    act.sem_inc(s["act_go"], 1)
                    nc.scalar.activation(sil[i][:], h1_ps[i][:], ACT.Silu, bias=b1[:, bass.ds(e, 1)]).then_inc(s["sil_done"], 1)
                    act.wait_ge(s["hid_done"], q + 1)
                    if not (isinstance(e, int) and e == 0 and c < 2):
                        act.wait_ge(s["down_done"], q - 1)
                    nc.scalar.copy(hid_h[i][:], hid[i][:]).then_inc(s["hhi_done"], 1)
            blocks(act, SH, step, SH, 0)

        @block.vector
        def _(dve):
            nc.vector.memset(zero[:], 0).then_inc(s["zero_done"], 1)
            dve.wait_ge(s["b_in"], 32)

            def gather(e, c, q):
                for j in range(NJ):
                    n = c * NJ + j
                    dve.wait_ge(s["down_done"], q + 1)
                    nc.vector.tensor_tensor(r.Y[:, n], y_ps[j][:], r.Y[:, n], ALU.add).then_inc(s["y_added"], 1)

            def step(e, k, par):
                for c in range(NCH):
                    q, i = e * NCH + c, c % 2
                    dve.wait_ge(s["up2_done"], q + 1)
                    dve.wait_ge(s["sil_done"], q + 1)
                    if not (isinstance(e, int) and e == 0 and c < 2):
                        dve.wait_ge(s["hlo_done"], q - 1)
                    nc.vector.scalar_tensor_tensor(hid[i][:], h2_ps[i][:], b2[:, bass.ds(e, 1)], sil[i][:],
                                                   ALU.add, ALU.mult).then_inc(s["hid_done"], 1)
                    if c >= 1:
                        gather(e, c - 1, q - 1)
                    elif not (isinstance(e, int) and e == 0):
                        gather(e - 1, NCH - 1, q - 1)
            blocks(dve, SH, step, SH, 0)
            gather(SH - 1, NCH - 1, SH * NCH - 1)

        @block.tensor
        def _(pe):
            def up(e, c, par):
                q, i = e * NCH + c, c % 2
                if c == 0:
                    pe.wait_ge(s["wlo_ready"], e + 1)
                if not (isinstance(e, int) and e == 0 and c < 2):
                    pe.wait_ge(s["hid_done"], q - 1)
                for m, (out, done) in enumerate(((h1_ps[i], s["up1_done"]), (h2_ps[i], s["up2_done"]))):
                    for k in range(KT):
                        last = split_matmuls(
                            nc, out[:], (w_h[par][:, m, k * P:(k + 1) * P], w_l[par][:, m, k * P:(k + 1) * P]),
                            (r.XH[:, k, c * CH:(c + 1) * CH], r.XL[:, k, c * CH:(c + 1) * CH]), k)
                    last.then_inc(done, 1)

            def down(q, c, par):
                pe.wait_ge(s["hlo_done"], q + 1)
                i = c % 2
                if not (isinstance(q, int) and q == 0):
                    pe.wait_ge(s["y_added"], NJ * q)
                for j in range(NJ):
                    t = slice(j * P, (j + 1) * P)
                    nc.tensor.matmul(y_ps[j][:], hid_h[i][:, t], w_h[par][:, 2], start=True, stop=False)
                    nc.tensor.matmul(y_ps[j][:], hid_h[i][:, t], w_l[par][:, 2], start=False, stop=False)
                    last = nc.tensor.matmul(y_ps[j][:], hid_l[i][:, t], w_h[par][:, 2], start=False, stop=True)
                last.then_inc(s["down_done"], 1)

            def step(e, k, par):
                for c in range(NCH):
                    up(e, c, par)
                    if c >= 1:
                        down(e * NCH + c - 1, c - 1, par)
                    elif not (isinstance(e, int) and e == 0):
                        down(e * NCH - 1, NCH - 1, 1 - par)
            blocks(pe, SH, step, SH, 0)
            down(SH * NCH - 1, NCH - 1, (SH - 1) % 2)


def phase_sparse(nc, d, r):
    NJ = TL // P
    BUF = 3
    with ExitStack() as ctx:
        sb = lambda n, s, t=F32: ctx.enter_context(nc.sbuf_tensor(n, s, t))
        three = lambda n, s, t=F32: [sb(f"{n}{i}", s, t) for i in range(BUF)]
        slot_token = sb("slot_token_sb", [P, COLS], mybir.dt.int32)
        now = three("slot_token_now", [P, NJ], mybir.dt.int32)
        rows = three("rows", [P, NJ, D])
        x_h, x_l = three("tile_x_h", [P, KT, TL], F32R), three("tile_x_l", [P, KT, TL], F32R)
        raw = three("ew_raw", [P, 3, D])
        w_h, w_l = three("ew_h", [P, 3, D], F32R), three("ew_l", [P, 3, D], F32R)
        bias = three("eb", [P, 2])
        sil, hid = three("tile_sil", [P, TL]), three("tile_hid", [P, TL])
        hid_h, hid_l = three("tile_hid_h", [P, TL], F32R), three("tile_hid_l", [P, TL], F32R)
        y_out = three("y_out", [P, NJ, D])
        x_turn = ctx.enter_context(nc.psum_tensor("rows_turn", [P, NJ, KT, P], F32))
        h_ps = [ctx.enter_context(nc.psum_tensor(f"h_ps{i}", [P, 2, TL], F32)) for i in range(BUF)]
        y_ps = ctx.enter_context(nc.psum_tensor("ey_ps", [P, NJ, D], F32))
        s = semaphores(nc, ctx, "t", "table_in w_in0 w_in1 w_in2 rows_in0 rows_in1 rows_in2 stored0 stored1 stored2 now_done "
                 "turned xhi_ready xlo_ready whi_ready wlo_ready w3lo_ready up_done sil_done hid_done hhi_done hlo_done "
                 "down_done y_ready go act_go")
        w_in, rows_in = [s["w_in0"], s["w_in1"], s["w_in2"]], [s["rows_in0"], s["rows_in1"], s["rows_in2"]]
        stored = [s["stored0"], s["stored1"], s["stored2"]]
        block = ctx.enter_context(nc.Block())

        @block.sync
        def _(sp):
            def load(t, par):
                e = sp.value_load(r.tile_expert[0:1, bass.ds(t, 1)], min_val=0, max_val=E - 1)
                for i, src in enumerate((d["ew1"], d["ew2"])):
                    sp.dma_start(raw[par][:, i].rearrange("p (k i) -> p k i", k=KT),
                                 src[bass.ds(e, 1)].rearrange("e (k p) i -> p (e k) i", p=P)).then_inc(w_in[par], 16)
                sp.dma_start(raw[par][:, 2], d["ew3"][bass.ds(e, 1)].rearrange("e p d -> (e p) d")).then_inc(w_in[par], 16)
                with nc.allow_non_contiguous_dma("biases with the hidden units on partitions"):
                    for i, src in enumerate((d["eb1"], d["eb2"])):
                        sp.dma_start(bias[par][:, i:i + 1], src[bass.ds(e, 1)].rearrange("e i -> i e")).then_inc(w_in[par], 16)

            def store(t, par):
                sp.wait_ge(s["y_ready"], t + 1)
                sp.dma_start(r.slot_y.rearrange("(p c) d -> p c d", p=P)[:, bass.ds(t * NJ, NJ)], y_out[par][:]).then_inc(stored[par], 16)

            sp.dma_start(slot_token[:], r.slot_token.rearrange("(p c) a -> p (c a)", p=P)).then_inc(s["table_in"], 16)
            for t in range(BUF):
                load(t, t)

            def step(t, k, par):
                static = isinstance(t, int)
                if not static or t + BUF < TILES:
                    sp.wait_ge(s["wlo_ready"], t + 1)
                    sp.wait_ge(s["w3lo_ready"], t + 1)
                    sp.wait_ge(s["hid_done"], t + 1)
                    load(t + BUF, par)
                if not static or t >= 1:
                    store(t - 1, (par - 1) % BUF)
            blocks(sp, TILES, step, 4, 3, BUF)
            store(TILES - 1, (TILES - 1) % BUF)
            for par in range(BUF):
                sp.wait_ge(stored[par], 16 * len(range(par, TILES, BUF)))

        @block.gpsimd
        def _(pool):
            def gather(t, k, par):
                if not (isinstance(t, int) and t < BUF):
                    pool.wait_ge(s["turned"], t - BUF + 1)
                pool.sem_inc(s["go"], 1)
                nc.gpsimd.tensor_copy(now[par][:], slot_token[:, bass.ds(t * NJ, NJ)]).then_inc(s["now_done"], 1)
                pool.wait_ge(s["now_done"], t + 1)
                pool.sem_inc(s["go"], 1)
                for j in range(NJ):
                    nc.gpsimd.indirect_dma_start(rows[par][:, j], None, r.x_dram, bass.IndirectOffsetOnAxis(
                        ap=now[par][:, j:j + 1], axis=0)).then_inc(rows_in[par], 16)

            def low_w3(t, k, par):
                pool.wait_ge(s["whi_ready"], t + 1)
                nc.gpsimd.tensor_tensor(w_l[par][:, 2], raw[par][:, 2], f32(w_h[par][:, 2]), ALU.subtract).then_inc(s["w3lo_ready"], 1)

            pool.wait_ge(s["table_in"], 16)
            for t in range(2):
                gather(t, 0, t)
            low_w3(0, 0, 0)

            def step(t, k, par):
                static = isinstance(t, int)
                if not static or t + 2 < TILES:
                    gather(t + 2, k + (par + 2) // BUF, (par + 2) % BUF)
                if not static or t + 1 < TILES:
                    low_w3(t + 1, k + (par + 1) // BUF, (par + 1) % BUF)
                pool.wait_ge(s["hhi_done"], t + 1)
                nc.gpsimd.tensor_tensor(hid_l[par][:], hid[par][:], f32(hid_h[par][:]), ALU.subtract).then_inc(s["hlo_done"], 1)
            blocks(pool, TILES, step, 4, 3, BUF)

        @block.scalar
        def _(act):
            def high_x(t, par):
                act.wait_ge(s["turned"], t + 1)
                if not (isinstance(t, int) and t < BUF):
                    act.wait_ge(s["up_done"], t - BUF + 1)
                nc.scalar.copy(x_h[par][:].rearrange("p k (j q) -> p j k q", j=NJ), x_turn[:]).then_inc(s["xhi_ready"], 1)

            def high_w(t, k, par):
                act.wait_ge(w_in[par], 80 * (k + 1))
                if not (isinstance(t, int) and t < BUF):
                    act.wait_ge(s["down_done"], t - BUF + 1)
                nc.scalar.copy(w_h[par][:], raw[par][:]).then_inc(s["whi_ready"], 1)

            high_x(0, 0)
            high_w(0, 0, 0)

            def step(t, k, par):
                if not isinstance(t, int) or t + 1 < TILES:
                    high_x(t + 1, (par + 1) % BUF)
                    high_w(t + 1, k + (par + 1) // BUF, (par + 1) % BUF)
                act.wait_ge(s["up_done"], t + 1)
                act.sem_inc(s["act_go"], 1)
                nc.scalar.activation(sil[par][:], h_ps[par][:, 0], ACT.Silu, bias=bias[par][:, 0:1]).then_inc(s["sil_done"], 1)
                act.wait_ge(s["hid_done"], t + 1)
                nc.scalar.copy(hid_h[par][:], hid[par][:]).then_inc(s["hhi_done"], 1)
            blocks(act, TILES, step, 4, 3, BUF)

        @block.vector
        def _(dve):
            def low(t, par):
                dve.wait_ge(s["xhi_ready"], t + 1)
                nc.vector.tensor_tensor(x_l[par][:].rearrange("p k (j q) -> p j k q", j=NJ), x_turn[:],
                                        f32(x_h[par][:]).rearrange("p k (j q) -> p j k q", j=NJ), ALU.subtract).then_inc(s["xlo_ready"], 1)
                dve.wait_ge(s["whi_ready"], t + 1)
                nc.vector.tensor_tensor(w_l[par][:, 0:2], raw[par][:, 0:2], f32(w_h[par][:, 0:2]), ALU.subtract).then_inc(s["wlo_ready"], 1)

            def take_y(t, k, par):
                dve.wait_ge(s["down_done"], t + 1)
                if not (isinstance(t, int) and t < BUF):
                    dve.wait_ge(stored[par], 16 * k)
                nc.vector.tensor_copy(y_out[par][:], y_ps[:]).then_inc(s["y_ready"], 1)

            low(0, 0)

            def step(t, k, par):
                static = isinstance(t, int)
                if not static or t + 1 < TILES:
                    low(t + 1, (par + 1) % BUF)
                dve.wait_ge(s["sil_done"], t + 1)
                if not (static and t < BUF):
                    dve.wait_ge(s["hlo_done"], t - BUF + 1)
                nc.vector.scalar_tensor_tensor(hid[par][:], h_ps[par][:, 1], bias[par][:, 1:2], sil[par][:],
                                               ALU.add, ALU.mult).then_inc(s["hid_done"], 1)
                if not static or t >= 1:
                    take_y(t - 1, k - 1 if par == 0 else k, (par - 1) % BUF)
            blocks(dve, TILES, step, 4, 3, BUF)
            take_y(TILES - 1, (TILES - 1) // BUF, (TILES - 1) % BUF)

        @block.tensor
        def _(pe):
            def turn(t, k, par):
                pe.wait_ge(rows_in[par], 16 * NJ * (k + 1))
                if not (isinstance(t, int) and t == 0):
                    pe.wait_ge(s["xlo_ready"], t)
                for j in range(NJ):
                    for i in range(KT):
                        last = nc.tensor.transpose(x_turn[:, j, i], rows[par][:, j, i * P:(i + 1) * P], r.ident[:])
                last.then_inc(s["turned"], 1)

            def up(t, par):
                pe.wait_ge(s["xlo_ready"], t + 1)
                pe.wait_ge(s["wlo_ready"], t + 1)
                if not (isinstance(t, int) and t < BUF):
                    pe.wait_ge(s["hid_done"], t - BUF + 1)
                for m in range(2):
                    for i in range(KT):
                        of = slice(i * P, (i + 1) * P)
                        for n, (a, b) in enumerate(((w_h, x_h), (w_h, x_l), (w_l, x_h))):
                            last = nc.tensor.matmul(h_ps[par][:, m], a[par][:, m, of], b[par][:, i], start=(m + i + n == 0),
                                                    stop=(i == KT - 1 and n == 2), skip_group_check=True)
                last.then_inc(s["up_done"], 1)

            def down(t, par):
                pe.wait_ge(s["hlo_done"], t + 1)
                pe.wait_ge(s["w3lo_ready"], t + 1)
                if not (isinstance(t, int) and t == 0):
                    pe.wait_ge(s["y_ready"], t)
                for j in range(NJ):
                    q = slice(j * P, (j + 1) * P)
                    nc.tensor.matmul(y_ps[:, j], hid_h[par][:, q], w_h[par][:, 2], start=True, stop=False)
                    nc.tensor.matmul(y_ps[:, j], hid_h[par][:, q], w_l[par][:, 2], start=False, stop=False)
                    last = nc.tensor.matmul(y_ps[:, j], hid_l[par][:, q], w_h[par][:, 2], start=False, stop=True)
                last.then_inc(s["down_done"], 1)

            turn(0, 0, 0)

            def step(t, k, par):
                static = isinstance(t, int)
                if not static or t + 1 < TILES:
                    turn(t + 1, k + (par + 1) // BUF, (par + 1) % BUF)
                up(t, par)
                if not static or t >= 1:
                    down(t - 1, (par - 1) % BUF)
            blocks(pe, TILES, step, 4, 3, BUF)
            down(TILES - 1, (TILES - 1) % BUF)


def phase_combine(nc, d, r):
    BUF = 4
    with ExitStack() as ctx:
        sb = lambda n, s, t=F32: ctx.enter_context(nc.sbuf_tensor(n, s, t))
        now = [sb(f"address_now{i}", [P, 2], mybir.dt.int32) for i in range(BUF)]
        part = [sb(f"part{i}", [P, 2, D]) for i in range(BUF)]
        s = semaphores(nc, ctx, "c", "part_in0 part_in1 part_in2 part_in3 now_done added stored go")
        part_in = [s["part_in0"], s["part_in1"], s["part_in2"], s["part_in3"]]
        block = ctx.enter_context(nc.Block())

        @block.gpsimd
        def _(pool):
            def step(n, k, par):
                if not (isinstance(n, int) and n < BUF):
                    pool.wait_ge(s["added"], 2 * (n - BUF + 1))
                pool.sem_inc(s["go"], 1)
                nc.gpsimd.tensor_copy(now[par][:], r.address[:, :, bass.ds(n, 1)].rearrange("p s a -> p (s a)")).then_inc(s["now_done"], 1)
                pool.wait_ge(s["now_done"], n + 1)
                pool.sem_inc(s["go"], 1)
                for choice in range(2):
                    nc.gpsimd.indirect_dma_start(part[par][:, choice], None, r.slot_y, bass.IndirectOffsetOnAxis(
                        ap=now[par][:, choice:choice + 1], axis=0)).then_inc(part_in[par], 16)
            blocks(pool, NB, step, 4, 4, BUF)

        @block.vector
        def _(dve):
            def step(n, k, par):
                dve.wait_ge(part_in[par], 32 * (k + 1))
                for choice in range(2):
                    dve.wait_ge(s["added"], 2 * n + choice) if not (isinstance(n, int) and n == 0 and choice == 0) else None
                    nc.vector.scalar_tensor_tensor(r.Y[:, n], part[par][:, choice], r.value[:, choice, bass.ds(n, 1)],
                                                   r.Y[:, n], ALU.mult, ALU.add).then_inc(s["added"], 1)
            blocks(dve, NB, step, 4, 4, BUF)

        @block.sync
        def _(sp):
            def step(n, k, par):
                sp.wait_ge(s["added"], 2 * n + 2)
                sp.dma_start(d["out"].rearrange("b t d -> (b t) d")[bass.ds(n * P, P)], r.Y[:, n]).then_inc(s["stored"], 16)
            blocks(sp, NB, step, 4, 4, BUF)
            sp.wait_ge(s["stored"], 16 * NB)


def program(nc, d):
    r, w = Buffers(), Buffers()
    with ExitStack() as ctx:
        sb = sb_late = lambda n, s, t=F32: ctx.enter_context(nc.sbuf_tensor(n, s, t))
        r.Y = sb("Y", [P, NB, D])
        r.AN = sb("AN", [P, NB, D])
        r.ident = sb("ident", [P, P])
        r.ident_r = sb("ident_r", [P, P], F32R)
        r.mask_r = sb("mask_r", [P, G, P], F32R)
        r.eps = sb("eps", [P, 1])
        w.o_h = sb("wo_h", [P, KT, D], F32R)
        w.o_l = sb("wo_l", [P, KT, D], F32R)
        r.qk_dram = nc.dram_tensor("qk_turned", [2, QK, B * T], F32, kind="Internal").ap()
        with ExitStack() as early:
            sb = lambda n, s, t=F32: early.enter_context(nc.sbuf_tensor(n, s, t))
            r.V = sb("V", [P, NB, HKV, 2 * DH])
            with ExitStack() as first:
                sb = lambda n, s, t=F32: first.enter_context(nc.sbuf_tensor(n, s, t))
                r.mask = sb("mask", [P, P])
                r.cos = sb("cos", [P, NB, DH])
                r.sin = sb("sin", [P, NB, DH])
                r.bias = sb("bias", [P, D])
                w.qkv_h = sb("wqkv_h", [P, KT, QK + P], F32R)
                w.qkv_l = sb("wqkv_l", [P, KT, QK + P], F32R)
                w.l_h = sb("wl_h", [P, KT, D], F32R)
                w.l_l = sb("wl_l", [P, KT, D], F32R)
                retire(nc, phase_weights(nc, d, r, w))
                retire(nc, phase_project(nc, d, r, w))
            phase_attention(nc, d, r)
        r.value = sb_late("value", [P, 2, NB])
        r.address = sb_late("address", [P, 2, NB], mybir.dt.int32)
        r.token = sb_late("token", [P, NB], mybir.dt.int32)
        r.tile_expert = sb_late("tile_expert", [1, TILES], mybir.dt.int32)
        r.x_dram = nc.dram_tensor("x1_rows", [B * T, D], F32, kind="Internal").ap()
        r.slot_token = nc.dram_tensor("slot_token", [P * COLS, 1], mybir.dt.int32, kind="Internal").ap()
        r.slot_y = nc.dram_tensor("slot_y", [P * COLS, D], F32, kind="Internal").ap()
        with ExitStack() as late:
            sb = lambda n, s, t=F32: late.enter_context(nc.sbuf_tensor(n, s, t))
            r.XH = sb("x1T_hi", [P, KT, B * T], F32R)
            r.XL = sb("x1T_lo", [P, KT, B * T], F32R)
            r.LG = sb("logits", [P, NB, E])
            phase_mix(nc, d, r, w)
            phase_bind(nc, d, r)
            phase_route(nc, d, r)
            phase_shared(nc, d, r)
        phase_sparse(nc, d, r)
        phase_combine(nc, d, r)


_SHORT = {
    "L0_attn_X": "X", "L0_attn_Wq": "Wq", "L0_attn_Wk": "Wk", "L0_attn_Wv": "Wv", "L0_attn_Wo": "Wo",
    "L0_ffn_W": "W", "L0_ffn_bias": "bias", "L0_ffn_A": "A", "L0_ffn_Bf": "Bf", "L0_ffn_coeffs": "coeffs",
    "L0_ffn_scales": "scales", "L1_attn_bv_q": "bvq", "L1_attn_bv_k": "bvk", "L1_attn_bv_v": "bvv",
    "L1_ffn_router_w": "router_w", "L1_ffn_router_b": "router_b", "L1_ffn_router_bias": "router_bias",
    "L1_ffn_ew1": "ew1", "L1_ffn_eb1": "eb1", "L1_ffn_ew2": "ew2", "L1_ffn_eb2": "eb2", "L1_ffn_ew3": "ew3",
    "L1_ffn_eb3": "eb3", "L1_ffn_sw1": "sw1", "L1_ffn_sb1": "sb1", "L1_ffn_sw2": "sw2", "L1_ffn_sb2": "sb2",
    "L1_ffn_sw3": "sw3", "L1_ffn_sb3": "sb3",
}
_OUT = ((B, T, D), "float32")


def shape_constants():
    half = np.float32(HALF)
    inv = (np.float32(1.0) / np.float32(10000.0) ** (np.arange(HALF, dtype=np.float32) / half)).astype(np.float32)
    ang = np.arange(T, dtype=np.float32)[:, None] * inv[None, :]
    wide = lambda a: np.ascontiguousarray(
        np.tile(np.concatenate([a, a], 1).reshape(TB, P, DH).transpose(1, 0, 2), (1, B, 1)).astype(np.float32))
    i = np.arange(P)
    return {
        "ident": np.eye(P, dtype=np.float32),
        "mask": np.where(i[None, :] > i[:, None], np.float32(MASKED), np.float32(0)).astype(np.float32),
        "before": np.triu(np.ones((P, P), np.float32), 1), "upto": np.tril(np.ones((E, E), np.float32)),
        "cos": wide(np.cos(ang)), "sin": wide(np.sin(ang)),
    }


def kernel(**inputs):
    import concourse.bacc as _bacc
    from concourse.bass_utils import run_bass_kernel_spmd as _run

    nc = _bacc.Bacc("TRN2", target_bir_lowering=False, num_devices=1)
    given = {short: np.ascontiguousarray(inputs[name]) for name, short in _SHORT.items()}
    given.update(shape_constants())
    arrays = {f"in_{short}_dram": a for short, a in given.items()}
    d = {
        short: nc.dram_tensor(f"in_{short}_dram", a.shape, mybir.dt.from_np(a.dtype), kind="ExternalInput").ap()
        for short, a in given.items()}
    d["out"] = nc.dram_tensor("out_0_dram", _OUT[0], F32, kind="ExternalOutput").ap()
    program(nc, d)
    r = _run(nc, [arrays], core_ids=[0])
    return r.results[0]["out_0_dram"]
```

```python
from contextlib import ExitStack

import numpy as np
import concourse.bass as bass
from concourse import mybir

F32 = mybir.dt.float32
F32R = mybir.dt.float32r
ALU = mybir.AluOpType
ACT = mybir.ActivationFunctionType
AX = mybir.AxisListType

P = 128
B, T, D = 2, 1024, 512
NB = B * T // P
TB = T // P
KT = D // P
H, HKV, DH = 32, 8, 16
G = H // HKV
HALF = DH // 2
QK = D + HKV * DH
QT = QK // P
LR = 256
BH, BD = 4, 128
E, INTER = 16, 128
EG = 4
SH = 2
TL = 256
TILES = (2 * B * T + E * (TL - 1)) // TL
MOST = B * T // TL
BIAS_ROWS = 96
COLS = TILES * TL // P
EPS = 1e-5
MASKED = -float(2 ** 100)
CH = 512
NCH = B * T // CH
STACK = 4 * DH
SHIFT_ROW = 96
ROWS = SHIFT_ROW + 2


class Buffers:
    pass


def f32(ap):
    return ap.bitcast(F32)


def semaphores(nc, ctx, phase, names):
    return {name: ctx.enter_context(nc.semaphore(f"{phase}_{name}")) for name in names.split()}


def retire(nc, s):
    with nc.Block() as block:
        @block.sync
        def _(sp):
            for name in s:
                sp.sem_clear(s[name])


def blocks(eng, total, step, first=3, last=3, period=2):
    n = 0
    while n < first:
        step(n, n // period, n % period)
        n += 1
    turns = (total - last - first) // period
    if turns > 0:
        with eng.Fori(0, turns) as i:
            for m in range(n, n + period):
                step(i * period + m, i + m // period, m % period)
        n += turns * period
    while n < total:
        step(n, n // period, n % period)
        n += 1


def phase_weights(nc, d, r, w):
    with ExitStack() as ctx:
        sb = lambda n, s, t=F32: ctx.enter_context(nc.sbuf_tensor(n, s, t))
        wqkv = sb("wqkv_raw", [P, KT, QK + HKV * DH])
        wl = sb("wl_raw", [P, KT, D])
        am = sb("a_raw", [P, 2, D])
        bf = sb("bf_raw", [P, KT, LR])
        bw = sb("bw", [P, KT, LR])
        bwT = sb("bwT", [P, 2, D])
        co = sb("coeffs_all", [P, E])
        sc = sb("scales_all", [P, E])
        we = sb("we", [P, E])
        turned = [ctx.enter_context(nc.psum_tensor(f"bw_turned{i}", [P, D], F32)) for i in range(2)]
        folded = [ctx.enter_context(nc.psum_tensor(f"w_folded{i}", [P, D], F32)) for i in range(KT)]
        s = semaphores(nc, ctx, "w", "x_in qkv_in low_in wl_in const_in kscaled hi_done we_done bw_done turned_done bwT_done "
                 "folded_done folded_hi all_done idr ones")
        block = ctx.enter_context(nc.Block())

        @block.sync
        def _(sp):
            for k in range(KT):
                sp.dma_start(bf[:, k].rearrange("p (e r) -> p e r", e=E),
                             d["Bf"][:, k * P:(k + 1) * P].rearrange("e p r -> p e r")).then_inc(s["low_in"], 16)
            sp.dma_start(co[:], d["coeffs"].rearrange("(a e) -> a e", a=1).broadcast_to([P, E])).then_inc(s["low_in"], 16)
            sp.dma_start(sc[:], d["scales"].rearrange("(a e) -> a e", a=1).broadcast_to([P, E])).then_inc(s["low_in"], 16)
            sp.dma_start(am[:], d["A"].rearrange("e r d -> (e r) d").rearrange("(h p) d -> p h d", p=P)).then_inc(s["low_in"], 16)
            sp.dma_start(wl[:], d["W"].rearrange("(k p) d -> p k d", p=P)).then_inc(s["wl_in"], 16)
            for n in range(0, NB, 4):
                sp.dma_start(r.Y[:, n:n + 4], d["X"].rearrange("b t d -> (b t) d").rearrange(
                    "(n p) d -> p n d", p=P)[:, n:n + 4]).then_inc(s["x_in"], 16)
            sp.wait_ge(s["x_in"], 16 * NB // 4)

        @block.scalar
        def _(act):
            act.dma_start(r.ident[:], d["ident"]).then_inc(s["const_in"], 16)
            act.dma_start(r.mask[:], d["mask"]).then_inc(s["const_in"], 16)
            act.dma_start(r.cos[:], d["cos"]).then_inc(s["const_in"], 16)
            act.dma_start(r.sin[:], d["sin"]).then_inc(s["const_in"], 16)
            act.dma_start(r.bias[:], d["bias"].rearrange("(a e) -> a e", a=1).broadcast_to([P, D])).then_inc(s["const_in"], 16)
            act.dma_start(wqkv[:, :, 0:D], d["Wq"].rearrange("(k p) n -> p k n", p=P)).then_inc(s["qkv_in"], 16)
            act.dma_start(wqkv[:, :, D:QK], d["Wk"].rearrange("(k p) n -> p k n", p=P)).then_inc(s["qkv_in"], 16)
            act.dma_start(wqkv[:, :, QK:], d["Wv"].rearrange("(k p) n -> p k n", p=P)).then_inc(s["qkv_in"], 16)
            act.wait_ge(s["kscaled"], 1)
            nc.scalar.copy(w.qkv_h[:], wqkv[:]).then_inc(s["hi_done"], 1)
            for k in range(KT):
                act.wait_ge(s["folded_done"], k + 1)
                nc.scalar.copy(w.l_h[:, k], folded[k][:]).then_inc(s["folded_hi"], 1)

        @block.gpsimd
        def _(pool):
            nc.gpsimd.memset(r.V[:], 1.0).then_inc(s["ones"], 1)
            pool.wait_ge(s["qkv_in"], 48)
            nc.gpsimd.tensor_scalar(wqkv[:, :, D:QK], wqkv[:, :, D:QK], DH ** -0.5, None, ALU.mult).then_inc(s["kscaled"], 1)
            pool.wait_ge(s["hi_done"], 1)
            nc.gpsimd.tensor_tensor(w.qkv_l[:], wqkv[:], f32(w.qkv_h[:]), ALU.subtract).then_inc(s["all_done"], 1)

        @block.vector
        def _(dve):
            nc.vector.memset(r.eps[:], EPS).then_inc(s["ones"], 1)
            dve.wait_ge(s["low_in"], 16 * (KT + 3))
            nc.vector.tensor_tensor(we[:], co[:], sc[:], ALU.mult).then_inc(s["we_done"], 1)
            dve.wait_ge(s["we_done"], 1)
            for k in range(KT):
                nc.vector.tensor_tensor(bw[:, k].rearrange("p (e r) -> p e r", e=E),
                                        bf[:, k].rearrange("p (e r) -> p e r", e=E),
                                        we[:].rearrange("p (e a) -> p e a", a=1).broadcast_to([P, E, LR // E]),
                                        ALU.mult).then_inc(s["bw_done"], 1)
            dve.wait_ge(s["const_in"], 80)
            nc.vector.tensor_copy(r.ident_r[:], r.ident[:]).then_inc(s["idr"], 1)
            nc.vector.tensor_copy(r.mask_r[:], r.mask[:].rearrange("p (a s) -> p a s", a=1).broadcast_to([P, G, P])).then_inc(s["idr"], 1)
            for h in range(2):
                dve.wait_ge(s["turned_done"], h + 1)
                nc.vector.tensor_copy(bwT[:, h], turned[h][:]).then_inc(s["bwT_done"], 1)
            for k in range(KT):
                dve.wait_ge(s["folded_hi"], k + 1)
                nc.vector.tensor_tensor(w.l_l[:, k], folded[k][:], f32(w.l_h[:, k]), ALU.subtract).then_inc(s["all_done"], 1)

        @block.tensor
        def _(pe):
            pe.wait_ge(s["bw_done"], KT)
            pe.wait_ge(s["const_in"], 80)
            for h in range(2):
                for k in range(KT):
                    last = nc.tensor.transpose(turned[h][:, k * P:(k + 1) * P], bw[:, k, h * P:(h + 1) * P], r.ident[:])
                last.then_inc(s["turned_done"], 1)
            pe.wait_ge(s["bwT_done"], 2)
            pe.wait_ge(s["wl_in"], 16)
            for k in range(KT):
                for h in range(2):
                    nc.tensor.matmul(folded[k][:], am[:, h, k * P:(k + 1) * P], bwT[:, h], start=(h == 0), stop=False,
                                     skip_group_check=True)
                for o in range(KT):
                    last = nc.tensor.matmul(folded[k][:, o * P:(o + 1) * P], wl[:, o, k * P:(k + 1) * P], r.ident[:],
                                            start=False, stop=(o == KT - 1), skip_group_check=True)
                last.then_inc(s["folded_done"], 1)
    return s


def split_matmuls(nc, out, lhs, rhs, k):
    (lh, ll), (rh, rl) = lhs, rhs
    nc.tensor.matmul(out, lh, rh, start=(k == 0), stop=False)
    nc.tensor.matmul(out, lh, rl, start=False, stop=False)
    return nc.tensor.matmul(out, ll, rh, start=False, stop=(k == KT - 1))


def phase_project(nc, d, r, w):
    with ExitStack() as ctx:
        sb = lambda n, s, t=F32: ctx.enter_context(nc.sbuf_tensor(n, s, t))
        wo = sb("wo_raw", [P, KT, D])
        stats = sb("stats", [P, 2, 6])
        moments = sb("moments", [P, 2, 2])
        std = sb("std", [P, 2])
        rstd = sb("rstd", [P, 2])
        xn = sb("xn", [P, 2, D])
        xT_h = [sb(f"xT_h{i}", [P, KT, P], F32R) for i in range(2)]
        xT_l = [sb(f"xT_l{i}", [P, KT, P], F32R) for i in range(2)]
        by_cos = sb("by_cos", [P, QK])
        by_sin = sb("by_sin", [P, QK])
        turned = sb("turned", [P, 2, QK])
        qkT_h = sb("qkT_h", [P, 2, QT, P], F32R)
        qkT_l = sb("qkT_l", [P, 2, QT, P], F32R)
        ps = lambda n: ctx.enter_context(nc.psum_tensor(n, [P, D], F32))
        x_turn = [ps("x_turn0"), ps("x_turn1")]
        q_ps, kv_ps, lin_ps, q_turn, k_turn = ps("q_ps"), ps("kv_ps"), ps("lin_ps"), ps("q_turn"), ps("k_turn")
        s = semaphores(nc, ctx, "p", "stats_done moments_done std_done rstd_done xn_ready bias_added x_turned xhi_ready "
                 "xlo_ready q_done kv_done lin_done qmul_done kmul_done v_read lin_added rot_done qk_turned "
                 "qhi_ready qlo_ready stored0 stored1 wo_in wo_hi wo_lo padded stack_in")
        stored = [s["stored0"], s["stored1"]]
        block = ctx.enter_context(nc.Block())

        @block.vector
        def _(dve):
            def statistics(n, par):
                nc.vector.bn_stats(stats[:, par], r.Y[:, n]).then_inc(s["stats_done"], 1)

            def norm(n, par):
                nc.vector.bn_aggr(moments[:, par], stats[:, par]).then_inc(s["moments_done"], 1)
                dve.wait_ge(s["std_done"], n + 1)
                nc.vector.reciprocal(rstd[:, par:par + 1], std[:, par:par + 1]).then_inc(s["rstd_done"], 1)
                dve.wait_ge(s["rstd_done"], n + 1)
                nc.vector.tensor_scalar(xn[:, par], r.Y[:, n], moments[:, par, 0:1], rstd[:, par:par + 1],
                                        ALU.subtract, ALU.mult).then_inc(s["xn_ready"], 1)

            def low_half(n, par):
                dve.wait_ge(s["xhi_ready"], n + 1)
                nc.vector.tensor_tensor(xT_l[par][:], x_turn[par][:].rearrange("p (k t) -> p k t", k=KT),
                                        f32(xT_h[par][:]), ALU.subtract).then_inc(s["xlo_ready"], 1)

            def rope_products(n):
                for ps_, a, b, ready, done in ((q_ps, 0, D, s["q_done"], s["qmul_done"]), (kv_ps, D, QK, s["kv_done"], s["kmul_done"])):
                    dve.wait_ge(ready, n + 1)
                    if a == 0 and not (isinstance(n, int) and n == 0):
                        dve.wait_ge(s["rot_done"], n * 2)
                    heads = (b - a) // DH
                    src = ps_[:, 0:b - a].rearrange("p (h x c) -> p h x c", x=2, c=HALF)
                    for table, out in ((r.cos, by_cos), (r.sin, by_sin)):
                        fac = table[:, n].rearrange("p (a x c) -> p a x c", a=1, x=2).broadcast_to([P, heads, 2, HALF])
                        last = nc.vector.tensor_tensor(
                            out[:, a:b].rearrange("p (h x c) -> p h x c", x=2, c=HALF), src, fac, ALU.mult)
                    last.then_inc(done, 1)

            def add_linear(n):
                dve.wait_ge(s["lin_done"], n + 1)
                dve.wait_ge(s["bias_added"], n + 1)
                nc.vector.tensor_tensor(r.Y[:, n], lin_ps[:], r.Y[:, n], ALU.add).then_inc(s["lin_added"], 1)

            def low_qk(n, par):
                dve.wait_ge(s["qhi_ready"], n + 1)
                nc.vector.tensor_tensor(qkT_l[:, par, 0:KT], q_turn[:].rearrange("p (k t) -> p k t", k=KT),
                                        f32(qkT_h[:, par, 0:KT]), ALU.subtract)
                nc.vector.tensor_tensor(qkT_l[:, par, KT], k_turn[:, 0:P],
                                        f32(qkT_h[:, par, KT]), ALU.subtract).then_inc(s["qlo_ready"], 1)

            for n in range(2):
                statistics(n, n)
                dve.wait_ge(s["stats_done"], n + 1)
                norm(n, n)
            low_half(0, 0)

            def step(n, k, par):
                static = isinstance(n, int)
                if not static or n + 2 < NB:
                    statistics(n + 2, par)
                    dve.wait_ge(s["stats_done"], n + 3)
                if not static or n + 1 < NB:
                    low_half(n + 1, 1 - par)
                if not static or n + 2 < NB:
                    norm(n + 2, par)
                rope_products(n)
                add_linear(n)
                if not static or n >= 1:
                    low_qk(n - 1, 1 - par)
            blocks(dve, NB, step)
            low_qk(NB - 1, 1)

        @block.scalar
        def _(act):
            def root(n, par):
                act.wait_ge(s["moments_done"], n + 1)
                nc.scalar.activation(std[:, par:par + 1], moments[:, par, 1:2], ACT.Sqrt, bias=r.eps[:]).then_inc(s["std_done"], 1)

            def high_half(n, par):
                act.wait_ge(s["x_turned"], n + 1)
                if not (isinstance(n, int) and n < 2):
                    act.wait_ge(s["lin_done"], n - 1)
                nc.scalar.copy(xT_h[par][:], x_turn[par][:].rearrange("p (k t) -> p k t", k=KT)).then_inc(s["xhi_ready"], 1)

            def keep_v(n):
                act.wait_ge(s["kmul_done"], n + 1)
                nc.scalar.copy(r.V[:, n, :, 0:DH], kv_ps[:, P:2 * P].rearrange("p (h c) -> p h c", c=DH)).then_inc(s["v_read"], 1)

            def high_qk(n, k, par):
                act.wait_ge(s["qk_turned"], n + 1)
                if not (isinstance(n, int) and n < 2):
                    act.wait_ge(stored[par], k * 32)
                nc.scalar.copy(qkT_h[:, par, 0:KT], q_turn[:].rearrange("p (k t) -> p k t", k=KT))
                nc.scalar.copy(qkT_h[:, par, KT], k_turn[:, 0:P]).then_inc(s["qhi_ready"], 1)

            root(0, 0)
            root(1, 1)
            high_half(0, 0)

            def step(n, k, par):
                static = isinstance(n, int)
                if not static or n + 1 < NB:
                    high_half(n + 1, 1 - par)
                if not static or n + 2 < NB:
                    root(n + 2, par)
                keep_v(n)
                if not static or n >= 1:
                    high_qk(n - 1, k if par else k - 1, 1 - par)
                if static and n == 1:
                    act.wait_ge(s["wo_in"], 16)
                    nc.scalar.copy(w.o_h[:], wo[:]).then_inc(s["wo_hi"], 1)
            blocks(act, NB, step)
            high_qk(NB - 1, (NB - 1) // 2, 1)

        @block.gpsimd
        def _(pool):
            def add_bias(n):
                pool.wait_ge(s["xn_ready"], n + 1)
                nc.gpsimd.tensor_tensor(r.Y[:, n], r.Y[:, n], r.bias[:], ALU.add).then_inc(s["bias_added"], 1)

            def rotate(n, par):
                pool.wait_ge(s["kmul_done"], n + 1)
                if not (isinstance(n, int) and n < 2):
                    pool.wait_ge(s["qk_turned"], n - 1)
                c = by_cos[:].rearrange("p (h x c) -> p h x c", x=2, c=HALF)
                sn = by_sin[:].rearrange("p (h x c) -> p h x c", x=2, c=HALF)
                o = turned[:, par].rearrange("p (h x c) -> p h x c", x=2, c=HALF)
                nc.gpsimd.tensor_tensor(o[:, :, 0], c[:, :, 0], sn[:, :, 1], ALU.subtract).then_inc(s["rot_done"], 1)
                nc.gpsimd.tensor_tensor(o[:, :, 1], c[:, :, 1], sn[:, :, 0], ALU.add).then_inc(s["rot_done"], 1)

            pad_stacks(nc, r.q_stack0, r.k_stack0, s["padded"])
            pool.wait_ge(s["padded"], 3)
            add_bias(0)
            beside = (1, 2, NB - 3, NB - 2)

            def step(n, k, par):
                if not isinstance(n, int) or n + 1 < NB:
                    add_bias(n + 1)
                rotate(n, par)
                if isinstance(n, int) and n in beside:
                    i = beside.index(n)
                    pool.wait_ge(s["wo_hi"], 1)
                    nc.gpsimd.tensor_tensor(w.o_l[:, i], wo[:, i], f32(w.o_h[:, i]), ALU.subtract).then_inc(s["wo_lo"], 1)
            blocks(pool, NB, step)

        @block.tensor
        def _(pe):
            def turn_x(n, par):
                pe.wait_ge(s["xn_ready"], n + 1)
                if not (isinstance(n, int) and n < 2):
                    pe.wait_ge(s["xlo_ready"], n - 1)
                for k in range(KT):
                    last = nc.tensor.transpose(x_turn[par][:, k * P:(k + 1) * P], xn[:, par, k * P:(k + 1) * P], r.ident[:])
                last.then_inc(s["x_turned"], 1)

            def project(n, par):
                first = isinstance(n, int) and n == 0
                pe.wait_ge(s["xlo_ready"], n + 1)
                for out, cols, wh, wlo, free, done in (
                        (q_ps[:], (0, D), w.qkv_h, w.qkv_l, s["qmul_done"], s["q_done"]),
                        (kv_ps[:, 0:2 * P], (D, QK + P), w.qkv_h, w.qkv_l, s["v_read"], s["kv_done"]),
                        (lin_ps[:], (0, D), w.l_h, w.l_l, s["lin_added"], s["lin_done"])):
                    if not first:
                        pe.wait_ge(free, n)
                    for k in range(KT):
                        last = split_matmuls(nc, out, (xT_h[par][:, k], xT_l[par][:, k]),
                                             (wh[:, k, cols[0]:cols[1]], wlo[:, k, cols[0]:cols[1]]), k)
                    last.then_inc(done, 1)

            def turn_qk(n, par):
                pe.wait_ge(s["rot_done"], 2 * n + 2)
                if not (isinstance(n, int) and n == 0):
                    pe.wait_ge(s["qlo_ready"], n)
                for k in range(KT):
                    nc.tensor.transpose(q_turn[:, k * P:(k + 1) * P], turned[:, par, k * P:(k + 1) * P], r.ident[:])
                nc.tensor.transpose(k_turn[:, 0:P], turned[:, par, D:QK], r.ident[:]).then_inc(s["qk_turned"], 1)

            turn_x(0, 0)

            def step(n, k, par):
                static = isinstance(n, int)
                if not static or n + 1 < NB:
                    turn_x(n + 1, 1 - par)
                project(n, par)
                if not static or n >= 1:
                    turn_qk(n - 1, 1 - par)
            blocks(pe, NB, step)
            turn_qk(NB - 1, 1)

        @block.sync
        def _(sp):
            sp.dma_start(wo[:], d["Wo"].rearrange("(k p) n -> p k n", p=P)).then_inc(s["wo_in"], 16)

            def step(n, k, par):
                if isinstance(n, int) and n == NB - 3:
                    for i in range(2):
                        sp.wait_ge(stored[i], 32 * TB // 2)
                    load_k_stack(sp, r, r.k_stack0, 0, 0, s["stack_in"])
                    for tc in range(2):
                        load_q_stack(sp, r, r.q_stack0, 0, 0, tc, s["stack_in"])
                sp.wait_ge(s["qlo_ready"], n + 1)
                for half, src in enumerate((qkT_h, qkT_l)):
                    sp.dma_start(r.qk_dram[half].rearrange("(q p) t -> p q t", p=P)[:, :, bass.ds(n * P, P)],
                                 f32(src[:, par])).then_inc(stored[par], 16)
            blocks(sp, NB, step)
            for par in range(2):
                sp.wait_ge(stored[par], 32 * NB // 2)
            sp.wait_ge(s["stack_in"], 12 * 16)
    return s


def pad_stacks(nc, q_stack, k_stack, padded):
    nc.gpsimd.memset(f32(k_stack[STACK:SHIFT_ROW]), 0.0).then_inc(padded, 1)
    nc.gpsimd.memset(f32(k_stack[SHIFT_ROW:ROWS]), 1.0).then_inc(padded, 1)
    nc.gpsimd.memset(f32(q_stack[STACK:SHIFT_ROW]), 0.0).then_inc(padded, 1)


def load_q_stack(sp, r, stack, b, kv, tc, loaded):
    for j, half in enumerate((0, 0, 1, 1)):
        sp.dma_start(f32(stack[DH * j:DH * j + DH, :, tc * CH:(tc + 1) * CH]),
                     r.qk_dram[half, bass.ds(kv * (G * DH), G * DH), bass.ds(b * T + tc * CH, CH)].rearrange(
                         "(h c) t -> c h t", c=DH)).then_inc(loaded, 16)


def load_k_stack(sp, r, stack, b, kv, loaded):
    for j, half in enumerate((0, 1, 0, 1)):
        sp.dma_start(f32(stack[DH * j:DH * j + DH, :]),
                     r.qk_dram[half, bass.ds(D + kv * DH, DH), bass.ds(b * T, T)]).then_inc(loaded, 16)


def units():
    return [(tc, sb) for tc in range(T // CH) for sb in range((tc + 1) * CH // P)]


def max_units():
    out = []
    for tb in range(TB):
        for sc in range(tb * P // CH + 1):
            w = min((tb + 1) * P - sc * CH, CH)
            heads = 4 if w <= CH // 4 else 2 if w <= CH // 2 else 1
            out += [(tb, sc, h, heads, w) for h in range(0, G, heads)]
    return sorted(out, key=lambda m: m[0] >= CH // P)


def phase_attention(nc, d, r):
    U, M = units(), max_units()
    NU, NM = len(U), len(M)
    NG = B * HKV
    NBUF = 3
    TAIL = 2
    columns = [CH + 2 * P - max(0, sb * P - tc * CH) for tc, sb in U]
    share = lambda u: round(NM * sum(columns[:u]) / sum(columns))
    HEAD = NM - share(TAIL)
    LAG = 2
    DIAG = [u for u, (tc, sb) in enumerate(U) if sb * P >= tc * CH]
    ND = len(DIAG)
    M_LATE = [m[0] for m in M].index(CH // P)
    LAST0 = CH // P - 1
    COPY_O0 = LAST0 + LAG + 1
    TURN_O0 = COPY_O0 + 1
    COPY_O1 = LAG
    TURN_O1 = COPY_O1 + 1
    TURN_SHIFT = TURN_O1 + 1
    with ExitStack() as ctx:
        sb_ = lambda n, s, t=F32: ctx.enter_context(nc.sbuf_tensor(n, s, t))
        qs = [r.q_stack0] + [sb_(f"q_stack{i}", [ROWS, G, T], F32R) for i in range(1, NBUF)]
        ks = [r.k_stack0] + [sb_(f"k_stack{i}", [ROWS, T], F32R) for i in range(1, NBUF)]
        v = [sb_(f"v_cur{i}", [P, TB, 2 * DH]) for i in range(NBUF)]
        probs = [sb_(f"probs{i}", [P, G, CH]) for i in range(3)]
        negmax = sb_("negmax", [P, 2, G, TB])
        shift = sb_("shift", [P, G * TB])
        shiftT_h = sb_("shiftT_h", [G * TB, P], F32R)
        shiftT_l = sb_("shiftT_l", [G * TB, P], F32R)
        o_sb = sb_("o_sb", [P, 2, CH])
        rden = sb_("rden", [P, CH // P, G])
        s_ps = [ctx.enter_context(nc.psum_tensor(f"s_ps{i}", [P, 2, CH], F32)) for i in range(2)]
        m_ps = [ctx.enter_context(nc.psum_tensor(f"m_ps{i}", [P, CH], F32)) for i in range(2)]
        o_ps = ctx.enter_context(nc.psum_tensor("o_ps", [P, CH], F32))
        t_ps = ctx.enter_context(nc.psum_tensor("t_ps", [P, CH], F32))
        s = semaphores(nc, ctx, "a", "padded q0_in0 q0_in1 q0_in2 q1_in0 q1_in1 q1_in2 k_in0 k_in1 k_in2 v_ready m_scored "
                 "m_read combined turned turned_read shift_hi shift_ready shift_in0 shift_in1 shift_in2 "
                 "scored exped masked pv_done o_read rden_done mask_go")
        q0_in, q1_in, k_in = [s["q0_in0"], s["q0_in1"], s["q0_in2"]], [s["q1_in0"], s["q1_in1"], s["q1_in2"]], [s["k_in0"], s["k_in1"], s["k_in2"]]
        shift_in = [s["shift_in0"], s["shift_in1"], s["shift_in2"]]
        block = ctx.enter_context(nc.Block())

        def width(u):
            tc, sb = U[u]
            off = max(0, sb * P - tc * CH)
            return tc, sb, off

        @block.sync
        def _(sp):
            def place(g):
                return (g // HKV, g % HKV)

            def load_q(g, par, tc):
                b, kv = place(g)
                load_q_stack(sp, r, qs[par], b, kv, tc, (q0_in, q1_in)[tc][par])

            def load_k(g, par):
                b, kv = place(g)
                load_k_stack(sp, r, ks[par], b, kv, k_in[par])

            def send_shift(g, par):
                sp.wait_ge(s["shift_ready"], g + 1)
                for j, src in enumerate((shiftT_h, shiftT_l)):
                    sp.dma_start(f32(qs[par][SHIFT_ROW + j:SHIFT_ROW + j + 1]).rearrange("a h (n t) -> a (h n) t", t=P),
                                 f32(src[:])).then_inc(shift_in[par], 16)

            for g in range(1, NBUF):
                load_k(g, g)
                load_q(g, g, 0)
                load_q(g, g, 1)
            send_shift(0, 0)

            def step(g, k, par):
                static = isinstance(g, int)
                if not static or g + 1 < NG:
                    send_shift(g + 1, (par + 1) % NBUF)
                if not static or g + NBUF < NG:
                    sp.wait_ge(s["scored"], 2 * NU * g + 2 * (LAST0 + 1))
                    load_q(g + NBUF, par, 0)
                    sp.wait_ge(s["scored"], 2 * NU * (g + 1))
                    load_k(g + NBUF, par)
                    load_q(g + NBUF, par, 1)
            blocks(sp, NG, step, 2, 5, NBUF)

        @block.gpsimd
        def _(pool):
            for i in range(1, NBUF):
                pad_stacks(nc, qs[i], ks[i], s["padded"])

            def take_v(g, par):
                nc.gpsimd.tensor_copy(v[par][:], r.V[:, bass.ds(g // HKV * TB, TB), g % HKV]).then_inc(s["v_ready"], 1)

            pool.wait_ge(s["padded"], 3 * (NBUF - 1))
            take_v(0, 0)

            def step(g, k, par):
                if not isinstance(g, int) or g + 1 < NG:
                    if not (isinstance(g, int) and g < 2):
                        pool.wait_ge(s["pv_done"], (g - 1) * NU)
                    take_v(g + 1, (par + 1) % NBUF)
                for i, u in enumerate(DIAG):
                    tc, sb, off = width(u)
                    pool.wait_ge(s["exped"], 2 * NU * g + 2 * u + 2)
                    pool.sem_inc(s["mask_go"], 1)
                    blk = probs[u % 3][:, :, off:off + P]
                    nc.gpsimd.affine_select(out=blk, in_=blk, compare_op=ALU.is_ge, fill=0.0, base=0,
                                            pattern=[[0, G], [1, P]], channel_multiplier=-1).then_inc(s["masked"], 1)
            blocks(pool, NG, step, 2, 2, NBUF)

        @block.scalar
        def _(act):
            def copy_o(g, tc):
                act.wait_ge(s["pv_done"], NU * g + (LAST0 + 1 if tc == 0 else NU))
                if not (isinstance(g, int) and g == 0):
                    act.wait_ge(s["turned"], 3 * g + tc)
                nc.scalar.copy(o_sb[:, tc], o_ps[:]).then_inc(s["o_read"], 1)

            def step(g, k, par):
                for u in range(NU):
                    tc, sb, off = width(u)
                    if u == COPY_O1 and not (isinstance(g, int) and g == 0):
                        copy_o(g - 1, 1)
                    if u == COPY_O0:
                        copy_o(g, 0)
                    if not (isinstance(g, int) and g == 0 and u < 3):
                        act.wait_ge(s["pv_done"], NU * g + u - 2)
                    for hp in range(2):
                        act.wait_ge(s["scored"], 2 * NU * g + 2 * u + hp + 1)
                        nc.scalar.activation(probs[u % 3][:, 2 * hp:2 * hp + 2, off:], s_ps[hp][:, :, off:],
                                             ACT.Exp).then_inc(s["exped"], 1)
            blocks(act, NG, step, 2, 2, NBUF)
            copy_o(NG - 1, 1)

        def maxima_beside(g, u):
            if u < TAIL:
                later, first, last = 1, share(u) + HEAD, share(u + 1) + HEAD
            else:
                later, first, last = 2, share(u) - share(TAIL), share(u + 1) - share(TAIL)
            if isinstance(g, int) and g + later >= NG:
                return []
            return [(g + later, later, m) for m in range(first, last)]

        @block.vector
        def _(dve):
            def max_unit(g, m):
                tb, sc, h, heads, w = M[m]
                dve.wait_ge(s["m_scored"], NM * g + m + 1)
                nc.vector.tensor_reduce(negmax[:, sc, h:h + heads, tb],
                                        m_ps[m % 2][:, 0:heads * w].rearrange("p (h s) -> p h s", h=heads), AX.X,
                                        ALU.max, negate=True).then_inc(s["m_read"], 1)

            def combine(g):
                dve.wait_ge(s["m_read"], NM * (g + 1))
                out = shift[:].rearrange("p (h n) -> p h n", n=TB)
                nc.vector.tensor_tensor(out[:, :, CH // P:], negmax[:, 0, :, CH // P:], negmax[:, 1, :, CH // P:], ALU.min)
                nc.vector.tensor_copy(out[:, :, 0:CH // P], negmax[:, 0, :, 0:CH // P]).then_inc(s["combined"], 1)

            def take_shift(g, use, sent, before):
                dve.wait_ge(s["turned"], use + 1)
                if not (isinstance(g, int) and g == 0):
                    dve.wait_ge(shift_in[before], 32 * sent)
                nc.vector.tensor_copy(shiftT_h[:], t_ps[0:G * TB, 0:P]).then_inc(s["shift_hi"], 1)
                dve.wait_ge(s["shift_hi"], g + 1)
                nc.vector.tensor_tensor(shiftT_l[:], t_ps[0:G * TB, 0:P], f32(shiftT_h[:]), ALU.subtract).then_inc(s["shift_ready"], 1)
                dve.wait_ge(s["shift_ready"], g + 1)
                dve.sem_inc(s["turned_read"], 1)

            def normalise(g, tc, use, count):
                dve.wait_ge(s["turned"], use + 1)
                o = t_ps[:].rearrange("p (n h c) -> p n h c", h=G, c=2 * DH)
                nc.vector.reciprocal(rden[:], o[:, :, :, DH]).then_inc(s["rden_done"], 1)
                dve.wait_ge(s["rden_done"], count + 1)
                nc.vector.tensor_tensor(
                    r.AN[:, bass.ds(g // HKV * TB + tc * (CH // P), CH // P), bass.ds(g % HKV * (G * DH), G * DH)].rearrange(
                        "p n (h c) -> p n h c", c=DH),
                    o[:, :, :, 0:DH], rden[:].rearrange("p n (h a) -> p n h a", a=1).broadcast_to([P, CH // P, G, DH]),
                    ALU.mult).then_inc(s["turned_read"], 1)

            for m in range(NM):
                max_unit(0, m)
            combine(0)
            dve.wait_ge(s["combined"], 1)
            for m in range(HEAD // 2):
                max_unit(1, m)
            take_shift(0, 0, 0, 0)
            for m in range(HEAD // 2, HEAD):
                max_unit(1, m)

            def step(g, k, par):
                static = isinstance(g, int)
                more = not static or g + 1 < NG
                for u in range(NU):
                    if more and u == TAIL:
                        combine(g + 1)
                        dve.wait_ge(s["combined"], g + 2)
                    for gm, later, m in maxima_beside(g, u):
                        max_unit(gm, m)
                    if u == TURN_O1 and not (static and g == 0):
                        normalise(g - 1, 1, 3 * g, 2 * g - 1)
                    if more and u == TURN_SHIFT:
                        take_shift(g + 1, 3 * g + 1, k + 1, par)
                    if u == TURN_O0:
                        normalise(g, 0, 3 * g + 2 if more else 3 * g + 1, 2 * g)
            blocks(dve, NG, step, 2, 2, NBUF)
            normalise(NG - 1, 1, 3 * NG - 1, 2 * NG - 1)

        @block.tensor
        def _(pe):
            def max_scores(g, k, par, m):
                tb, sc, h, heads, w = M[m]
                if m == 0:
                    if isinstance(g, int) and 0 < g < NBUF:
                        pe.wait_ge(s["padded"], 3 * g)
                loads = k if par == 0 else k + 1
                if m == 0 and not (isinstance(g, int) and g == 0):
                    pe.wait_ge(k_in[par], 64 * loads)
                    pe.wait_ge(q0_in[par], 64 * loads)
                if m == M_LATE and not (isinstance(g, int) and g == 0):
                    pe.wait_ge(q1_in[par], 64 * loads)
                if not (isinstance(g, int) and g == 0 and m < 2):
                    pe.wait_ge(s["m_read"], NM * g + m - 1)
                diag = tb * P - sc * CH
                bank = m_ps[m % 2]
                for j in range(heads):
                    last = nc.tensor.matmul(bank[:, j * w:(j + 1) * w], qs[par][0:SHIFT_ROW, h + j, tb * P:(tb + 1) * P],
                                            ks[par][0:SHIFT_ROW, sc * CH:sc * CH + w], start=(j == 0),
                                            stop=(diag >= CH and j == heads - 1), skip_group_check=True)
                if diag < CH:
                    last = nc.tensor.matmul(bank[:, 0:heads * w].rearrange("p (h s) -> p h s", h=heads)[:, :, diag:diag + P],
                                            r.ident_r[:], r.mask_r[:, 0:heads], start=False, stop=True,
                                            skip_group_check=True)
                last.then_inc(s["m_scored"], 1)

            def scores(g, u, hp, par):
                tc, sb, off = width(u)
                if not (isinstance(g, int) and g == 0 and u == 0):
                    pe.wait_ge(s["exped"], 2 * NU * g + 2 * u + hp - 1)
                for j in range(2):
                    h = 2 * hp + j
                    last = nc.tensor.matmul(s_ps[hp][:, j, off:], ks[par][:, sb * P:(sb + 1) * P],
                                            qs[par][:, h, tc * CH + off:(tc + 1) * CH], start=True, stop=True)
                last.then_inc(s["scored"], 1)

            def pv(g, u, par):
                tc, sb, off = width(u)
                pe.wait_ge(s["exped"], 2 * NU * g + 2 * u + 2)
                if u in DIAG:
                    pe.wait_ge(s["masked"], ND * g + DIAG.index(u) + 1)
                if u == 0:
                    pe.wait_ge(s["v_ready"], g + 1)
                if sb == 0 and not (isinstance(g, int) and g == 0 and tc == 0):
                    pe.wait_ge(s["o_read"], 2 * g + tc)
                for h in range(G):
                    last = nc.tensor.matmul(o_ps[2 * DH * h:2 * DH * (h + 1), off:], v[par][:, sb, :],
                                            probs[u % 3][:, h, off:], start=(sb == 0),
                                            stop=(sb == (tc + 1) * CH // P - 1), skip_group_check=True)
                last.then_inc(s["pv_done"], 1)

            def turn_o(g, tc, use):
                pe.wait_ge(s["o_read"], 2 * g + tc + 1)
                pe.wait_ge(s["turned_read"], use)
                for j in range(CH // P):
                    last = nc.tensor.transpose(t_ps[:, j * P:(j + 1) * P], o_sb[:, tc, j * P:(j + 1) * P], r.ident[:])
                last.then_inc(s["turned"], 1)

            def turn_shift(g, use):
                pe.wait_ge(s["combined"], g + 1)
                if not (isinstance(g, int) and g == 0):
                    pe.wait_ge(s["turned_read"], use)
                nc.tensor.transpose(t_ps[0:G * TB, 0:P], shift[:], r.ident[:]).then_inc(s["turned"], 1)

            for m in range(NM):
                max_scores(0, 0, 0, m)
            for m in range(HEAD // 2):
                max_scores(1, 0, 1, m)
            turn_shift(0, 0)
            for m in range(HEAD // 2, HEAD):
                max_scores(1, 0, 1, m)

            def step(g, k, par):
                static = isinstance(g, int)
                more = not static or g + 1 < NG
                pe.wait_ge(shift_in[par], 32 * (k + 1))
                for u in range(NU):
                    beside = [(gm, k + (par + later) // NBUF, (par + later) % NBUF, m)
                              for gm, later, m in maxima_beside(g, u)]
                    for unit in beside[0:1]:
                        max_scores(*unit)
                    scores(g, u, 0, par)
                    for unit in beside[1:2]:
                        max_scores(*unit)
                    if u == TURN_O1 and not (static and g == 0):
                        turn_o(g - 1, 1, 3 * g)
                    if more and u == TURN_SHIFT:
                        turn_shift(g + 1, 3 * g + 1)
                    if u == TURN_O0:
                        turn_o(g, 0, 3 * g + 2 if more else 3 * g + 1)
                    if u >= LAG:
                        pv(g, u - LAG, par)
                    elif not (static and g == 0):
                        pv(g - 1, NU + u - LAG, (par - 1) % NBUF)
                    for unit in beside[2:]:
                        max_scores(*unit)
                    scores(g, u, 1, par)
            blocks(pe, NG, step, 2, 2, NBUF)
            for u in range(NU - LAG, NU):
                pv(NG - 1, u, (NG - 1) % NBUF)
            turn_o(NG - 1, 1, 3 * NG - 1)


def phase_mix(nc, d, r, w):
    with ExitStack() as ctx:
        sb = lambda n, s, t=F32: ctx.enter_context(nc.sbuf_tensor(n, s, t))
        bv = sb("bv", [P, 3, BH, BD])
        alpha = sb("alpha", [P, 3, BH])
        sign = sb("sign", [P, 3, BH, BD])
        STAGED = 4
        an = sb("an", [P, STAGED, D])
        aT_h = [sb(f"aT_h{i}", [P, KT, P], F32R) for i in range(2)]
        aT_l = [sb(f"aT_l{i}", [P, KT, P], F32R) for i in range(2)]
        stats = sb("stats1", [P, 2, 6])
        moments = sb("moments1", [P, 2, 2])
        std = sb("std1", [P, 2])
        rstd = sb("rstd1", [P, 2])
        xn = sb("xn1", [P, 2, D])
        xT = [sb(f"xT_full{i}", [P, KT, P]) for i in range(2)]
        router_w = sb("router_w", [P, KT, E])
        router_b = sb("router_b", [P, E])
        ps = lambda n: ctx.enter_context(nc.psum_tensor(n, [P, D], F32))
        a_turn = [ps("a_turn0"), ps("a_turn1")]
        o_ps = [ps("mix_ps0"), ps("mix_ps1")]
        x_turn = [ps("x1_turn0"), ps("x1_turn1")]
        l_ps = ps("logits_ps")
        s = semaphores(nc, ctx, "m", "bv_in summed alpha_done sign_done hard_done unbound bound router_in an_ready a_turned "
                 "ahi_ready alo_ready mixed added stats_done moments_done std_done rstd_done xn_ready "
                 "xn_kept x_turned xhi_ready xlo_ready logits_done logits_read copy_go stats_go")
        block = ctx.enter_context(nc.Block())
        tiles = lambda ap: ap.rearrange("p (k t) -> p k t", k=KT)

        @block.sync
        def _(sp):
            sp.dma_start(router_w[:], d["router_w"].rearrange("(k p) e -> p k e", p=P)).then_inc(s["router_in"], 16)
            sp.dma_start(router_b[:], d["router_b"].rearrange("(a e) -> a e", a=1).broadcast_to([P, E])).then_inc(s["router_in"], 16)
            for i, src in enumerate((d["bvq"], d["bvk"], d["bvv"])):
                sp.dma_start(bv[:, i], src.rearrange("(a h) c -> a h c", a=1).broadcast_to([P, BH, BD])).then_inc(s["bv_in"], 16)
            sp.wait_ge(s["router_in"], 32)
            sp.wait_ge(s["bv_in"], 48)

        @block.gpsimd
        def _(pool):
            def stage(n, par):
                if not (isinstance(n, int) and n < STAGED):
                    pool.wait_ge(s["a_turned"], n - STAGED + 1)
                    pool.sem_inc(s["copy_go"], 1)
                nc.gpsimd.tensor_copy(an[:, par], r.AN[:, n]).then_inc(s["an_ready"], 1)

            def keep(n, par):
                pool.wait_ge(s["xn_ready"], n + 1)
                pool.sem_inc(s["copy_go"], 1)
                nc.gpsimd.tensor_copy(r.AN[:, n], xn[:, par]).then_inc(s["xn_kept"], 1)

            for n in range(STAGED):
                stage(n, n)

            def step(n, k, par):
                if not isinstance(n, int) or n + STAGED < NB:
                    stage(n + STAGED, par)
                keep(n, par % 2)
            blocks(pool, NB, step, STAGED, STAGED, STAGED)

        @block.scalar
        def _(act):
            def high_a(n, par):
                act.wait_ge(s["a_turned"], n + 1)
                if not (isinstance(n, int) and n < 2):
                    act.wait_ge(s["mixed"], n - 1)
                nc.scalar.copy(aT_h[par][:], tiles(a_turn[par][:])).then_inc(s["ahi_ready"], 1)

            def root(n, par):
                act.wait_ge(s["moments_done"], n + 1)
                nc.scalar.activation(std[:, par:par + 1], moments[:, par, 1:2], ACT.Sqrt, bias=r.eps[:]).then_inc(s["std_done"], 1)

            def high_x(n, par):
                act.wait_ge(s["x_turned"], n + 1)
                if not (isinstance(n, int) and n < 2):
                    act.wait_ge(s["logits_done"], n - 1)
                nc.scalar.copy(xT[par][:], tiles(x_turn[par][:])).then_inc(s["xhi_ready"], 1)
                nc.scalar.copy(r.XH[:, :, bass.ds(n * P, P)], tiles(x_turn[par][:])).then_inc(s["xhi_ready"], 1)

            high_a(0, 0)

            def step(n, k, par):
                static = isinstance(n, int)
                if not static or n + 1 < NB:
                    high_a(n + 1, 1 - par)
                if not static or n >= 1:
                    high_x(n - 1, 1 - par)
                root(n, par)
            blocks(act, NB, step)
            high_x(NB - 1, 1)

        @block.vector
        def _(dve):
            def low_a(n, par):
                dve.wait_ge(s["ahi_ready"], n + 1)
                nc.vector.tensor_tensor(aT_l[par][:], tiles(a_turn[par][:]), f32(aT_h[par][:]), ALU.subtract).then_inc(s["alo_ready"], 1)

            def add(n, par):
                dve.wait_ge(s["mixed"], n + 1)
                nc.vector.tensor_tensor(r.Y[:, n], o_ps[par][:], r.Y[:, n], ALU.add).then_inc(s["added"], 1)
                dve.wait_ge(s["added"], n + 1)
                dve.sem_inc(s["stats_go"], 1)
                nc.vector.bn_stats(stats[:, par], r.Y[:, n]).then_inc(s["stats_done"], 1)

            def low_x(n, par):
                dve.wait_ge(s["xhi_ready"], 2 * n + 2)
                nc.vector.tensor_tensor(r.XL[:, :, bass.ds(n * P, P)], tiles(x_turn[par][:]), f32(r.XH[:, :, bass.ds(n * P, P)]), ALU.subtract).then_inc(s["xlo_ready"], 1)

            def norm(n, par):
                nc.vector.bn_aggr(moments[:, par], stats[:, par]).then_inc(s["moments_done"], 1)
                dve.wait_ge(s["std_done"], n + 1)
                nc.vector.reciprocal(rstd[:, par:par + 1], std[:, par:par + 1]).then_inc(s["rstd_done"], 1)
                dve.wait_ge(s["rstd_done"], n + 1)
                if not (isinstance(n, int) and n < 2):
                    dve.wait_ge(s["xn_kept"], n - 1)
                nc.vector.tensor_scalar(xn[:, par], r.Y[:, n], moments[:, par, 0:1], rstd[:, par:par + 1],
                                        ALU.subtract, ALU.mult).then_inc(s["xn_ready"], 1)

            def take_logits(n):
                dve.wait_ge(s["logits_done"], n + 1)
                nc.vector.tensor_tensor(r.LG[:, n], l_ps[:, 0:E], router_b[:], ALU.add).then_inc(s["logits_read"], 1)

            dve.wait_ge(s["router_in"], 32)
            low_a(0, 0)

            def make_bindings(part):
                if part == 0:
                    dve.wait_ge(s["bv_in"], 48)
                    nc.vector.tensor_reduce(alpha[:], bv[:], AX.X, ALU.add, apply_absolute_value=True).then_inc(s["summed"], 1)
                    nc.vector.tensor_scalar(sign[:], bv[:], 0.0, 2.0, ALU.is_ge, ALU.mult).then_inc(s["sign_done"], 1)
                    dve.wait_ge(s["summed"], 1)
                    nc.vector.tensor_scalar(alpha[:], alpha[:], 1.0 / BD, None, ALU.mult).then_inc(s["alpha_done"], 1)
                elif part == 1:
                    dve.wait_ge(s["sign_done"], 1)
                    nc.vector.tensor_scalar(sign[:], sign[:], -1.0, None, ALU.add).then_inc(s["sign_done"], 1)
                    dve.wait_ge(s["sign_done"], 2)
                    dve.wait_ge(s["alpha_done"], 1)
                    nc.vector.tensor_tensor(r.bind[:], sign[:], alpha[:].rearrange("p i (h a) -> p i h a", a=1).broadcast_to(
                        [P, 3, BH, BD]), ALU.mult).then_inc(s["hard_done"], 1)
                elif part == 2:
                    dve.wait_ge(s["hard_done"], 1)
                    nc.vector.tensor_tensor(sign[:], r.bind[:], bv[:], ALU.subtract).then_inc(s["unbound"], 1)
                else:
                    dve.wait_ge(s["unbound"], 1)
                    nc.vector.tensor_tensor(r.bind[:], sign[:], bv[:], ALU.add).then_inc(s["bound"], 1)

            def step(n, k, par):
                static = isinstance(n, int)
                if not static or n + 1 < NB:
                    low_a(n + 1, 1 - par)
                add(n, par)
                dve.wait_ge(s["stats_done"], n + 1)
                if not static or n >= 1:
                    low_x(n - 1, 1 - par)
                norm(n, par)
                if not static or n >= 2:
                    take_logits(n - 2)
                if static and n < 4:
                    make_bindings(n)
            blocks(dve, NB, step, 4, 4)
            low_x(NB - 1, 1)
            take_logits(NB - 2)
            take_logits(NB - 1)

        @block.tensor
        def _(pe):
            def turn_a(n, staged):
                par = staged % 2
                pe.wait_ge(s["an_ready"], n + 1)
                if not (isinstance(n, int) and n < 2):
                    pe.wait_ge(s["alo_ready"], n - 1)
                for k in range(KT):
                    last = nc.tensor.transpose(a_turn[par][:, k * P:(k + 1) * P], an[:, staged, k * P:(k + 1) * P], r.ident[:])
                last.then_inc(s["a_turned"], 1)

            def mix(n, par):
                pe.wait_ge(s["alo_ready"], n + 1)
                if not (isinstance(n, int) and n < 2):
                    pe.wait_ge(s["added"], n - 1)
                for k in range(KT):
                    last = split_matmuls(nc, o_ps[par][:], (aT_h[par][:, k], aT_l[par][:, k]), (w.o_h[:, k], w.o_l[:, k]), k)
                last.then_inc(s["mixed"], 1)

            def turn_x(n, par):
                pe.wait_ge(s["xn_ready"], n + 1)
                if not (isinstance(n, int) and n < 2):
                    pe.wait_ge(s["xlo_ready"], n - 1)
                for k in range(KT):
                    last = nc.tensor.transpose(x_turn[par][:, k * P:(k + 1) * P], xn[:, par, k * P:(k + 1) * P], r.ident[:])
                last.then_inc(s["x_turned"], 1)

            def logits(n, par):
                pe.wait_ge(s["xhi_ready"], 2 * n + 1)
                if not (isinstance(n, int) and n < 1):
                    pe.wait_ge(s["logits_read"], n)
                for k in range(KT):
                    last = nc.tensor.matmul(l_ps[:, 0:E], xT[par][:, k], router_w[:, k], start=(k == 0), stop=(k == KT - 1))
                last.then_inc(s["logits_done"], 1)

            pe.wait_ge(s["router_in"], 32)
            turn_a(0, 0)
            def step(n, k, par):
                static = isinstance(n, int)
                if not static or n + 1 < NB:
                    turn_a(n + 1, (par + 1) % STAGED)
                par = par % 2
                mix(n, par)
                if not static or n >= 2:
                    logits(n - 2, par)
                if not static or n >= 1:
                    turn_x(n - 1, 1 - par)
            blocks(pe, NB, step, 3, 1, STAGED)
            logits(NB - 2, 0)
            turn_x(NB - 1, 1)
            logits(NB - 1, 1)


def phase_bind(nc, d, r):
    U = units()
    NU = len(U)
    DIAG = [u for u, (tc, sb) in enumerate(U) if sb * P >= tc * CH]
    ND = len(DIAG)
    NG = B * BH
    SCALE = 4.0 * float(np.float32(BD ** -0.5))
    with ExitStack() as ctx:
        sb_ = lambda n, s, t=F32: ctx.enter_context(nc.sbuf_tensor(n, s, t))
        cols = sb_("bind_cols", [P, 2, BH])
        both = sb_("bind_both", [P, BH])
        ks = sb_("ks", [P, T])
        vb = [sb_(f"vb{i}", [P, TB, BD]) for i in range(2)]
        k_h = [sb_(f"k_h{i}", [P, T], F32R) for i in range(2)]
        k_l = [sb_(f"k_l{i}", [P, T], F32R) for i in range(2)]
        gate = [sb_(f"gate{i}", [P, CH]) for i in range(3)]
        s_ps = [ctx.enter_context(nc.psum_tensor(f"bs_ps{i}", [P, CH], F32)) for i in range(3)]
        o_ps = [ctx.enter_context(nc.psum_tensor(f"bo_ps{i}", [P, CH], F32)) for i in range(2)]
        c_ps = [ctx.enter_context(nc.psum_tensor(f"bc_ps{i}", [P, CH], F32)) for i in range(2)]
        hots, picked = (r.bind[:, i].rearrange("p h c -> p (h c)").rearrange("p (s n e) -> p s n e", s=2, n=NB)
                        for i in range(2))
        sc = sb_("route_scores", [P, NB, E])
        eq = sb_("eq", [P, NB, E])
        rank = sb_("rank", [P, NB, E])
        chosen = sb_("chosen", [P, NB, E])
        NGR = E // EG
        BIG = float(2 ** 100)
        rb = sb_("router_bias", [P, E])
        b3 = sb_("b3", [BIAS_ROWS, D])
        b3_stack = sb_("b3_stack", [BIAS_ROWS, D], F32R)
        g_stack = [sb_(f"g_stack{i}", [BIAS_ROWS, CH], F32R) for i in range(2)]
        top = sb_("top", [P, NB])
        less = sb_("less", [P, NB, E])
        before = sb_("before", [P, P])
        ones = sb_("ones", [P, P])
        steps_i = sb_("steps_i", [P, TILES + 1], mybir.dt.int32)
        steps = sb_("steps", [P, TILES + 1])
        upto = sb_("upto", [P, E, E])
        count = sb_("count", [P, E])
        reach = sb_("reach", [P, NB])
        over = sb_("over", [P, E, MOST])
        tiles = sb_("tiles", [P, E])
        end = sb_("end", [P, E])
        begin = sb_("begin", [P, E])
        of_tile = sb_("of_tile", [P, TILES])
        place = sb_("pair_rank", [P, 2, NB])
        first = sb_("pair_first", [P, 2, NB])
        column = sb_("column", [P, 2, NB])
        scaled = sb_("scaled", [P, 2, NB])
        group_hots = sb_("group_hots", [P, 2, NB, EG])
        ex = sb_("ex", [P, NB, E])
        den = sb_("den", [P, NB])
        rden = sb_("rden1", [P, NB])
        desc = sb_("desc", [P, E])
        desc_i = sb_("desc_i", [P, E], mybir.dt.int32)
        gm = sb_("gm", [P, NB, EG])
        best = sb_("best", [P, NB])
        least = sb_("least", [P, NB])
        keep = sb_("keep", [P, NB, EG])
        pen = sb_("pen", [P, NB, EG])
        gates = sb_("gates", [P, NB, E + 1])
        zero = sb_("zero", [P, COLS], mybir.dt.int32)
        gt_ps = ctx.enter_context(nc.psum_tensor("gt_ps", [P, CH], F32))
        rank_ps, count_ps = c_ps
        ROUTE_STEP = 3
        s = semaphores(nc, ctx, "b", "in_done lowered exp_done gates_done g_turned g_hi g_lo biased bias_added iota_done "
                 "ones_done chosen_done ranked chain placed b3_hi b3_lo zeroed table_zero table_clear "
                 "scattered x_stored turned cols_done x_ready k_made k_high both_done k_ready v_ready scored gated masked "
                 "pv_done added mask_go")
        block = ctx.enter_context(nc.Block())

        IN_DONE = 16 * (3 + 2 * BIAS_ROWS // 32)

        def width(u):
            tc, sb = U[u]
            return tc, sb, max(0, sb * P - tc * CH)

        @block.sync
        def _(sp):
            sp.dma_start(r.x_dram.rearrange("(n p) d -> p n d", p=P), r.AN[:]).then_inc(s["x_stored"], 16)
            sp.dma_start(rb[:], d["router_bias"].rearrange("(a e) -> a e", a=1).broadcast_to([P, E])).then_inc(s["in_done"], 16)
            sp.dma_start(before[:], d["before"]).then_inc(s["in_done"], 16)
            sp.dma_start(upto[:], d["upto"].rearrange("(a e) f -> a e f", a=1).broadcast_to([P, E, E])).then_inc(s["in_done"], 16)
            sp.wait_ge(s["table_zero"], 1)
            sp.dma_start(r.slot_token.rearrange("(p c) a -> p (c a)", p=P), zero[:]).then_inc(s["table_clear"], 16)
            sp.wait_ge(s["zeroed"], 1)
            for row in range(0, BIAS_ROWS, 32):
                sp.dma_start(b3[row:row + E], d["eb3"]).then_inc(s["in_done"], 16)
                sp.dma_start(b3[row + E:row + E + 1], d["sb3"].rearrange("(a e) -> a e", a=1)).then_inc(s["in_done"], 16)
            sp.wait_ge(s["in_done"], IN_DONE)
            sp.wait_ge(s["x_stored"], 16)

        @block.gpsimd
        def _(pool):
            nc.gpsimd.memset(b3[:], 0.0).then_inc(s["zeroed"], 1)
            nc.gpsimd.memset(zero[:], 0).then_inc(s["table_zero"], 1)
            nc.gpsimd.iota(desc_i[:], pattern=[[-1, E]], base=E, channel_multiplier=0).then_inc(s["iota_done"], 1)
            nc.gpsimd.iota(steps_i[:], pattern=[[1, TILES + 1]], base=0, channel_multiplier=0).then_inc(s["iota_done"], 1)
            nc.gpsimd.iota(r.token[:], pattern=[[P, NB]], base=0, channel_multiplier=1).then_inc(s["iota_done"], 1)
            nc.gpsimd.memset(ones[:], 1.0).then_inc(s["ones_done"], 1)
            def scatter(pair):
                n, choice = pair // 2, pair % 2
                nc.gpsimd.indirect_dma_start(
                    r.slot_token, bass.IndirectOffsetOnAxis(ap=r.address[:, choice, n:n + 1], axis=0),
                    r.token[:, n:n + 1], None).then_inc(s["scattered"], 16)

            def step(g, k, par):
                for u in DIAG:
                    if u == CH // P * (T // CH) and g >= ROUTE_STEP:
                        if g == ROUTE_STEP:
                            pool.wait_ge(s["table_clear"], 16)
                            pool.wait_ge(s["placed"], 1)
                            pool.wait_ge(s["iota_done"], 3)
                        share = 2 * NB // (NG - ROUTE_STEP)
                        for pair in range(share * (g - ROUTE_STEP), share * (g - ROUTE_STEP + 1) if g < NG - 1 else 2 * NB):
                            scatter(pair)
                    tc, sb, off = width(u)
                    pool.wait_ge(s["gated"], NU * g + u + 1)
                    pool.sem_inc(s["mask_go"], 1)
                    blk = gate[u % 3][:, off:off + P]
                    nc.gpsimd.affine_select(out=blk, in_=blk, compare_op=ALU.is_ge, fill=0.0, base=0,
                                            pattern=[[1, P]], channel_multiplier=-1).then_inc(s["masked"], 1)
            blocks(pool, NG, step, NG, 0)
            pool.wait_ge(s["scattered"], 2 * NB * 16)

        @block.scalar
        def _(act):
            def high_k(g, par):
                act.wait_ge(s["k_made"], g + 1)
                if not (isinstance(g, int) and g < 2):
                    act.wait_ge(s["scored"], NU * (g - 1))
                nc.scalar.copy(k_h[par][:], ks[:]).then_inc(s["k_high"], 1)

            high_k(0, 0)

            def step(g, k, par):
                for u in range(NU):
                    tc, sb, off = width(u)
                    act.wait_ge(s["scored"], NU * g + u + 1)
                    if not (isinstance(g, int) and g == 0 and u < 3):
                        act.wait_ge(s["pv_done"], NU * g + u - 2)
                    nc.scalar.activation(gate[u % 3][:, off:], s_ps[u % 3][:, off:], ACT.Sigmoid, scale=SCALE).then_inc(s["gated"], 1)
                    if isinstance(g, int) and g == ROUTE_STEP and u % 3 == 0:
                        c = u // 3
                        act.wait_ge(s["g_turned"], c + 1)
                        if c >= 2:
                            act.wait_ge(s["biased"], (c - 1) * (CH // P))
                        for row in (0, 32):
                            nc.scalar.copy(g_stack[c % 2][row:row + E + 1], gt_ps[0:E + 1, :]).then_inc(s["g_hi"], 1)
                    late = isinstance(g, int) and g in (1, 2)
                    if u == (NU - 1 if late else CH // P + 3) and (not isinstance(g, int) or g + 1 < NG):
                        high_k(g + 1, 1 - par)
                if isinstance(g, int) and g == 0:
                    act.wait_ge(s["lowered"], 1)
                    nc.scalar.activation(ex[:], less[:], ACT.Exp).then_inc(s["exp_done"], 1)
                    act.wait_ge(s["in_done"], IN_DONE)
                    nc.scalar.copy(b3_stack[:], b3[:]).then_inc(s["b3_hi"], 1)
            blocks(act, NG, step, ROUTE_STEP + 1, 2)

        @block.vector
        def _(dve):
            dve.wait_ge(s["turned"], 1)
            for i in range(2):
                last = nc.vector.tensor_copy(cols[:, i], c_ps[i][:].rearrange("p (h c) -> p h c", h=BH)[:, :, 0])
            last.then_inc(s["cols_done"], 1)
            dve.wait_ge(s["cols_done"], 1)
            nc.vector.tensor_tensor(both[:], cols[:, 0], cols[:, 1], ALU.mult).then_inc(s["both_done"], 1)
            dve.wait_ge(s["both_done"], 1)

            def make_kv(g, par):
                b, h = g // BH, g % BH
                if not (isinstance(g, int) and g < 2):
                    dve.wait_ge(s["scored"], NU * (g - 1))
                    dve.wait_ge(s["pv_done"], NU * (g - 1))
                if not (isinstance(g, int) and g == 0):
                    dve.wait_ge(s["k_ready"], g)
                nc.vector.tensor_tensor(ks[:], f32(r.XH[:, h, bass.ds(b * T, T)]), f32(r.XL[:, h, bass.ds(b * T, T)]),
                                        ALU.add).then_inc(s["x_ready"], 1)
                dve.wait_ge(s["x_ready"], g + 1)
                nc.vector.tensor_scalar(ks[:], ks[:], both[:, bass.ds(h, 1)], None, ALU.mult).then_inc(s["k_made"], 1)
                nc.vector.tensor_tensor(vb[par][:], r.AN[:, bass.ds(b * TB, TB), bass.ds(h * BD, BD)],
                                        r.bind[:, 2, bass.ds(h, 1), :].broadcast_to([P, TB, BD]), ALU.mult).then_inc(s["v_ready"], 1)
                dve.wait_ge(s["k_high"], g + 1)
                nc.vector.tensor_tensor(k_l[par][:], ks[:], f32(k_h[par][:]), ALU.subtract).then_inc(s["k_ready"], 1)

            make_kv(0, 0)
            wide = lambda ap, k: ap.rearrange("p (n a) -> p n a", a=1).broadcast_to([P, NB, k])
            pairs = lambda ap: ap.rearrange("p s n e -> p s (n e)")
            made = [0]

            def done(ins):
                made[0] += 1
                ins.then_inc(s["chain"], 1)
                dve.wait_ge(s["chain"], made[0])

            V = nc.vector

            def first_best(vals, k, hot):
                done(V.tensor_reduce(best[:], vals, AX.X, ALU.max))
                done(V.tensor_tensor(eq[:, :, 0:k], vals, wide(best[:], k), ALU.is_equal))
                done(V.tensor_tensor(rank[:, :, 0:k], eq[:, :, 0:k],
                                     desc[:, 0:k].rearrange("p (a e) -> p a e", a=1).broadcast_to([P, NB, k]), ALU.mult))
                done(V.tensor_reduce(least[:], rank[:, :, 0:k], AX.X, ALU.max))
                done(V.tensor_tensor(hot, rank[:, :, 0:k], wide(least[:], k), ALU.is_equal))
                return hot

            def choose():
                done(V.tensor_reduce(top[:], r.LG[:], AX.X, ALU.max))
                V.tensor_tensor(less[:], r.LG[:], wide(top[:], E), ALU.subtract).then_inc(s["lowered"], 1)
                dve.wait_ge(s["exp_done"], 1)
                done(V.tensor_reduce(den[:], ex[:], AX.X, ALU.add))
                done(V.reciprocal(rden[:], den[:]))
                done(V.tensor_tensor(less[:], ex[:], wide(rden[:], E), ALU.mult))
                dve.wait_ge(s["in_done"], IN_DONE)
                dve.wait_ge(s["iota_done"], 3)
                done(V.tensor_copy(desc[:], desc_i[:]))
                done(V.tensor_copy(steps[:], steps_i[:]))
                done(V.tensor_tensor(sc[:], less[:], rb[:].rearrange("p (a e) -> p a e", a=1).broadcast_to([P, NB, E]), ALU.add))
                done(V.tensor_reduce(gm[:], sc[:].rearrange("p n (g e) -> p n g e", e=NGR), AX.X, ALU.max))
                hot0 = first_best(gm[:], EG, group_hots[:, 0])
                done(V.scalar_tensor_tensor(less[:, :, 0:EG], hot0, -BIG, gm[:], ALU.mult, ALU.add))
                hot1 = first_best(less[:, :, 0:EG], EG, group_hots[:, 1])
                done(V.tensor_tensor(keep[:], hot0, hot1, ALU.add))
                done(V.tensor_scalar(pen[:], keep[:], -1.0, BIG, ALU.add, ALU.mult))
                done(V.tensor_tensor(ex[:].rearrange("p n (g e) -> p n g e", e=NGR),
                                     sc[:].rearrange("p n (g e) -> p n g e", e=NGR),
                                     pen[:].rearrange("p n (g a) -> p n g a", a=1).broadcast_to([P, NB, EG, NGR]), ALU.add))
                hot0 = first_best(ex[:], E, hots[:, 0])
                done(V.scalar_tensor_tensor(less[:], hot0, -2.0 * BIG, ex[:], ALU.mult, ALU.add))
                hot1 = first_best(less[:], E, hots[:, 1])
                V.tensor_tensor(chosen[:], hot0, hot1, ALU.add).then_inc(s["chosen_done"], 1)
                dve.wait_ge(s["chosen_done"], 1)
                V.memset(gates[:, :, E:E + 1], 1.0).then_inc(s["gates_done"], 1)
                V.tensor_tensor(gates[:, :, 0:E], chosen[:], sc[:], ALU.mult).then_inc(s["gates_done"], 1)
                both = lambda ap: ap.rearrange("p (a n) e -> p a (n e)", a=1).broadcast_to([P, 2, NB * E])
                done(V.tensor_tensor(pairs(picked[:]), pairs(hots[:]), both(sc[:]), ALU.mult))
                done(V.tensor_reduce(r.value[:], picked[:], AX.X, ALU.add))

            def sort_pairs():
                dve.wait_ge(s["ranked"], 1)
                done(V.tensor_copy(count[:], count_ps[:, 0:E]))
                done(V.tensor_scalar(reach[:, 0:MOST], steps[:, 0:MOST], float(TL), None, ALU.mult))
                done(V.tensor_tensor(over[:], count[:].rearrange("p (e a) -> p e a", a=1).broadcast_to([P, E, MOST]),
                                     reach[:, 0:MOST].rearrange("p (a j) -> p a j", a=1).broadcast_to([P, E, MOST]), ALU.is_gt))
                done(V.tensor_reduce(tiles[:], over[:], AX.X, ALU.add))
                done(V.tensor_tensor(eq[:], upto[:], tiles[:].rearrange("p (a e) -> p a e", a=1).broadcast_to([P, E, E]), ALU.mult))
                done(V.tensor_reduce(end[:], eq[:], AX.X, ALU.add))
                done(V.tensor_tensor(begin[:], end[:], tiles[:], ALU.subtract))
                done(V.tensor_tensor(picked[:].rearrange("p s n e -> p (s n) e")[:, 0:TILES], steps[:, 0:TILES].rearrange("p (t a) -> p t a", a=1).broadcast_to([P, TILES, E]),
                                     end[:].rearrange("p (a e) -> p a e", a=1).broadcast_to([P, TILES, E]), ALU.is_ge))
                done(V.tensor_reduce(of_tile[:], picked[:].rearrange("p s n e -> p (s n) e")[:, 0:TILES], AX.X, ALU.add))
                done(V.tensor_scalar(of_tile[:], of_tile[:], float(E - 1), None, ALU.min))
                done(V.tensor_copy(r.tile_expert[:], of_tile[0:1]))
                done(V.tensor_tensor(pairs(picked[:]), pairs(hots[:]), rank_ps[:, 0:NB * E].rearrange("p (a f) -> p a f", a=1).broadcast_to([P, 2, NB * E]), ALU.mult))
                done(V.tensor_reduce(place[:], picked[:], AX.X, ALU.add))
                done(V.tensor_tensor(picked[:].rearrange("p s n e -> p (s n) e"), hots[:].rearrange("p s n e -> p (s n) e"),
                                     begin[:].rearrange("p (a e) -> p a e", a=1).broadcast_to([P, 2 * NB, E]), ALU.mult))
                done(V.tensor_reduce(first[:], picked[:], AX.X, ALU.add))
                flat = lambda ap: ap.rearrange("p s n -> p (s n)")
                done(V.tensor_scalar(reach[:], steps[:, 1:NB + 1], float(P), None, ALU.mult))
                done(V.tensor_tensor(picked[:].rearrange("p s n e -> p (s n) e"), flat(place[:]).rearrange("p (f a) -> p f a", a=1).broadcast_to([P, 2 * NB, NB]),
                                     reach[:].rearrange("p (a j) -> p a j", a=1).broadcast_to([P, 2 * NB, NB]), ALU.is_ge))
                done(V.tensor_reduce(flat(column[:]), picked[:].rearrange("p s n e -> p (s n) e"), AX.X, ALU.add))
                done(V.tensor_scalar(scaled[:], place[:], float(COLS), None, ALU.mult))
                done(V.scalar_tensor_tensor(place[:], column[:], float(1 - P * COLS), scaled[:], ALU.mult, ALU.add))
                done(V.scalar_tensor_tensor(scaled[:], first[:], float(TL // P), place[:], ALU.mult, ALU.add))
                done(V.tensor_copy(r.address[:], scaled[:]))
                dve.sem_inc(s["placed"], 1)

            def add_biases(c):
                dve.wait_ge(s["g_hi"], 2 * c + 2)
                V.tensor_tensor(g_stack[c % 2][64:64 + E + 1], gt_ps[0:E + 1, :], f32(g_stack[c % 2][0:E + 1]),
                                ALU.subtract).then_inc(s["g_lo"], 1)
                for n in range(c * (CH // P), (c + 1) * (CH // P)):
                    dve.wait_ge(s["biased"], n + 1)
                    V.tensor_tensor(r.Y[:, n], c_ps[n % 2][:], r.Y[:, n], ALU.add).then_inc(s["bias_added"], 1)

            def step(g, k, par):
                b, h = g // BH, g % BH
                beside = isinstance(g, int) and g == ROUTE_STEP
                for tc in range(2):
                    if beside:
                        add_biases(2 * tc)
                        add_biases(2 * tc + 1)
                    dve.wait_ge(s["pv_done"], NU * g + (CH // P if tc == 0 else NU))
                    y = r.Y[:, bass.ds(b * TB + tc * (CH // P), CH // P), bass.ds(h * BD, BD)]
                    nc.vector.tensor_tensor(y, o_ps[tc][:].rearrange("p (n c) -> p n c", c=BD), y, ALU.add).then_inc(s["added"], 1)
                    if tc == 0 and (not isinstance(g, int) or g + 1 < NG):
                        make_kv(g + 1, 1 - par)
                if isinstance(g, int) and g == 0:
                    choose()
                    for i in range(2):
                        V.memset(f32(g_stack[i][:]), 0.0).then_inc(s["b3_lo"], 1)
                    dve.wait_ge(s["b3_hi"], 1)
                    V.tensor_tensor(b3_stack[32:64], b3[32:64], f32(b3_stack[32:64]), ALU.subtract).then_inc(s["b3_lo"], 1)
                if isinstance(g, int) and g == 1:
                    sort_pairs()
            blocks(dve, NG, step, ROUTE_STEP + 1, 2)

        @block.tensor
        def _(pe):
            for i in range(2):
                for h in range(BH):
                    last = nc.tensor.transpose(c_ps[i][:, h * BD:(h + 1) * BD], r.bind[:, i, h], r.ident[:])
            last.then_inc(s["turned"], 1)

            def scores(g, u, par):
                tc, sb, off = width(u)
                if u == 0:
                    pe.wait_ge(s["k_ready"], g + 1)
                if not (isinstance(g, int) and g == 0 and u < 3):
                    pe.wait_ge(s["gated"], NU * g + u - 2)
                b, h = g // BH, g % BH
                keys, queries = slice(sb * P, (sb + 1) * P), slice(b * T + tc * CH + off, b * T + (tc + 1) * CH)
                for i, (a, x) in enumerate(((k_h, r.XH), (k_h, r.XL), (k_l, r.XH))):
                    last = nc.tensor.matmul(s_ps[u % 3][:, off:], a[par][:, keys], x[:, h, queries], start=(i == 0), stop=(i == 2))
                last.then_inc(s["scored"], 1)

            def pv(g, u, par):
                tc, sb, off = width(u)
                pe.wait_ge(s["gated"], NU * g + u + 1)
                if u in DIAG:
                    pe.wait_ge(s["masked"], ND * g + DIAG.index(u) + 1)
                if u == 0:
                    pe.wait_ge(s["v_ready"], g + 1)
                if sb == 0 and not (isinstance(g, int) and g == 0):
                    pe.wait_ge(s["added"], 2 * g - 1 + tc)
                for j in range(off // P, CH // P):
                    last = nc.tensor.matmul(o_ps[tc][:, j * P:(j + 1) * P], gate[u % 3][:, j * P:(j + 1) * P], vb[par][:, sb],
                                            start=(sb == 0 and j == 0), stop=(sb == tc * CH // P + j), skip_group_check=True)
                last.then_inc(s["pv_done"], 1)

            def rank_pairs():
                pe.wait_ge(s["in_done"], IN_DONE)
                pe.wait_ge(s["ones_done"], 1)
                pe.wait_ge(s["chosen_done"], 1)
                pick = chosen[:].rearrange("p n e -> p (n e)")
                nc.tensor.matmul(rank_ps[:, 0:NB * E], before[:], pick, start=True, stop=False, skip_group_check=True)
                for back in range(1, NB):
                    nc.tensor.matmul(rank_ps[:, back * E:NB * E], ones[:], pick[:, 0:(NB - back) * E], start=False,
                                     stop=(back == NB - 1), skip_group_check=True)
                for n in range(NB):
                    last = nc.tensor.matmul(count_ps[:, 0:E], ones[:], chosen[:, n], start=(n == 0), stop=(n == NB - 1))
                last.then_inc(s["ranked"], 1)

            def turn_gates(c):
                pe.wait_ge(s["gates_done"], 2)
                if c >= 1:
                    pe.wait_ge(s["g_lo"], c)
                for j in range(CH // P):
                    last = nc.tensor.transpose(gt_ps[0:E + 1, j * P:(j + 1) * P], gates[:, c * (CH // P) + j], r.ident[:])
                last.then_inc(s["g_turned"], 1)

            def bias(n):
                c, j = n // (CH // P), n % (CH // P)
                pe.wait_ge(s["g_lo"], c + 1)
                pe.wait_ge(s["b3_lo"], 3)
                if n < 2:
                    pe.wait_ge(s["placed"], 1)
                else:
                    pe.wait_ge(s["bias_added"], n - 1)
                nc.tensor.matmul(c_ps[n % 2][:], g_stack[c % 2][:, j * P:(j + 1) * P], b3_stack[:], start=True,
                                 stop=True).then_inc(s["biased"], 1)

            def step(g, k, par):
                for u in range(NU):
                    scores(g, u, par)
                    if u >= 1:
                        pv(g, u - 1, par)
                    if isinstance(g, int) and g == ROUTE_STEP:
                        if u % 3 == 0:
                            turn_gates(u // 3)
                        else:
                            bias(4 * (u // 3) + 2 * (u % 3) - 2)
                            bias(4 * (u // 3) + 2 * (u % 3) - 1)
                pv(g, NU - 1, par)
                if isinstance(g, int) and g == 1:
                    rank_pairs()
            blocks(pe, NG, step, NG, 0)


def phase_sparse(nc, d, r, w):
    NJ = TL // P
    BUF = len(w.e_h)
    with ExitStack() as ctx:
        sb = lambda n, s, t=F32: ctx.enter_context(nc.sbuf_tensor(n, s, t))
        three = lambda n, s, t=F32: [sb(f"{n}{i}", s, t) for i in range(BUF)]
        slot_token = sb("slot_token_sb", [P, COLS], mybir.dt.int32)
        now = three("slot_token_now", [P, NJ], mybir.dt.int32)
        assert (3 + NJ) * BUF < NB and 2 * TL <= D
        raw = [r.AN[:, 3 * i:3 * i + 3] for i in range(BUF)]
        rows = [r.AN[:, 3 * BUF + NJ * i:3 * BUF + NJ * (i + 1)] for i in range(BUF)]
        x_h, x_l = ([wo[:].rearrange("p k (i q) -> p i k q", i=2)[:, 0], wo[:].rearrange("p k (i q) -> p i k q", i=2)[:, 1],
                     sb(f"tile_{name}", [P, KT, TL], F32R)[:]] for wo, name in ((w.o_h, "x_h"), (w.o_l, "x_l")))
        w_h, w_l = w.e_h, w.e_l
        bias = three("eb", [P, 2])
        sil, hid = r.AN[:, NB - 1, 0:TL], r.AN[:, NB - 1, TL:2 * TL]
        hid_h, hid_l = three("tile_hid_h", [P, TL], F32R), three("tile_hid_l", [P, TL], F32R)
        y_out = three("y_out", [P, NJ, D])
        x_turn = ctx.enter_context(nc.psum_tensor("rows_turn", [P, NJ, KT, P], F32))
        h_ps = [ctx.enter_context(nc.psum_tensor(f"h_ps{i}", [P, 2, TL], F32)) for i in range(BUF)]
        y_ps = ctx.enter_context(nc.psum_tensor("ey_ps", [P, NJ, D], F32))
        s = semaphores(nc, ctx, "t", "table_in w_in0 w_in1 w_in2 rows_in0 rows_in1 rows_in2 stored0 stored1 stored2 now_done "
                 "turned xhi_ready xlo_ready whi_ready wlo_ready w3lo_ready up_done sil_done hid_done "
                 "hhi_done hlo_done down_done y_ready go act_go")
        w_in, rows_in = [s["w_in0"], s["w_in1"], s["w_in2"]], [s["rows_in0"], s["rows_in1"], s["rows_in2"]]
        stored = [s["stored0"], s["stored1"], s["stored2"]]
        block = ctx.enter_context(nc.Block())

        @block.sync
        def _(sp):
            def load(t, par):
                e = sp.value_load(r.tile_expert[0:1, bass.ds(t, 1)], min_val=0, max_val=E - 1)
                for i, src in enumerate((d["ew1"], d["ew2"])):
                    sp.dma_start(raw[par][:, i].rearrange("p (k i) -> p k i", k=KT),
                                 src[bass.ds(e, 1)].rearrange("e (k p) i -> p (e k) i", p=P)).then_inc(w_in[par], 16)
                sp.dma_start(raw[par][:, 2], d["ew3"][bass.ds(e, 1)].rearrange("e p d -> (e p) d")).then_inc(w_in[par], 16)
                with nc.allow_non_contiguous_dma("biases with the hidden units on partitions"):
                    for i, src in enumerate((d["eb1"], d["eb2"])):
                        sp.dma_start(bias[par][:, i:i + 1], src[bass.ds(e, 1)].rearrange("e i -> i e")).then_inc(w_in[par], 16)

            def load_shared(t):
                of = slice((t - TILES) * INTER, (t - TILES + 1) * INTER)
                for i, src in enumerate((d["sw1"][:, of], d["sw2"][:, of])):
                    sp.dma_start(raw[t % BUF][:, i].rearrange("p (k i) -> p k i", k=KT),
                                 src.rearrange("(k p) i -> p k i", p=P)).then_inc(w_in[t % BUF], 16)
                sp.dma_start(raw[t % BUF][:, 2], d["sw3"][of, :]).then_inc(w_in[t % BUF], 16)

            def store(t, par):
                sp.wait_ge(s["y_ready"], t + 1)
                sp.dma_start(r.slot_y.rearrange("(p c) d -> p c d", p=P)[:, bass.ds(t * NJ, NJ)], y_out[par][:]).then_inc(stored[par], 16)

            sp.dma_start(slot_token[:], r.slot_token.rearrange("(p c) a -> p (c a)", p=P)).then_inc(s["table_in"], 16)
            for t in range(BUF):
                load(t, t)

            def step(t, k, par):
                static = isinstance(t, int)
                if not static or t + BUF < TILES + SH:
                    sp.wait_ge(s["wlo_ready"], t + 1)
                    sp.wait_ge(s["w3lo_ready"], t + 1)
                    sp.wait_ge(s["hid_done"], t + 1)
                    if static and t + BUF >= TILES:
                        load_shared(t + BUF)
                    else:
                        load(t + BUF, par)
                if not static or t >= 1:
                    store(t - 1, (par - 1) % BUF)
            blocks(sp, TILES, step, 4, 3, BUF)
            store(TILES - 1, (TILES - 1) % BUF)
            for par in range(BUF):
                sp.wait_ge(stored[par], 16 * len(range(par, TILES, BUF)))

        @block.gpsimd
        def _(pool):
            def gather(t, k, par):
                if not (isinstance(t, int) and t < BUF):
                    pool.wait_ge(s["turned"], t - BUF + 1)
                pool.sem_inc(s["go"], 1)
                nc.gpsimd.tensor_copy(now[par][:], slot_token[:, bass.ds(t * NJ, NJ)]).then_inc(s["now_done"], 1)
                pool.wait_ge(s["now_done"], t + 1)
                pool.sem_inc(s["go"], 1)
                for j in range(NJ):
                    nc.gpsimd.indirect_dma_start(rows[par][:, j], None, r.x_dram, bass.IndirectOffsetOnAxis(
                        ap=now[par][:, j:j + 1], axis=0)).then_inc(rows_in[par], 16)

            def low_w3(t, k, par):
                pool.wait_ge(s["whi_ready"], t + 1)
                nc.gpsimd.tensor_tensor(w_l[par][:, 2], raw[par][:, 2], f32(w_h[par][:, 2]), ALU.subtract).then_inc(s["w3lo_ready"], 1)

            pool.wait_ge(s["table_in"], 16)
            for t in range(2):
                gather(t, 0, t)
            low_w3(0, 0, 0)

            def step(t, k, par):
                static = isinstance(t, int)
                if not static or t + 2 < TILES:
                    gather(t + 2, k + (par + 2) // BUF, (par + 2) % BUF)
                low_w3(t + 1, k + (par + 1) // BUF, (par + 1) % BUF)
                pool.wait_ge(s["hhi_done"], t + 1)
                nc.gpsimd.tensor_tensor(hid_l[par][:], hid, f32(hid_h[par][:]), ALU.subtract).then_inc(s["hlo_done"], 1)
            blocks(pool, TILES, step, 4, 3, BUF)
            for t in range(TILES + 1, TILES + SH):
                low_w3(t, t // BUF, t % BUF)

        @block.scalar
        def _(act):
            def high_x(t, par):
                act.wait_ge(s["turned"], t + 1)
                if not (isinstance(t, int) and t < BUF):
                    act.wait_ge(s["up_done"], t - BUF + 1)
                nc.scalar.copy(x_h[par].rearrange("p k (j q) -> p j k q", j=NJ), x_turn[:]).then_inc(s["xhi_ready"], 1)

            def high_w(t, k, par, dmas=5):
                act.wait_ge(w_in[par], 80 * k + 16 * dmas)
                if not (isinstance(t, int) and t < BUF):
                    act.wait_ge(s["down_done"], t - BUF + 1)
                nc.scalar.copy(w_h[par][:], raw[par]).then_inc(s["whi_ready"], 1)

            high_x(0, 0)
            high_w(0, 0, 0)

            def step(t, k, par):
                if not isinstance(t, int) or t + 1 < TILES:
                    high_x(t + 1, (par + 1) % BUF)
                    high_w(t + 1, k + (par + 1) // BUF, (par + 1) % BUF)
                else:
                    high_w(t + 1, k + (par + 1) // BUF, (par + 1) % BUF, 3)
                act.wait_ge(s["up_done"], t + 1)
                if not (isinstance(t, int) and t == 0):
                    act.wait_ge(s["hid_done"], t)
                act.sem_inc(s["act_go"], 1)
                nc.scalar.activation(sil, h_ps[par][:, 0], ACT.Silu, bias=bias[par][:, 0:1]).then_inc(s["sil_done"], 1)
                act.wait_ge(s["hid_done"], t + 1)
                nc.scalar.copy(hid_h[par][:], hid).then_inc(s["hhi_done"], 1)
            blocks(act, TILES, step, 4, 3, BUF)
            for t in range(TILES + 1, TILES + SH):
                high_w(t, t // BUF, t % BUF, 3)

        @block.vector
        def _(dve):
            def low(t, par):
                dve.wait_ge(s["xhi_ready"], t + 1)
                nc.vector.tensor_tensor(x_l[par].rearrange("p k (j q) -> p j k q", j=NJ), x_turn[:],
                                        f32(x_h[par]).rearrange("p k (j q) -> p j k q", j=NJ), ALU.subtract).then_inc(s["xlo_ready"], 1)
                low_w(t, par)

            def low_w(t, par):
                dve.wait_ge(s["whi_ready"], t + 1)
                nc.vector.tensor_tensor(w_l[par][:, 0:2], raw[par][:, 0:2], f32(w_h[par][:, 0:2]), ALU.subtract).then_inc(s["wlo_ready"], 1)

            def take_y(t, k, par):
                dve.wait_ge(s["down_done"], t + 1)
                if not (isinstance(t, int) and t < BUF):
                    dve.wait_ge(stored[par], 16 * k)
                nc.vector.tensor_copy(y_out[par][:], y_ps[:]).then_inc(s["y_ready"], 1)

            low(0, 0)

            def step(t, k, par):
                static = isinstance(t, int)
                if not static or t + 1 < TILES:
                    low(t + 1, (par + 1) % BUF)
                else:
                    low_w(t + 1, (par + 1) % BUF)
                dve.wait_ge(s["sil_done"], t + 1)
                if not (static and t == 0):
                    dve.wait_ge(s["hlo_done"], t)
                nc.vector.scalar_tensor_tensor(hid, h_ps[par][:, 1], bias[par][:, 1:2], sil,
                                               ALU.add, ALU.mult).then_inc(s["hid_done"], 1)
                if not static or t >= 1:
                    take_y(t - 1, k - 1 if par == 0 else k, (par - 1) % BUF)
            blocks(dve, TILES, step, 4, 3, BUF)
            take_y(TILES - 1, (TILES - 1) // BUF, (TILES - 1) % BUF)
            for t in range(TILES + 1, TILES + SH):
                low_w(t, t % BUF)

        @block.tensor
        def _(pe):
            def turn(t, k, par):
                pe.wait_ge(rows_in[par], 16 * NJ * (k + 1))
                if not (isinstance(t, int) and t == 0):
                    pe.wait_ge(s["xlo_ready"], t)
                for j in range(NJ):
                    for i in range(KT):
                        last = nc.tensor.transpose(x_turn[:, j, i], rows[par][:, j, i * P:(i + 1) * P], r.ident[:])
                last.then_inc(s["turned"], 1)

            def up(t, par):
                pe.wait_ge(s["xlo_ready"], t + 1)
                pe.wait_ge(s["wlo_ready"], t + 1)
                if not (isinstance(t, int) and t < BUF):
                    pe.wait_ge(s["hid_done"], t - BUF + 1)
                for m in range(2):
                    for i in range(KT):
                        of = slice(i * P, (i + 1) * P)
                        for n, (a, b) in enumerate(((w_h, x_h), (w_h, x_l), (w_l, x_h))):
                            last = nc.tensor.matmul(h_ps[par][:, m], a[par][:, m, of], b[par][:, i], start=(m + i + n == 0),
                                                    stop=(i == KT - 1 and n == 2), skip_group_check=True)
                last.then_inc(s["up_done"], 1)

            def down(t, par):
                pe.wait_ge(s["hlo_done"], t + 1)
                pe.wait_ge(s["w3lo_ready"], t + 1)
                if not (isinstance(t, int) and t == 0):
                    pe.wait_ge(s["y_ready"], t)
                for j in range(NJ):
                    q = slice(j * P, (j + 1) * P)
                    nc.tensor.matmul(y_ps[:, j], hid_h[par][:, q], w_h[par][:, 2], start=True, stop=False)
                    nc.tensor.matmul(y_ps[:, j], hid_h[par][:, q], w_l[par][:, 2], start=False, stop=False)
                    last = nc.tensor.matmul(y_ps[:, j], hid_l[par][:, q], w_h[par][:, 2], start=False, stop=True)
                last.then_inc(s["down_done"], 1)

            turn(0, 0, 0)

            def step(t, k, par):
                static = isinstance(t, int)
                if not static or t + 1 < TILES:
                    turn(t + 1, k + (par + 1) // BUF, (par + 1) % BUF)
                up(t, par)
                if not static or t >= 1:
                    down(t - 1, (par - 1) % BUF)
            blocks(pe, TILES, step, 4, 3, BUF)
            down(TILES - 1, (TILES - 1) % BUF)


def phase_shared(nc, d, r, w):
    AHEAD = 4
    assert 2 * SH * NCH == NB
    with ExitStack() as ctx:
        sb = lambda n, s, t=F32: ctx.enter_context(nc.sbuf_tensor(n, s, t))
        w_h = [w.e_h[(TILES + e) % len(w.e_h)] for e in range(SH)]
        w_l = [w.e_l[(TILES + e) % len(w.e_l)] for e in range(SH)]
        b1 = sb("b1", [P, SH])
        b2 = sb("b2", [P, SH])
        sil = [sb(f"sil{i}", [P, CH]) for i in range(2)]
        hid = [sb(f"hid{i}", [P, CH]) for i in range(2)]
        hid_h = [sb(f"hid_h{i}", [P, CH], F32R) for i in range(2)]
        hid_l = [sb(f"hid_l{i}", [P, CH], F32R) for i in range(2)]
        part = [r.AN[:, 2 * i:2 * i + 2] for i in range(AHEAD)]
        h1_ps = [ctx.enter_context(nc.psum_tensor(f"h1_ps{i}", [P, CH], F32)) for i in range(2)]
        h2_ps = [ctx.enter_context(nc.psum_tensor(f"h2_ps{i}", [P, CH], F32)) for i in range(2)]
        y_ps = [ctx.enter_context(nc.psum_tensor(f"y_ps{i}", [P, D], F32)) for i in range(4)]
        s = semaphores(nc, ctx, "e", "b_in up1_done up2_done sil_done hid_done hhi_done hlo_done down_done y_added act_go "
                 "parts_in0 parts_in1 parts_in2 parts_in3 combined stored")
        parts_in = [s["parts_in0"], s["parts_in1"], s["parts_in2"], s["parts_in3"]]
        block = ctx.enter_context(nc.Block())
        NJ = CH // P

        @block.sync
        def _(sp):
            with nc.allow_non_contiguous_dma("biases with the hidden units on partitions"):
                for dst, src in ((b1, d["sb1"]), (b2, d["sb2"])):
                    sp.dma_start(dst[:], src.rearrange("(h i) -> i h", h=2)).then_inc(s["b_in"], 16)
            yv = d["out"].rearrange("b t d -> (b t) d").rearrange("(n p) d -> p n d", p=P)
            for n in range(0, NB, 2):
                sp.wait_ge(s["y_added"], NB * (SH - 1) + n + 2)
                sp.wait_ge(s["combined"], 2 * (n + 2))
                sp.dma_start(yv[:, n:n + 2], r.Y[:, n:n + 2]).then_inc(s["stored"], 16)
            sp.wait_ge(s["stored"], 16 * NB // 2)

        @block.gpsimd
        def _(pool):
            def gather_parts(n):
                if n >= AHEAD:
                    pool.wait_ge(s["combined"], 2 * (n - AHEAD + 1))
                for choice in range(2):
                    nc.gpsimd.indirect_dma_start(part[n % AHEAD][:, choice], None, r.slot_y, bass.IndirectOffsetOnAxis(
                        ap=r.address[:, choice, n:n + 1], axis=0)).then_inc(parts_in[n % AHEAD], 16)

            for n in range(AHEAD):
                gather_parts(n)

            def step(e, k, par):
                for c in range(NCH):
                    q = e * NCH + c
                    pool.wait_ge(s["hhi_done"], q + 1)
                    nc.gpsimd.tensor_tensor(hid_l[c % 2][:], hid[c % 2][:], f32(hid_h[c % 2][:]), ALU.subtract).then_inc(s["hlo_done"], 1)
                    for n in range(AHEAD + 2 * q, min(AHEAD + 2 * q + 2, NB)):
                        gather_parts(n)
            blocks(pool, SH, step, SH, 0)

        @block.scalar
        def _(act):
            act.wait_ge(s["b_in"], 32)

            def step(e, k, par):
                for c in range(NCH):
                    q, i = e * NCH + c, c % 2
                    act.wait_ge(s["up1_done"], q + 1)
                    if not (isinstance(e, int) and e == 0 and c < 2):
                        act.wait_ge(s["hid_done"], q - 1)
                    act.sem_inc(s["act_go"], 1)
                    nc.scalar.activation(sil[i][:], h1_ps[i][:], ACT.Silu, bias=b1[:, bass.ds(e, 1)]).then_inc(s["sil_done"], 1)
                    act.wait_ge(s["hid_done"], q + 1)
                    if not (isinstance(e, int) and e == 0 and c < 2):
                        act.wait_ge(s["down_done"], q - 1)
                    nc.scalar.copy(hid_h[i][:], hid[i][:]).then_inc(s["hhi_done"], 1)
            blocks(act, SH, step, SH, 0)

        @block.vector
        def _(dve):
            dve.wait_ge(s["b_in"], 32)

            def add_products(e, c, q):
                for j in range(NJ):
                    n = c * NJ + j
                    dve.wait_ge(s["down_done"], q + 1)
                    nc.vector.tensor_tensor(r.Y[:, n], y_ps[j][:], r.Y[:, n], ALU.add).then_inc(s["y_added"], 1)

            def combine(n):
                dve.wait_ge(parts_in[n % AHEAD], 32 * (n // AHEAD + 1))
                for choice in range(2):
                    nc.vector.scalar_tensor_tensor(r.Y[:, n], part[n % AHEAD][:, choice], r.value[:, choice, n:n + 1],
                                                   r.Y[:, n], ALU.mult, ALU.add).then_inc(s["combined"], 1)
                    dve.wait_ge(s["combined"], 2 * n + choice + 1)

            def step(e, k, par):
                for c in range(NCH):
                    q, i = e * NCH + c, c % 2
                    dve.wait_ge(s["up2_done"], q + 1)
                    dve.wait_ge(s["sil_done"], q + 1)
                    if not (isinstance(e, int) and e == 0 and c < 2):
                        dve.wait_ge(s["hlo_done"], q - 1)
                    nc.vector.scalar_tensor_tensor(hid[i][:], h2_ps[i][:], b2[:, bass.ds(e, 1)], sil[i][:],
                                                   ALU.add, ALU.mult).then_inc(s["hid_done"], 1)
                    if c >= 1:
                        add_products(e, c - 1, q - 1)
                    elif not (isinstance(e, int) and e == 0):
                        add_products(e - 1, NCH - 1, q - 1)
                    if q >= 1:
                        dve.wait_ge(s["y_added"], NJ * q)
                    for n in range(2 * q, 2 * q + 2):
                        combine(n)

            blocks(dve, SH, step, SH, 0)
            add_products(SH - 1, NCH - 1, SH * NCH - 1)

        @block.tensor
        def _(pe):
            def up(e, c, par):
                q, i = e * NCH + c, c % 2
                if not (isinstance(e, int) and e == 0 and c < 2):
                    pe.wait_ge(s["hid_done"], q - 1)
                for m, (out, done) in enumerate(((h1_ps[i], s["up1_done"]), (h2_ps[i], s["up2_done"]))):
                    for k in range(KT):
                        last = split_matmuls(
                            nc, out[:], (w_h[par][:, m, k * P:(k + 1) * P], w_l[par][:, m, k * P:(k + 1) * P]),
                            (r.XH[:, k, c * CH:(c + 1) * CH], r.XL[:, k, c * CH:(c + 1) * CH]), k)
                    last.then_inc(done, 1)

            def down(q, c, par):
                pe.wait_ge(s["hlo_done"], q + 1)
                i = c % 2
                if not (isinstance(q, int) and q == 0):
                    pe.wait_ge(s["y_added"], NJ * q)
                for j in range(NJ):
                    t = slice(j * P, (j + 1) * P)
                    nc.tensor.matmul(y_ps[j][:], hid_h[i][:, t], w_h[par][:, 2], start=True, stop=False)
                    nc.tensor.matmul(y_ps[j][:], hid_h[i][:, t], w_l[par][:, 2], start=False, stop=False)
                    last = nc.tensor.matmul(y_ps[j][:], hid_l[i][:, t], w_h[par][:, 2], start=False, stop=True)
                last.then_inc(s["down_done"], 1)

            def step(e, k, par):
                for c in range(NCH):
                    up(e, c, par)
                    if c >= 1:
                        down(e * NCH + c - 1, c - 1, par)
                    elif not (isinstance(e, int) and e == 0):
                        down(e * NCH - 1, NCH - 1, 1 - par)
            blocks(pe, SH, step, SH, 0)
            down(SH * NCH - 1, NCH - 1, (SH - 1) % 2)


def program(nc, d):
    r, w = Buffers(), Buffers()
    with ExitStack() as ctx:
        sb = outer = lambda n, s, t=F32: ctx.enter_context(nc.sbuf_tensor(n, s, t))
        r.Y = sb("Y", [P, NB, D])
        r.AN = sb("AN", [P, NB, D])
        r.ident = sb("ident", [P, P])
        r.eps = sb("eps", [P, 1])
        w.o_h = sb("wo_h", [P, KT, D], F32R)
        w.o_l = sb("wo_l", [P, KT, D], F32R)
        r.qk_dram = nc.dram_tensor("qk_turned", [2, QK, B * T], F32, kind="Internal").ap()
        with ExitStack() as early:
            sb = lambda n, s, t=F32: early.enter_context(nc.sbuf_tensor(n, s, t))
            r.mask_r = sb("mask_r", [P, G, P], F32R)
            r.ident_r = sb("ident_r", [P, P], F32R)
            r.V = sb("V", [P, NB, HKV, 2 * DH])
            r.q_stack0 = sb("q_stack0", [ROWS, G, T], F32R)
            r.k_stack0 = sb("k_stack0", [ROWS, T], F32R)
            with ExitStack() as first:
                sb = lambda n, s, t=F32: first.enter_context(nc.sbuf_tensor(n, s, t))
                r.mask = sb("mask", [P, P])
                r.cos = sb("cos", [P, NB, DH])
                r.sin = sb("sin", [P, NB, DH])
                r.bias = sb("bias", [P, D])
                w.qkv_h = sb("wqkv_h", [P, KT, QK + P], F32R)
                w.qkv_l = sb("wqkv_l", [P, KT, QK + P], F32R)
                w.l_h = sb("wl_h", [P, KT, D], F32R)
                w.l_l = sb("wl_l", [P, KT, D], F32R)
                retire(nc, phase_weights(nc, d, r, w))
                retire(nc, phase_project(nc, d, r, w))
            phase_attention(nc, d, r)
        r.value = outer("value", [P, 2, NB])
        r.address = outer("address", [P, 2, NB], mybir.dt.int32)
        r.token = outer("token", [P, NB], mybir.dt.int32)
        r.tile_expert = outer("tile_expert", [1, TILES], mybir.dt.int32)
        r.x_dram = nc.dram_tensor("x1_rows", [B * T, D], F32, kind="Internal").ap()
        r.slot_token = nc.dram_tensor("slot_token", [P * COLS, 1], mybir.dt.int32, kind="Internal").ap()
        r.slot_y = nc.dram_tensor("slot_y", [P * COLS, D], F32, kind="Internal").ap()
        with ExitStack() as late:
            sb = lambda n, s, t=F32: late.enter_context(nc.sbuf_tensor(n, s, t))
            r.XH = sb("x1T_hi", [P, KT, B * T], F32R)
            r.XL = sb("x1T_lo", [P, KT, B * T], F32R)
            with nc.sbuf_tensor("logits", [P, NB, E], F32) as r.LG, nc.sbuf_tensor("bind", [P, 3, BH, BD], F32) as r.bind:
                phase_mix(nc, d, r, w)
                phase_bind(nc, d, r)
            w.e_h = [sb(f"ew_h{i}", [P, 3, D], F32R) for i in range(3)]
            w.e_l = [sb(f"ew_l{i}", [P, 3, D], F32R) for i in range(3)]
            phase_sparse(nc, d, r, w)
            phase_shared(nc, d, r, w)


_SHORT = {
    "L0_attn_X": "X", "L0_attn_Wq": "Wq", "L0_attn_Wk": "Wk", "L0_attn_Wv": "Wv", "L0_attn_Wo": "Wo",
    "L0_ffn_W": "W", "L0_ffn_bias": "bias", "L0_ffn_A": "A", "L0_ffn_Bf": "Bf", "L0_ffn_coeffs": "coeffs",
    "L0_ffn_scales": "scales", "L1_attn_bv_q": "bvq", "L1_attn_bv_k": "bvk", "L1_attn_bv_v": "bvv",
    "L1_ffn_router_w": "router_w", "L1_ffn_router_b": "router_b", "L1_ffn_router_bias": "router_bias",
    "L1_ffn_ew1": "ew1", "L1_ffn_eb1": "eb1", "L1_ffn_ew2": "ew2", "L1_ffn_eb2": "eb2", "L1_ffn_ew3": "ew3",
    "L1_ffn_eb3": "eb3", "L1_ffn_sw1": "sw1", "L1_ffn_sb1": "sb1", "L1_ffn_sw2": "sw2", "L1_ffn_sb2": "sb2",
    "L1_ffn_sw3": "sw3", "L1_ffn_sb3": "sb3",
}
_OUT = ((B, T, D), "float32")


def shape_constants():
    half = np.float32(HALF)
    inv = (np.float32(1.0) / np.float32(10000.0) ** (np.arange(HALF, dtype=np.float32) / half)).astype(np.float32)
    ang = np.arange(T, dtype=np.float32)[:, None] * inv[None, :]
    wide = lambda a: np.ascontiguousarray(
        np.tile(np.concatenate([a, a], 1).reshape(TB, P, DH).transpose(1, 0, 2), (1, B, 1)).astype(np.float32))
    i = np.arange(P)
    return {
        "ident": np.eye(P, dtype=np.float32),
        "mask": np.where(i[None, :] > i[:, None], np.float32(MASKED), np.float32(0)).astype(np.float32),
        "before": np.triu(np.ones((P, P), np.float32), 1), "upto": np.tril(np.ones((E, E), np.float32)),
        "cos": wide(np.cos(ang)), "sin": wide(np.sin(ang)),
    }


def kernel(**inputs):
    import concourse.bacc as _bacc
    from concourse.bass_utils import run_bass_kernel_spmd as _run

    nc = _bacc.Bacc("TRN2", target_bir_lowering=False, num_devices=1)
    given = {short: np.ascontiguousarray(inputs[name]) for name, short in _SHORT.items()}
    given.update(shape_constants())
    arrays = {f"in_{short}_dram": a for short, a in given.items()}
    d = {
        short: nc.dram_tensor(f"in_{short}_dram", a.shape, mybir.dt.from_np(a.dtype), kind="ExternalInput").ap()
        for short, a in given.items()}
    d["out"] = nc.dram_tensor("out_0_dram", _OUT[0], F32, kind="ExternalOutput").ap()
    program(nc, d)
    r = _run(nc, [arrays], core_ids=[0])
    return r.results[0]["out_0_dram"]
```
